# Optimizing a Trainium2 kernel written in Bass

```python
import numpy as np
import jax
import jax.numpy as jnp

def _softmax(x, axis=-1):
    return jax.nn.softmax(x, axis=axis)

def _gelu(x):
    return jax.nn.gelu(x, approximate=True)

def _silu(x):
    return jax.nn.silu(x)

def _sigmoid(x):
    return jax.nn.sigmoid(x)

def _layernorm(x, axis=-1, eps=1e-05):
    m = jnp.mean(x, axis=axis, keepdims=True)
    v = jnp.var(x, axis=axis, keepdims=True)
    return (x - m) / jnp.sqrt(v + eps)

def _scatter_add(tgt, idx, src, axis=0):
    return tgt.at[idx].add(src)

def _segment_sum(src, seg, n):
    return jax.ops.segment_sum(src, seg, n)
kernel_name = 'mk_sandwich_d1_jaxref_r8_2bfc5d'

def setup_inputs(seed: int=0):
    np.random.seed(seed)
    _w = jnp.asarray

    def _L0_attn_setup():
        import jax, jax.numpy as jnp
        import numpy as np
        INFTY_APPROX = 1e+30
        ROTARY_BASE = 10000.0
        D_HEAD = 128

        def rope(x):
            *_, length, width = x.shape
            half = width // 2
            positions = jnp.arange(length)[:, None].astype(x.dtype)
            dims = jnp.arange(half).astype(x.dtype)
            ang_freqs = jnp.power(ROTARY_BASE, -dims / half)[None, :]
            radians = positions * ang_freqs
            cos = jnp.cos(radians)[None, None].astype(x.dtype)
            sin = jnp.sin(radians)[None, None].astype(x.dtype)
            even, odd = jnp.split(x, 2, axis=-1)
            r_even = even * cos - odd * sin
            r_odd = even * sin + odd * cos
            return jnp.concatenate([r_even, r_odd], axis=-1)
        key = jax.random.key(seed)
        ks = jax.random.split(key, 5)
        B, T, M, D = (4, 256, 128, D_HEAD)
        H = M // D
        x = jax.random.normal(ks[0], (B, T, M), dtype=jnp.float32)
        scale = M ** (-0.5)
        wq = jax.random.normal(ks[1], (H, M, D), dtype=jnp.float32) * scale
        wk = jax.random.normal(ks[2], (H, M, D), dtype=jnp.float32) * scale
        wv = jax.random.normal(ks[3], (H, M, D), dtype=jnp.float32) * scale
        wo = jax.random.normal(ks[4], (H, D, M), dtype=jnp.float32) * scale
        return {'x': x, 'wq': wq, 'wk': wk, 'wv': wv, 'wo': wo}
    _L0_attn_in = _L0_attn_setup()

    def _L0_ffn_setup():
        import jax, jax.numpy as jnp
        import numpy as np
        B, S, D = (2, 128, 128)
        L, H = (64, 16)
        HD = L // H
        F, E, K = (256, 8, 2)
        THETA = 10000.0
        EPS = 1e-05

        def _rmsnorm(x, g):
            return x * g * jax.lax.rsqrt(jnp.mean(x * x, axis=-1, keepdims=True) + EPS)

        def _rope(t, pos):
            inv_freq = 1.0 / THETA ** (jnp.arange(0, HD, 2, dtype=jnp.float32) / HD)
            ang = pos[:, None].astype(jnp.float32) * inv_freq[None, :]
            cos, sin = (jnp.cos(ang), jnp.sin(ang))
            t1, t2 = (t[..., 0::2], t[..., 1::2])
            r1 = t1 * cos - t2 * sin
            r2 = t1 * sin + t2 * cos
            return jnp.stack([r1, r2], axis=-1).reshape(t.shape)

        def _forward(x, g1, g2, w_down, wq, wk, wv, w_up, router_w, w1, w2, w3):
            b, s, _ = x.shape
            pos = jnp.arange(s)
            h = _rmsnorm(x, g1)
            c = h @ w_down
            split = lambda t: t.reshape(b, s, H, HD).transpose(0, 2, 1, 3)
            q = _rope(split(c @ wq), pos)
            k = _rope(split(c @ wk), pos)
            v = split(c @ wv)
            scores = jnp.einsum('bhqd,bhkd->bhqk', q, k) / jnp.sqrt(jnp.float32(HD))
            causal = jnp.tril(jnp.ones((s, s), bool))
            scores = jnp.where(causal, scores, -jnp.inf)
            attn = jax.nn.softmax(scores, axis=-1)
            o = jnp.einsum('bhqk,bhkd->bhqd', attn, v).transpose(0, 2, 1, 3).reshape(b, s, L)
            x = x + o @ w_up
            res = x
            t = _rmsnorm(x, g2).reshape(-1, D)
            probs = jax.nn.softmax(t @ router_w, axis=-1)
            vals, idx = jax.lax.top_k(probs, K)
            w = vals / jnp.sum(vals, axis=-1, keepdims=True)
            gate = jnp.sum(jax.nn.one_hot(idx, E, dtype=t.dtype) * w[..., None], axis=1)
            hid = jax.nn.silu(jnp.einsum('td,edf->tef', t, w1)) * jnp.einsum('td,edf->tef', t, w3)
            y_e = jnp.einsum('tef,efd->ted', hid, w2)
            y = jnp.einsum('ted,te->td', y_e, gate)
            return res + y.reshape(b, s, D)
        key = jax.random.key(seed)
        ks = jax.random.split(key, 12)
        g = lambda k, shape, scale: jax.random.normal(k, shape, dtype=jnp.float32) * scale
        return {'x': g(ks[0], (B, S, D), 1.0), 'g1': jnp.ones((D,), jnp.float32), 'g2': jnp.ones((D,), jnp.float32), 'w_down': g(ks[1], (D, L), 0.02), 'wq': g(ks[2], (L, L), 0.02), 'wk': g(ks[3], (L, L), 0.02), 'wv': g(ks[4], (L, L), 0.02), 'w_up': g(ks[5], (L, D), 0.02), 'router_w': g(ks[6], (D, E), 0.02), 'w1': g(ks[7], (E, D, F), 0.02), 'w3': g(ks[8], (E, D, F), 0.02), 'w2': g(ks[9], (E, F, D), 0.02)}
    _L0_ffn_in = _L0_ffn_setup()
    _d = {'L0_attn_x': _L0_attn_in['x'], 'L0_attn_wq': _L0_attn_in['wq'], 'L0_attn_wk': _L0_attn_in['wk'], 'L0_attn_wv': _L0_attn_in['wv'], 'L0_attn_wo': _L0_attn_in['wo'], 'L0_ffn_g1': _L0_ffn_in['g1'], 'L0_ffn_g2': _L0_ffn_in['g2'], 'L0_ffn_w_down': _L0_ffn_in['w_down'], 'L0_ffn_wq': _L0_ffn_in['wq'], 'L0_ffn_wk': _L0_ffn_in['wk'], 'L0_ffn_wv': _L0_ffn_in['wv'], 'L0_ffn_w_up': _L0_ffn_in['w_up'], 'L0_ffn_router_w': _L0_ffn_in['router_w'], 'L0_ffn_w1': _L0_ffn_in['w1'], 'L0_ffn_w2': _L0_ffn_in['w2'], 'L0_ffn_w3': _L0_ffn_in['w3']}
    _x0 = _d['L0_attn_x']
    _d['L0_attn_x'] = jax.random.normal(jax.random.fold_in(jax.random.key(seed), 1), (8, 512, 128), dtype=_x0.dtype)
    del _x0
    return _d

def reference(L0_attn_x, L0_attn_wq, L0_attn_wk, L0_attn_wv, L0_attn_wo, L0_ffn_g1, L0_ffn_g2, L0_ffn_w_down, L0_ffn_wq, L0_ffn_wk, L0_ffn_wv, L0_ffn_w_up, L0_ffn_router_w, L0_ffn_w1, L0_ffn_w2, L0_ffn_w3):

    def _L0_attn_ref(x, wq, wk, wv, wo):
        import jax, jax.numpy as jnp
        import numpy as np
        INFTY_APPROX = 1e+30
        ROTARY_BASE = 10000.0
        D_HEAD = 128

        def rope(x):
            *_, length, width = x.shape
            half = width // 2
            positions = jnp.arange(length)[:, None].astype(x.dtype)
            dims = jnp.arange(half).astype(x.dtype)
            ang_freqs = jnp.power(ROTARY_BASE, -dims / half)[None, :]
            radians = positions * ang_freqs
            cos = jnp.cos(radians)[None, None].astype(x.dtype)
            sin = jnp.sin(radians)[None, None].astype(x.dtype)
            even, odd = jnp.split(x, 2, axis=-1)
            r_even = even * cos - odd * sin
            r_odd = even * sin + odd * cos
            return jnp.concatenate([r_even, r_odd], axis=-1)
        q = jnp.einsum('bim,hmd->bhid', x, wq)
        k = jnp.einsum('bim,hmd->bhid', x, wk)
        v = jnp.einsum('bim,hmd->bhid', x, wv)
        q = rope(q)
        k = rope(k)
        mult = jnp.asarray(D_HEAD ** (-0.5), dtype=x.dtype)
        s = jnp.einsum('bhid,bhjd->bhij', q * mult, k * mult)
        T = s.shape[-1]
        i = jnp.arange(T)[:, None]
        j = jnp.arange(T)[None, :]
        mask = (i < j).astype(s.dtype)[None, None]
        s = s - jnp.asarray(INFTY_APPROX, dtype=s.dtype) * mask
        p = jax.nn.softmax(s, axis=-1)
        o = jnp.einsum('bhij,bhjd->bhid', p, v)
        r = jnp.einsum('bhid,hdm->bim', o, wo)
        return r

    def _L0_ffn_ref(x, g1, g2, w_down, wq, wk, wv, w_up, router_w, w1, w2, w3):
        import jax, jax.numpy as jnp
        import numpy as np
        B, S, D = (2, 128, 128)
        L, H = (64, 16)
        HD = L // H
        F, E, K = (256, 8, 2)
        THETA = 10000.0
        EPS = 1e-05

        def _rmsnorm(x, g):
            return x * g * jax.lax.rsqrt(jnp.mean(x * x, axis=-1, keepdims=True) + EPS)

        def _rope(t, pos):
            inv_freq = 1.0 / THETA ** (jnp.arange(0, HD, 2, dtype=jnp.float32) / HD)
            ang = pos[:, None].astype(jnp.float32) * inv_freq[None, :]
            cos, sin = (jnp.cos(ang), jnp.sin(ang))
            t1, t2 = (t[..., 0::2], t[..., 1::2])
            r1 = t1 * cos - t2 * sin
            r2 = t1 * sin + t2 * cos
            return jnp.stack([r1, r2], axis=-1).reshape(t.shape)

        def _forward(x, g1, g2, w_down, wq, wk, wv, w_up, router_w, w1, w2, w3):
            b, s, _ = x.shape
            pos = jnp.arange(s)
            h = _rmsnorm(x, g1)
            c = h @ w_down
            split = lambda t: t.reshape(b, s, H, HD).transpose(0, 2, 1, 3)
            q = _rope(split(c @ wq), pos)
            k = _rope(split(c @ wk), pos)
            v = split(c @ wv)
            scores = jnp.einsum('bhqd,bhkd->bhqk', q, k) / jnp.sqrt(jnp.float32(HD))
            causal = jnp.tril(jnp.ones((s, s), bool))
            scores = jnp.where(causal, scores, -jnp.inf)
            attn = jax.nn.softmax(scores, axis=-1)
            o = jnp.einsum('bhqk,bhkd->bhqd', attn, v).transpose(0, 2, 1, 3).reshape(b, s, L)
            x = x + o @ w_up
            res = x
            t = _rmsnorm(x, g2).reshape(-1, D)
            probs = jax.nn.softmax(t @ router_w, axis=-1)
            vals, idx = jax.lax.top_k(probs, K)
            w = vals / jnp.sum(vals, axis=-1, keepdims=True)
            gate = jnp.sum(jax.nn.one_hot(idx, E, dtype=t.dtype) * w[..., None], axis=1)
            hid = jax.nn.silu(jnp.einsum('td,edf->tef', t, w1)) * jnp.einsum('td,edf->tef', t, w3)
            y_e = jnp.einsum('tef,efd->ted', hid, w2)
            y = jnp.einsum('ted,te->td', y_e, gate)
            return res + y.reshape(b, s, D)
        return _forward(x, g1, g2, w_down, wq, wk, wv, w_up, router_w, w1, w2, w3)
    x = L0_attn_x
    x = x + _layernorm(_L0_attn_ref(_layernorm(x, axis=-1), L0_attn_wq, L0_attn_wk, L0_attn_wv, L0_attn_wo), axis=-1)
    x = x + _layernorm(_L0_ffn_ref(_layernorm(x, axis=-1), L0_ffn_g1, L0_ffn_g2, L0_ffn_w_down, L0_ffn_wq, L0_ffn_wk, L0_ffn_wv, L0_ffn_w_up, L0_ffn_router_w, L0_ffn_w1, L0_ffn_w2, L0_ffn_w3), axis=-1)
    return x

_drawn_inputs = setup_inputs


def setup_inputs(seed=0):
    import zlib

    import numpy as np

    out = dict(_drawn_inputs(seed))
    spreads = {'L0_ffn_g1': (1.0, 0.6), 'L0_ffn_g2': (1.0, 0.6)}
    factors = {'L0_ffn_w_down': 8.0,
     'L0_ffn_wq': 8.0,
     'L0_ffn_wk': 8.0,
     'L0_ffn_wv': 8.0,
     'L0_ffn_w_up': 8.0,
     'L0_ffn_router_w': 8.0,
     'L0_ffn_w1': 8.0,
     'L0_ffn_w2': 8.0,
     'L0_ffn_w3': 8.0}
    for name, (base, spread) in spreads.items():
        noise = np.random.default_rng([zlib.crc32(name.encode()), seed]).standard_normal(out[name].shape)
        drawn = base * np.exp(spread * noise) if base else spread * noise
        out[name] = jnp.asarray(drawn.astype(out[name].dtype))
    for name, factor in factors.items():
        out[name] = (out[name] * factor).astype(out[name].dtype)
    return out
```

```python
from contextlib import ExitStack

import concourse.bass as bass
from concourse import mybir

F32 = mybir.dt.float32
BF16 = mybir.dt.bfloat16
ACT = mybir.ActivationFunctionType
ALU = mybir.AluOpType
AX = mybir.AxisListType.X

P = 128
NB = 8
T = 512
NT = T // P
D = 128
L = 64
H = 16
HD = L // H
R = 4
G = H // R
SLOTS = 8
NE = 8
F = 256
FH = F // P
EPS = 1e-5
SCALE_A = 1.0 / D
SCALE_B = HD ** -0.5

JOBS = {
    "a_xT": ["a_xT"], "a_qkv": [f"a_qkv{t}" for t in range(NT)], "a_qkT": ["a_qT", "a_kT"],
    "a_scores": [f"a_s{t}" for t in range(NT)], "a_pT": ["a_p0", "a_p1", "a_p2"],
    "a_out": ["a_oT", "a_r"],
    "p_hT": ["p_hT"], "p_cT": ["p_cT"], "p_qkv": ["p_qkv0", "p_qkv1"],
    "p_rows": ["p_k0", "p_k1", "p_q0", "p_q1"],
    "m_max0": [f"max0_{n}" for n in range(11)],
    "m_finish": ["o3", "oT", "up", "tT", "logits"],
}
for _g in range(G):
    JOBS[f"m_shift{_g}"] = [f"shift{_g}"]
    JOBS[f"m_mix{_g}"] = [f"max{_g + 1}_{n}" for n in range(11)] if _g + 1 < G else []
    JOBS[f"m_pv{_g}"] = [f"o{_g - 1}"] if _g else []

SCHEDULE = [
    "a_xT", "p_hT", "m_max0", "a_qkv", "p_cT", "m_shift0", "m_mix0", "p_qkv",
    "m_shift1", "m_mix1", "m_pv0", "a_qkT", "m_shift2", "m_mix2", "m_pv1", "a_scores", "p_rows",
    "m_shift3", "m_mix3", "m_pv2", "a_pT", "a_out", "m_pv3", "m_finish",
]


def steps(stages):
    return [s for s in SCHEDULE if s[0] in stages]


def jobs(stages):
    return [j for s in steps(stages) for j in JOBS[s]]


MAX_JOBS = [(3, r, 1) for r in range(R)] + [(2, r, 1) for r in range(R)] + [(1, 0, 2), (1, 2, 2), (0, 0, R)]
PT_AT = {0: 0, 1: 512, 3: 896}
EXPS = R + 1
CREDIT = 1
N_CONSTS, N_WEIGHTS, N_FILLS = 19, 3 + NE, 7


class Batch:

    def __init__(self, n, parity):
        self.n, self.parity, self.now = n, parity, n + 1


class Ring:

    def __init__(self, full, free, order, before):
        self.full, self.free, self.order, self.before = full, free, order, before

    def bank(self, job):
        return self.order.index(job) % 2

    def count(self, job):
        return self.before + self.order.index(job) // 2 + 1


def wait(eng, sem, value):
    if not (isinstance(value, int) and value <= 0):
        eng.wait_ge(sem, value)


def program(nc, x, wq_a, wk_a, wv_a, wo_a, g1, g2, w_down, wq_b, wk_b, wv_b, w_up, router_w,
            w1, w2, w3, cos_a, sin_a, cos_b, sin_b, ident_f, future, future_t, slot_index, out):
    with ExitStack() as ctx:
        def sb(name, shape, dt=F32):
            return ctx.enter_context(nc.sbuf_tensor(name, shape, dt))

        def ps(name, shape, dt=F32):
            return ctx.enter_context(nc.psum_tensor(name, shape, dt))

        def sem(name):
            return ctx.enter_context(nc.semaphore(name))

        wqkv_a = sb("wqkv_a_sb", [P, 3 * D])
        wo_sb = sb("wo_sb", [P, D])
        wdown_sb = sb("wdown_sb", [P, L])
        wqkv_b = sb("wqkv_b_sb", [L, 3 * L])
        wup_sb = sb("wup_sb", [L, D])
        router_sb = sb("router_sb", [P, NE])
        g1_sb = sb("g1_sb", [P, 1])
        g2_sb = sb("g2_sb", [P, 1])
        cos_a_sb = sb("cos_a_sb", [P, NT, D])
        sin_a_sb = sb("sin_a_sb", [P, NT, D])
        cos_b_sb = sb("cos_b_sb", [P, 2, NT, L])
        sin_b_sb = sb("sin_b_sb", [P, 2, NT, L])
        idf = sb("idf", [P, P])
        idb = sb("idb", [P, P], BF16)
        future_sb = sb("future_sb", [P, R, P], BF16)
        future_T = sb("future_T", [P, 2, P], BF16)
        neg_half = sb("neg_half", [P, NT])
        x1 = sb("x1", [P, NB, NT, D])
        res = sb("res", [P, NB, NT, D])
        logits = sb("logits", [P, NB, NT, NE])
        future_in = sb("future_in", [P, P])
        future_t_in = sb("future_t_in", [P, P])
        a_st = sb("a_st", [P, NT, 6])
        a_mv = sb("a_mv", [P, NT, 2])
        a_ve = sb("a_ve", [P, NT])
        a_rstd = sb("a_rstd", [P, NT])
        a_xn = sb("a_xn", [P, NT, D])
        a_xT = sb("a_xT_sb", [P, T])
        a_qkv = sb("a_qkv_sb", [P, NT, 3 * D])
        a_work = sb("a_work", [P, 2, NT * 2 * D])
        a_m1, a_m2 = (a_work[:, n, :].rearrange("p (t a d) -> p t a d", t=NT, a=2) for n in range(2))
        a_qT = sb("a_qT_sb", [P, T])
        a_kT = sb("a_kT_sb", [P, T])
        a_nm = sb("a_nm", [P, NT])
        a_nb = sb("a_nb", [P, NT])
        a_p = sb("a_p_sb", [P, NT, T])
        a_sum = sb("a_sum", [P, NT])
        a_ri = sb("a_ri", [P, NT])
        a_pT = a_work[:, :, :].rearrange("p n w -> p (n w)")[:, 0:3 * T].rearrange("p (n w) -> p n w", n=3)
        p_st = sb("p_st", [P, NT, 6])
        p_mv = sb("p_mv", [P, NT, 2])
        p_ve = sb("p_ve", [P, NT])
        p_rstd = sb("p_rstd", [P, NT])
        p_m1 = sb("p_m1", [P, NT])
        p_m2 = sb("p_m2", [P, NT])
        p_ms = sb("p_ms", [P, NT])
        p_rs = sb("p_rs", [P, NT])
        h0 = sb("h0", [P, 2, NT, D])
        p_hT = sb("p_hT_sb", [P, T])
        p_cT = sb("p_cT_sb", [L, T])
        p_qk = sb("p_qk", [P, 2, NT, L])
        p_t1 = sb("p_t1", [P, 2, NT, L])
        p_t2 = sb("p_t2", [P, 2, NT, L])
        part1 = sb("part1", [P, 2, NT * H, HD], BF16)
        part2 = sb("part2", [P, 2, NT * H, HD], BF16)
        part3 = sb("part3", [P, 2, NT * H, HD], BF16)
        q_rows = sb("q_rows", [P, 2, NT, H, SLOTS, HD], BF16)
        k_rows = sb("k_rows", [P, NT, H, SLOTS, HD], BF16)
        k_all = sb("k_all", [P, G, T], BF16)
        kz = sb("kz", [P, 2, G, R, T], BF16)
        qT1 = sb("qT1", [P, 2, G, T], BF16)
        v_pad = sb("v_pad", [P, 2, NT, H, HD + 1])
        nmax = sb("nmax", [P, NT, H])
        nm_r1 = sb("nm_r1", [P, NT, R])
        nm_r2 = sb("nm_r2", [P, NT, R])
        qT2 = sb("qT2", [P, 2, T], BF16)
        pT = sb("pT", [P, 2, EXPS, 2 * T])
        oT_g = sb("oT_g", [P, 2, T])
        inv = sb("inv", [P, 2, NT, R])
        o_tok = sb("o_tok", [P, NT, L])
        oT_sb = sb("oT_sb", [L, T])
        m_sq = sb("m_sq", [P, NT])
        m_ms = sb("m_ms", [P, NT])
        m_rs = sb("m_rs", [P, NT])
        m_t = sb("m_t", [P, NT, D])
        m_tT = sb("m_tT", [P, T])
        def carve(tensor, shapes):
            views, at = [], 0
            for shape in shapes:
                size, names = 1, " ".join(f"d{n}" for n in range(len(shape)))
                for n in shape:
                    size *= n
                view = tensor[:, at:at + size]
                views.append(view.rearrange(f"p ({names}) -> p {names}",
                                            **{f"d{n}": v for n, v in enumerate(shape)}))
                at += size
            return views

        w1_sb, w3_sb, w2_sb, tT = carve(kz[:, :, :, :, :].rearrange("p a g r t -> p (a g r t)").bitcast(F32),
                                        [[NE, F], [NE, F], [NE, FH, D], [2, T]])
        hid, silu, y, gate, hot, lg2, e_tmp, slot_sb, top = carve(
            pT[:, :, :, :].rearrange("p a s t -> p (a s t)"),
            [[2, FH, T], [FH, T], [NT, D], [NB, NT, NE], [2, NB * NT, NE], [NB * NT, NE], [NB * NT, NE],
             [NB * NT, NE], [NB * NT, 4]])
        tokens_T = nc.dram_tensor("tokens_T", (NB, P, T), F32).ap()

        small = ps("small", [P, 2, T])
        wide = ps("wide", [P, 2, 2 * T])
        acc = ps("acc", [P, 2, T])

        small_full = [sem(f"small_full{i}") for i in range(2)]
        small_free = [sem(f"small_free{i}") for i in range(2)]
        wide_full = [sem(f"wide_full{i}") for i in range(2)]
        wide_free = [sem(f"wide_free{i}") for i in range(2)]
        acc_full = [sem(f"acc_full{i}") for i in range(2)]
        acc_free = [sem(f"acc_free{i}") for i in range(2)]
        consts_in = sem("consts_in")
        weights_in = sem("weights_in")
        fills = sem("fills")
        x_first = sem("x_first")
        x_rest = sem("x_rest")
        names = ["a_stats", "a_var", "a_vareps", "a_rstd", "a_xn", "a_rope1", "a_rope", "a_nmax", "a_nbias",
                 "a_exp", "a_inv", "a_r", "a_rstats", "a_rvar", "a_rvareps", "a_rrstd", "a_rn", "x1_ready",
                 "p_stats", "p_var", "p_vareps", "p_rstd", "p_h0", "p_w1", "p_w2", "p_ms", "p_rs",
                 "p_rope1", "p_rope", "p_part1", "p_rest1", "p_part2", "p_rest2", "p_part3", "p_rows",
                 "sq_done", "m_ms", "m_rs", "m_t", "res_ready", "up_done"]
        S = {n: sem("s_" + n) for n in names}
        kz_in = sem("kz_in")
        tT_kept = sem("tT_kept")
        tT_in = [sem("tT_in0"), sem("tT_in1")]
        cut = sem("cut")
        inv_done = sem("inv_done")
        filled = sem("filled")
        silu_done = [sem("silu_done0"), sem("silu_done1")]
        top_diff = sem("top_diff")
        top_exp = sem("top_exp")
        final_stats = sem("final_stats")
        final_mean = sem("final_mean")
        final_var = sem("final_var")
        final_norm = sem("final_norm")
        final_out = sem("final_out")
        final_step = sem("final_step")
        final_pow = sem("final_pow")
        out_done = sem("out_done")

        block = ctx.enter_context(nc.Block())

        def iterations(eng, body):
            nA, nAP, nAPM, nPM = (len(jobs(s)) for s in ("a", "ap", "apm", "pm"))
            wide_per = G * EXPS

            def one(stages, a, p, m, before, wide_before):
                ring = Ring(small_full, small_free, jobs(stages), before)
                body(stages, a, p, m, ring, wide_before)

            one("a", Batch(0, 0), None, None, 0, CREDIT)
            one("ap", Batch(1, 1), Batch(0, 0), None, nA // 2, CREDIT)
            with eng.Fori(1, NB // 2) as j:
                for par in range(2):
                    b = eng.snap(2 * j + par)
                    before = eng.snap((b - 2) * (nAPM // 2) + (nA + nAP) // 2)
                    one("apm", Batch(b, par), Batch(b - 1, 1 - par), Batch(b - 2, par), before,
                        eng.snap((b - 2) * (wide_per // 2) + CREDIT))
            before = (nA + nAP) // 2 + (NB - 2) * nAPM // 2
            one("pm", None, Batch(NB - 1, 1), Batch(NB - 2, 0), before, (NB - 2) * wide_per // 2 + CREDIT)
            one("m", None, None, Batch(NB - 1, 1), before + nPM // 2, (NB - 1) * wide_per // 2 + CREDIT)

        small_jobs = (len(jobs("a")) + len(jobs("ap")) + len(jobs("pm")) + len(jobs("m"))
                      + (NB - 2) * len(jobs("apm")))

        def held(eng, sem_, value):
            value = value if isinstance(value, int) else eng.compute_val(value)
            eng.wait_ge(fills, 1)
            wait(eng, sem_, value)

        @block.sync
        def _(sp):
            def load_x(n, loaded):
                sp.dma_start(x1[:, n, :, :], x[n].rearrange("(t p) d -> p t d", p=P)).then_inc(loaded, 16)

            load_x(0, x_first)
            for dst, src in ((idf[:, :], ident_f), (future_in[:, :], future), (future_t_in[:, :], future_t),
                             (wqkv_a[:, 0:D], wq_a[0]), (wqkv_a[:, D:2 * D], wk_a[0]),
                             (wqkv_a[:, 2 * D:3 * D], wv_a[0]),
                             (cos_a_sb[:, :, :], cos_a), (sin_a_sb[:, :, :], sin_a), (wo_sb[:, :], wo_a[0]),
                             (wdown_sb[:, :], w_down), (wqkv_b[:, 0:L], wq_b), (wqkv_b[:, L:2 * L], wk_b),
                             (wqkv_b[:, 2 * L:3 * L], wv_b), (wup_sb[:, :], w_up), (router_sb[:, :], router_w),
                             (g1_sb[:, :], g1.rearrange("(d o) -> d o", o=1)),
                             (g2_sb[:, :], g2.rearrange("(d o) -> d o", o=1)),
                             (cos_b_sb[:, :, :, :], cos_b), (sin_b_sb[:, :, :, :], sin_b),
                             ):
                sp.dma_start(dst, src).then_inc(consts_in, 16)
            for n in range(1, NB):
                load_x(n, x_rest)
            def body(stages, a, p, m, ring, wide_before):
                for step in steps(stages):
                    if step == "p_rows":
                        counts = [sp.compute_val(ring.count(j)) for j in ("p_k0", "p_k1")]
                        sp.wait_ge(fills, 1)
                        for j, c in zip(("p_k0", "p_k1"), counts):
                            sp.wait_ge(small_free[ring.bank(j)], c)
                        for r in range(R):
                            sp.dma_start(kz[32 * r:32 * r + 32, p.parity, :, r, :],
                                         k_all[32 * r:32 * r + 32, :, :]).then_inc(kz_in, 16)
                    if step == "m_finish":
                        c = sp.compute_val(ring.count("tT"))
                        sp.wait_ge(fills, 1)
                        sp.wait_ge(small_free[ring.bank("tT")], c)
                        sp.dma_start(tokens_T[m.n], m_tT[:, :]).then_inc(tT_kept, 16)

            sp.wait_ge(fills, N_FILLS)
            iterations(sp, body)
            sp.wait_ge(acc_full[(G - 1) % 2], CREDIT + NB * G // 2)
            sp.dma_start(slot_sb[:, :, :], slot_index).then_inc(weights_in, 16)
            sp.dma_start(w1_sb[:, :, :], w1.rearrange("e d f -> d e f")).then_inc(weights_in, 16)
            sp.dma_start(w3_sb[:, :, :], w3.rearrange("e d f -> d e f")).then_inc(weights_in, 16)
            for e in range(NE):
                sp.dma_start(w2_sb[:, e, :, :], w2[e].rearrange("(h p) d -> p h d", p=P)).then_inc(weights_in, 16)
            sp.wait_ge(tT_kept, 16 * (CREDIT + NB))
            for b in range(NB):
                if b >= 2:
                    sp.wait_ge(wide_full[1], CREDIT + NB * G * EXPS // 2 + (b - 1) * NE)
                sp.dma_start(tT[:, b % 2, :], tokens_T[b]).then_inc(tT_in[b % 2], 16)
            with sp.Fori(0, NB) as b:
                sp.wait_ge(final_out, b + 1)
                sp.dma_start(out[b].rearrange("(t p) d -> p t d", p=P), x1[:, b, :, :]).then_inc(out_done, 16)
            sp.wait_ge(out_done, 16 * NB)

        @block.tensor
        def _(pe):
            def take(ring, job, after=(), alone=False):
                need = [0, 0]
                need[ring.bank(job)] = ring.order.index(job) // 2
                for j in after:
                    need[ring.bank(j)] = max(need[ring.bank(j)], ring.order.index(j) // 2 + 1)
                for bank in range(2):
                    if need[bank] or bank == ring.bank(job):
                        (held if alone else wait)(pe, small_free[bank], ring.before + need[bank])
                return small[:, ring.bank(job), :]

            def ready(ring, job):
                pe.wait_ge(small_free[ring.bank(job)], ring.count(job))

            def full(ring, job, last):
                last.then_inc(small_full[ring.bank(job)], 1)

            def max_job(m, ring, g, n):
                job = f"max{g}_{n}"
                tile, r0, heads = MAX_JOBS[n]
                keys = (tile + 1) * P
                bank = take(ring, job)
                for r in range(r0, r0 + heads):
                    at = (r - r0) * keys
                    pe.matmul(bank[:, at:at + keys], qT1[:, m.parity, g, tile * P:(tile + 1) * P],
                              kz[:, m.parity, g, r, 0:keys], start=(r == r0), stop=False, skip_group_check=True)
                diagonal = bank[:, 0:heads * keys].rearrange("p (h k) -> p h k", h=heads)[:, :, keys - P:keys]
                last = pe.matmul(diagonal, idb[:, :], future_sb[:, 0:heads, :], start=False, stop=True,
                                 skip_group_check=True)
                full(ring, job, last)

            def exp_job(m, wide_before, g, s):
                w = g * EXPS + s
                wait(pe, wide_free[w % 2], wide_before + w // 2)
                bank = wide[:, w % 2, :]
                if s < R:
                    blocks = [(s, tile, at) for tile, at in PT_AT.items()]
                    diagonals = [bank[:, 0:P], bank[:, T:2 * T].rearrange("p (n k) -> p n k", k=P)[:, 0:NT:3, :]]
                else:
                    blocks = [(r, 2, r * 2 * P) for r in range(R)]
                    diagonals = [bank[:, n * T:(n + 1) * T].rearrange("p (n k) -> p n k", k=P)[:, 0:NT:2, :]
                                 for n in range(2)]
                for r, tile, at in blocks:
                    pe.matmul(bank[:, at:at + T - tile * P], kz[:, m.parity, g, r, tile * P:(tile + 1) * P],
                              qT2[:, g % 2, tile * P:T], start=(at % T == 0), stop=False, skip_group_check=True)
                for diagonal in diagonals:
                    n = 1 if len(diagonal.shape) == 2 else 2
                    last = pe.matmul(diagonal, idb[:, :], future_T[:, 0:n, :] if n > 1 else future_T[:, 0, :],
                                     start=False, stop=True, skip_group_check=True)
                last.then_inc(wide_full[w % 2], 1)

            def transposes(ring, job, source, rows, ident, after=(), alone=False):
                bank = take(ring, job, after, alone)
                for t in range(NT):
                    last = pe.transpose(bank[0:rows, t * P:(t + 1) * P], source(t), ident)
                full(ring, job, last)

            def turn_o(ring, g):
                pe.wait_ge(acc_free[g % 2], CREDIT + 2 * ring.m.n + g // 2 + 1)
                transposes(ring, f"o{g}", lambda t: oT_g[:, g % 2, t * P:(t + 1) * P], P, idf[:, :])

            def body(stages, a, p, m, ring, wide_before):
                ring.m = m
                for step in steps(stages):
                    if step == "a_xT":
                        pe.wait_ge(S["a_xn"], a.now)
                        transposes(ring, "a_xT", lambda t: a_xn[:, t, :], P, idf[:, :])
                    elif step == "a_qkv":
                        for t in range(NT):
                            bank = take(ring, f"a_qkv{t}", ["a_xT"] if t == 0 else ())
                            full(ring, f"a_qkv{t}", pe.matmul(bank[:, 0:3 * D], a_xT[:, t * P:(t + 1) * P],
                                                              wqkv_a[:, :], start=True, stop=True))
                    elif step == "a_qkT":
                        pe.wait_ge(S["a_rope"], a.now)
                        transposes(ring, "a_qT", lambda t: a_m1[:, t, 0, :], P, idf[:, :])
                        transposes(ring, "a_kT", lambda t: a_m1[:, t, 1, :], P, idf[:, :])
                    elif step == "a_scores":
                        for t in range(NT):
                            keys = (t + 1) * P
                            bank = take(ring, f"a_s{t}", ["a_qT", "a_kT"] if t == 0 else ())
                            pe.matmul(bank[:, 0:keys], a_qT[:, t * P:keys], a_kT[:, 0:keys],
                                      start=True, stop=False, skip_group_check=True)
                            full(ring, f"a_s{t}", pe.matmul(bank[:, t * P:keys], idb[:, :], future_sb[:, 0, :],
                                                            start=False, stop=True, skip_group_check=True))
                    elif step == "a_pT":
                        for job, blocks in (("a_p0", [(0, 0), (1, 0), (2, 0), (3, 0)]),
                                            ("a_p1", [(1, 1), (2, 1), (3, 1), (3, 3)]),
                                            ("a_p2", [(2, 2), (3, 2)])):
                            bank = take(ring, job, ["a_s2", "a_s3"] if job == "a_p0" else ())
                            for n, (i, k) in enumerate(blocks):
                                last = pe.transpose(bank[:, n * P:(n + 1) * P], a_p[:, i, k * P:(k + 1) * P], idf[:, :])
                            full(ring, job, last)
                    elif step == "a_out":
                        bank = take(ring, "a_oT", ["a_p0", "a_p1", "a_p2"])
                        for k, (n, at) in enumerate(((0, 0), (1, 0), (2, 0), (1, 3 * P))):
                            last = pe.matmul(bank[:, k * P:T], a_qkv[:, k, 2 * D:3 * D],
                                             a_pT[:, n, at:at + T - k * P], start=(k == 0), stop=(k == NT - 1),
                                             skip_group_check=True)
                        full(ring, "a_oT", last)
                        bank = take(ring, "a_r", ["a_oT"])
                        for t in range(NT):
                            last = pe.matmul(bank[:, t * P:(t + 1) * P], a_xT[:, t * P:(t + 1) * P], wo_sb[:, :],
                                             start=True, stop=True)
                        full(ring, "a_r", last)
                    elif step == "p_hT":
                        pe.wait_ge(S["p_h0"], p.now)
                        transposes(ring, "p_hT", lambda t: h0[:, p.parity, t, :], P, idf[:, :])
                    elif step == "p_cT":
                        bank = take(ring, "p_cT", ["p_hT"])
                        full(ring, "p_cT", pe.matmul(bank[0:L, :], wdown_sb[:, :], p_hT[:, :], start=True, stop=True))
                    elif step == "p_qkv":
                        for n in range(2):
                            bank = take(ring, f"p_qkv{n}", ["p_cT"] if n == 0 else ())
                            for t in (2 * n, 2 * n + 1):
                                at = (t % 2) * 3 * L
                                last = pe.matmul(bank[:, at:at + 3 * L], p_cT[:, t * P:(t + 1) * P], wqkv_b[:, :],
                                                 start=True, stop=True)
                            full(ring, f"p_qkv{n}", last)
                    elif step == "p_rows":
                        pe.wait_ge(S["p_rows"], p.now)
                        for kind, rows in (("k", lambda t, g: k_rows[:, t, g * R:(g + 1) * R, :, :]),
                                           ("q", lambda t, g: q_rows[:, p.parity, t, g * R:(g + 1) * R, :, :])):
                            for n in range(2):
                                bank = take(ring, f"p_{kind}{n}").bitcast(BF16)
                                for g in (2 * n, 2 * n + 1):
                                    for t in range(NT):
                                        at = (g % 2) * T + t * P
                                        last = pe.transpose(bank[:, at:at + P],
                                                            rows(t, g).rearrange("p h s d -> p (h s d)"), idb[:, :])
                                full(ring, f"p_{kind}{n}", last)
                    elif step == "m_max0":
                        pe.wait_ge(kz_in, 16 * R * m.now)
                        for n in range(len(MAX_JOBS)):
                            max_job(m, ring, 0, n)
                    elif step.startswith("m_shift"):
                        g = int(step[-1])
                        pe.wait_ge(cut, 5 * (G * m.n + g + 1))
                        bank = take(ring, step[2:]).bitcast(BF16)
                        for t in range(NT):
                            rows = q_rows[:, m.parity, t, g * R:(g + 1) * R, :, :].rearrange("p h s d -> p (h s d)")
                            last = pe.transpose(bank[:, t * P:(t + 1) * P], rows, idb[:, :])
                        full(ring, step[2:], last)
                    elif step.startswith("m_mix"):
                        g = int(step[-1])
                        ready(ring, f"shift{g}")
                        for s in range(EXPS):
                            exp_job(m, wide_before, g, s)
                            if g + 1 < G:
                                for n in range(len(MAX_JOBS) * s // EXPS, len(MAX_JOBS) * (s + 1) // EXPS):
                                    max_job(m, ring, g + 1, n)
                    elif step.startswith("m_pv"):
                        g = int(step[-1])
                        for w in (g * EXPS + EXPS - 2, g * EXPS + EXPS - 1):
                            pe.wait_ge(wide_free[w % 2], wide_before + w // 2 + 1)
                        wait(pe, acc_free[g % 2], CREDIT + 2 * m.n + g // 2)
                        for k in range(NT):
                            for r in range(R):
                                if k == 2:
                                    probs = pT[:, g % 2, R, r * 2 * P:(r + 1) * 2 * P]
                                else:
                                    probs = pT[:, g % 2, r, PT_AT[k]:PT_AT[k] + T - k * P]
                                last = pe.matmul(acc[32 * r:32 * r + HD + 1, g % 2, k * P:T],
                                                 v_pad[:, m.parity, k, g * R + r, :], probs,
                                                 start=(k == 0), stop=(k == NT - 1), skip_group_check=True)
                        last.then_inc(acc_full[g % 2], 1)
                        if g:
                            turn_o(ring, g - 1)
                    elif step == "m_finish":
                        turn_o(ring, G - 1)
                        transposes(ring, "oT", lambda t: o_tok[:, t, :], L, idf[:, :], [f"o{G - 1}"], alone=True)
                        bank = take(ring, "up", ["oT"])
                        for t in range(NT):
                            last = pe.matmul(bank[:, t * P:(t + 1) * P], oT_sb[:, t * P:(t + 1) * P], wup_sb[:, :],
                                             start=True, stop=True)
                        full(ring, "up", last)
                        pe.wait_ge(S["m_t"], m.now)
                        transposes(ring, "tT", lambda t: m_t[:, t, :], P, idf[:, :])
                        bank = take(ring, "logits", ["tT"])
                        for t in range(NT):
                            last = pe.matmul(bank[:, t * NE:(t + 1) * NE], m_tT[:, t * P:(t + 1) * P], router_sb[:, :],
                                             start=True, stop=True)
                        full(ring, "logits", last)

            pe.wait_ge(consts_in, 16 * N_CONSTS)
            pe.wait_ge(fills, N_FILLS)
            iterations(pe, body)

            pe.wait_ge(weights_in, 16 * N_WEIGHTS)
            with pe.Fori(0, NB // 2) as pair:
              for par in range(2):
                b = pe.snap(2 * pair + par)
                pe.wait_ge(tT_in[par], 16 * pair + 16)
                hid_jobs = pe.snap(b * NE + CREDIT + NB * G * EXPS // 2)
                y_jobs = pe.snap(b * (NE // 2) + CREDIT + NB * G // 2)

                def hidden(e):
                    for f in range(FH):
                        pe.wait_ge(wide_free[f], hid_jobs + e)
                        tokens = tT[:, par, :]
                        pe.matmul(wide[:, f, 0:T], w1_sb[:, e, f * P:(f + 1) * P], tokens, start=True, stop=True)
                        pe.matmul(wide[:, f, T:2 * T], w3_sb[:, e, f * P:(f + 1) * P], tokens,
                                  start=True, stop=True).then_inc(wide_full[f], 1)

                def down(e):
                    for f in range(FH):
                        pe.wait_ge(wide_free[f], hid_jobs + e + 1)
                    pe.wait_ge(acc_free[e % 2], y_jobs + e // 2)
                    for t in range(NT):
                        for f in range(FH):
                            last = pe.matmul(acc[:, e % 2, t * P:(t + 1) * P], hid[:, e % 2, f, t * P:(t + 1) * P],
                                             w2_sb[:, e, f, :], start=(f == 0), stop=(f == FH - 1))
                    last.then_inc(acc_full[e % 2], 1)

                for e in range(NE):
                    hidden(e)
                    if e:
                        down(e - 1)
                down(NE - 1)

        @block.scalar
        def _(act):
            def evacuate(ring, job, out_, in_=None, scale=1.0, before=()):
                b = small[:, ring.bank(job), :]
                act.wait_ge(small_full[ring.bank(job)], ring.count(job))
                act.activation(out_, b if in_ is None else in_(b), ACT.Copy, scale=scale)\
                   .then_inc(small_free[ring.bank(job)], 1)

            def body(stages, a, p, m, ring, wide_before):
                for step in steps(stages):
                    if step == "a_xT":
                        evacuate(ring, "a_xT", a_xT[:, :])
                    elif step == "a_qkv":
                        for t in range(NT):
                            evacuate(ring, f"a_qkv{t}", a_qkv[:, t, :], lambda b: b[:, 0:3 * D])
                    elif step == "a_qkT":
                        evacuate(ring, "a_qT", a_qT[:, :])
                    elif step == "a_scores":
                        for t in range(NT):
                            keys = (t + 1) * P
                            job = f"a_s{t}"
                            act.wait_ge(S["a_nbias"], NT * a.n + t + 1)
                            act.activation(a_p[:, t, 0:keys], small[:, ring.bank(job), 0:keys], ACT.Exp,
                                           bias=a_nb[:, t:t + 1], scale=SCALE_A, accum_out=a_sum[:, t:t + 1])\
                               .then_inc(small_free[ring.bank(job)], 1)
                    elif step == "a_pT":
                        evacuate(ring, "a_p0", a_pT[:, 0, :])
                        evacuate(ring, "a_p2", a_pT[:, 2, 0:2 * P], lambda b: b[:, 0:2 * P])
                    elif step == "a_out":
                        evacuate(ring, "a_oT", a_xT[:, :])
                    elif step == "p_hT":
                        evacuate(ring, "p_hT", p_hT[:, :], scale=g1_sb[:, 0:1])
                    elif step == "p_cT":
                        evacuate(ring, "p_cT", p_cT[:, :], lambda b: b[0:L, :])
                    elif step == "p_qkv":
                        act.wait_ge(S["p_rs"], p.now)
                        for n in range(2):
                            job = f"p_qkv{n}"
                            act.wait_ge(small_full[ring.bank(job)], ring.count(job))
                            for t in (2 * n, 2 * n + 1):
                                bank = small[:, ring.bank(job), (t % 2) * 3 * L:(t % 2 + 1) * 3 * L]
                                act.activation(p_qk[:, :, t, :], bank[:, 0:2 * L].rearrange("p (a l) -> p a l", a=2),
                                               ACT.Copy, scale=p_rs[:, t:t + 1])
                                last = act.activation(v_pad[:, p.parity, t, :, 0:HD],
                                                      bank[:, 2 * L:3 * L].rearrange("p (h d) -> p h d", h=H),
                                                      ACT.Copy, scale=p_rs[:, t:t + 1])
                            last.then_inc(small_free[ring.bank(job)], 1)
                    elif step == "p_rows":
                        for n in range(2):
                            evacuate(ring, f"p_q{n}", qT1[:, p.parity, 2 * n:2 * n + 2, :].rearrange("p g t -> p (g t)"),
                                     lambda b: b.bitcast(BF16))
                    elif step.startswith("m_mix"):
                        g = int(step[-1])
                        wait(act, acc_full[g % 2], CREDIT + 2 * m.n + g // 2)
                        for s in range(EXPS):
                            w = g * EXPS + s
                            act.wait_ge(wide_full[w % 2], wide_before + w // 2 + 1)
                            act.activation(pT[:, g % 2, s, :], wide[:, w % 2, :], ACT.Exp, scale=SCALE_B)\
                               .then_inc(wide_free[w % 2], 1)
                    elif step.startswith("m_pv"):
                        g = int(step[-1])
                        act.wait_ge(acc_full[g % 2], CREDIT + 2 * m.n + g // 2 + 1)
                        act.activation(oT_g[:, g % 2, :], acc[:, g % 2, :], ACT.Copy).then_inc(acc_free[g % 2], 1)
                    elif step == "m_finish":
                        evacuate(ring, "oT", oT_sb[:, :], lambda b: b[0:L, :])
                        act.wait_ge(small_free[ring.bank("up")], ring.count("up"))
                        for t in range(NT):
                            last = act.activation(m_t[:, t, :], res[:, m.n, t, :], ACT.Square,
                                                  accum_out=m_sq[:, t:t + 1])
                        last.then_inc(S["sq_done"], 1)
                        act.wait_ge(tT_kept, 16 * (CREDIT + m.n))
                        evacuate(ring, "tT", m_tT[:, :], scale=g2_sb[:, 0:1])

            act.wait_ge(consts_in, 16 * N_CONSTS)
            act.wait_ge(fills, N_FILLS)
            iterations(act, body)
            act.wait_ge(top_diff, 1)
            act.activation(top[:, :, 3], top[:, :, 2], ACT.Exp).then_inc(top_exp, 1)
            with act.Fori(0, NB) as b:
                hid_jobs = act.snap(b * NE + CREDIT + NB * G * EXPS // 2)
                for e in range(NE):
                    for f in range(FH):
                        act.wait_ge(wide_full[f], hid_jobs + e + 1)
                        act.wait_ge(wide_free[f], hid_jobs + e)
                        act.activation(silu[:, f, :], wide[:, f, 0:T], ACT.Silu).then_inc(silu_done[f], 1)

        @block.gpsimd
        def _(pool):
            def rsqrt(out_, in_, need, value, done):
                pool.wait_ge(need, value)
                pool.tensor_tensor(out_, in_, neg_half[:, :], ALU.pow).then_inc(done, 1)

            def body(stages, a, p, m, ring, wide_before):
                for step in steps(stages):
                    if step == "a_xT":
                        rsqrt(a_rstd[:, :], a_ve[:, :], S["a_vareps"], a.now, S["a_rstd"])
                    elif step == "p_hT":
                        rsqrt(p_rstd[:, :], p_ve[:, :], S["p_vareps"], p.now, S["p_rstd"])
                        rsqrt(p_rs[:, :], p_ms[:, :], S["p_ms"], p.now, S["p_rs"])
                    elif step == "a_qkv":
                        for j in ("a_qkv2", "a_qkv3"):
                            pool.wait_ge(small_free[ring.bank(j)], ring.count(j))
                        qk = a_qkv[:, :, 0:2 * D].rearrange("p t (a d) -> p t a d", a=2)
                        for n in range(2):
                            pool.tensor_tensor(a_m1[:, :, n, :], qk[:, :, n, :], cos_a_sb[:, :, :],
                                               ALU.mult).then_inc(S["a_rope1"], 1)
                            for half in range(2):
                                lo, other = half * D // 2, (1 - half) * D // 2
                                pool.tensor_tensor(a_m2[:, :, n, lo:lo + D // 2], qk[:, :, n, other:other + D // 2],
                                                   sin_a_sb[:, :, lo:lo + D // 2], ALU.mult).then_inc(S["a_rope1"], 1)
                        pool.wait_ge(S["a_rope1"], 6 * a.now)
                        pool.tensor_tensor(a_m1[:, :, :, :], a_m1[:, :, :, :], a_m2[:, :, :, :],
                                           ALU.add).then_inc(S["a_rope"], 1)
                    elif step == "a_out":
                        rsqrt(a_rstd[:, :], a_ve[:, :], S["a_rvareps"], a.now, S["a_rrstd"])
                        pool.wait_ge(S["a_rn"], a.now)
                        pool.tensor_tensor(x1[:, a.n, :, :], x1[:, a.n, :, :], a_xn[:, :, :],
                                           ALU.add).then_inc(S["x1_ready"], 1)
                    elif step == "p_qkv":
                        for j in ("p_qkv0", "p_qkv1"):
                            pool.wait_ge(small_free[ring.bank(j)], ring.count(j))
                        flat = lambda b: b[:, :, :, :].rearrange("p a t l -> p (a t l)")
                        qk, t1, t2, cos, sin = (flat(b) for b in (p_qk, p_t1, p_t2, cos_b_sb, sin_b_sb))
                        pair = lambda b, n: b.rearrange("p (n two) -> p n two", two=2)[:, :, n]
                        pool.tensor_tensor(t1, qk, cos, ALU.mult).then_inc(S["p_rope1"], 1)
                        for n in range(2):
                            pool.tensor_tensor(pair(t2, n), pair(qk, 1 - n), pair(sin, n),
                                               ALU.mult).then_inc(S["p_rope1"], 1)
                        pool.wait_ge(S["p_rope1"], 3 * p.now)
                        pool.tensor_tensor(t1, t1, t2, ALU.add).then_inc(S["p_rope"], 1)
                        parts = [b[:, :, :, :].rearrange("p a n d -> p (a n d)") for b in (part1, part2, part3)]
                        held(pool, S["p_rope"], p.now)
                        pool.tensor_copy(parts[0], t1).then_inc(S["p_part1"], 1)
                        pool.wait_ge(S["p_part1"], p.now)
                        pool.tensor_tensor(t2, t1, parts[0], ALU.subtract).then_inc(S["p_rest1"], 1)
                        held(pool, S["p_rest1"], p.now)
                        pool.tensor_copy(parts[1], t2).then_inc(S["p_part2"], 1)
                        pool.wait_ge(S["p_part2"], p.now)
                        pool.tensor_tensor(t1, t2, parts[1], ALU.subtract).then_inc(S["p_rest2"], 1)
                        held(pool, S["p_rest2"], p.now)
                        pool.tensor_copy(parts[2], t1).then_inc(S["p_part3"], 1)
                        held(pool, S["p_part3"], p.now)
                        q = q_rows[:, p.parity, :, :, :, :].rearrange("p t h s d -> p (t h) s d")
                        k = k_rows[:, :, :, :, :].rearrange("p t h s d -> p (t h) s d")
                        for b, n, lo, hi, step_ in ((part1, 3, 0, 3, 1), (part2, 2, 3, 5, 1), (part3, 1, 5, 6, 1)):
                            src = b[:, 0, :, :].unsqueeze(2).to_broadcast([P, NT * H, n, HD])
                            pool.tensor_copy(q[:, :, lo:hi, :], src)
                        pool.memset(q[:, :, 6, 0:3], 0.0)
                        for b, slots in ((part1, (0, 3, 5)), (part2, (1, 4)), (part3, (2,))):
                            for s in slots:
                                last = pool.tensor_copy(k[:, :, s, :], b[:, 1, :, :])
                        last.then_inc(S["p_rows"], 1)
                    elif step == "m_finish":
                        rsqrt(m_rs[:, :], m_ms[:, :], S["m_ms"], m.now, S["m_rs"])
                        pool.wait_ge(S["m_rs"], m.now)
                        pool.tensor_tensor(m_t[:, :, :], res[:, m.n, :, :],
                                           m_rs[:, :].unsqueeze(2).to_broadcast([P, NT, D]),
                                           ALU.mult).then_inc(S["m_t"], 1)

            for s in (*wide_full, *wide_free, *acc_full, *acc_free):
                pool.sem_inc(s, CREDIT)
            pool.sem_inc(tT_kept, 16 * CREDIT)
            pool.memset(neg_half[:, :], -0.5).then_inc(fills, 1)
            pool.memset(kz[:, :, :, :, :].rearrange("p a g r t -> p (a g r t)").bitcast(F32), 0.0).then_inc(fills, 1)
            pool.wait_ge(fills, N_FILLS)
            pool.wait_ge(consts_in, 16 * N_CONSTS)
            iterations(pool, body)
            with pool.Fori(0, NB) as b:
                pool.wait_ge(final_var, b + 1)
                pool.tensor_tensor(a_rstd[:, :], a_ve[:, :], neg_half[:, :], ALU.pow).then_inc(final_pow, 1)
                pool.wait_ge(final_norm, b + 1)
                pool.tensor_tensor(x1[:, b, :, :], x1[:, b, :, :], a_xn[:, :, :], ALU.add).then_inc(final_out, 1)

        @block.vector
        def _(dve):
            def empty(ring, job, ins):
                ins.then_inc(small_free[ring.bank(job)], 1)

            def await_job(ring, job):
                dve.wait_ge(small_full[ring.bank(job)], ring.count(job))
                return small[:, ring.bank(job), :]

            def norm_stats(src, st, mv, ve, now, stats, var, vareps):
                for t in range(NT):
                    last = dve.bn_stats(st[:, t, :], src(t))
                last.then_inc(stats, 1)
                held(dve, stats, now)
                for t in range(NT):
                    last = dve.bn_aggr(mv[:, t, :], st[:, t, :])
                last.then_inc(var, 1)
                dve.wait_ge(var, now)
                dve.tensor_scalar(ve[:, :], mv[:, :, 1], EPS, None, ALU.add).then_inc(vareps, 1)

            def normalise(dst, src, mv, rstd, done):
                for t in range(NT):
                    last = dve.tensor_scalar(dst(t), src(t), mv[:, t, 0:1], rstd[:, t:t + 1],
                                             ALU.subtract, ALU.mult)
                last.then_inc(done, 1)

            def max_job(m, ring, g, n):
                job = f"max{g}_{n}"
                tile, r0, heads = MAX_JOBS[n]
                bank = await_job(ring, job)
                ins = dve.tensor_reduce(nmax[:, tile, g * R + r0:g * R + r0 + heads],
                                        bank[:, 0:heads * (tile + 1) * P].rearrange("p (h k) -> p h k", h=heads),
                                        AX, ALU.max, negate=True)
                empty(ring, job, ins)

            def body(stages, a, p, m, ring, wide_before):
                for step in steps(stages):
                    if step == "a_xT":
                        if isinstance(a.n, int) and a.n == 0:
                            dve.wait_ge(x_first, 16)
                        else:
                            dve.wait_ge(x_rest, 16 * (NB - 1))
                        norm_stats(lambda t: x1[:, a.n, t, :], a_st, a_mv, a_ve, a.now,
                                   S["a_stats"], S["a_var"], S["a_vareps"])
                        dve.wait_ge(S["a_rstd"], a.now)
                        normalise(lambda t: a_xn[:, t, :], lambda t: x1[:, a.n, t, :], a_mv, a_rstd, S["a_xn"])
                    elif step == "a_qkT":
                        empty(ring, "a_kT", dve.tensor_copy(a_kT[:, :], await_job(ring, "a_kT")))
                    elif step == "a_scores":
                        for t in range(NT):
                            bank = await_job(ring, f"a_s{t}")
                            dve.tensor_reduce(a_nm[:, t:t + 1], bank[:, 0:(t + 1) * P], AX, ALU.max, negate=True)\
                               .then_inc(S["a_nmax"], 1)
                            dve.wait_ge(S["a_nmax"], NT * a.n + t + 1)
                            dve.tensor_scalar(a_nb[:, t:t + 1], a_nm[:, t:t + 1], SCALE_A, None, ALU.mult)\
                               .then_inc(S["a_nbias"], 1)
                    elif step == "a_pT":
                        empty(ring, "a_p1", dve.tensor_copy(a_pT[:, 1, :], await_job(ring, "a_p1")))
                    elif step == "a_out":
                        dve.wait_ge(small_free[ring.bank("a_s3")], ring.count("a_s3"))
                        dve.reciprocal(a_ri[:, :], a_sum[:, :]).then_inc(S["a_inv"], 1)
                        bank = await_job(ring, "a_r")
                        dve.wait_ge(S["a_inv"], a.now)
                        ins = dve.tensor_tensor(a_xn[:, :, :], bank.rearrange("p (t d) -> p t d", t=NT),
                                                a_ri[:, :].unsqueeze(2).to_broadcast([P, NT, D]), ALU.mult)
                        empty(ring, "a_r", ins)
                        held(dve, small_free[ring.bank("a_r")], ring.count("a_r"))
                        norm_stats(lambda t: a_xn[:, t, :], a_st, a_mv, a_ve, a.now,
                                   S["a_rstats"], S["a_rvar"], S["a_rvareps"])
                        dve.wait_ge(S["a_rrstd"], a.now)
                        normalise(lambda t: a_xn[:, t, :], lambda t: a_xn[:, t, :], a_mv, a_rstd, S["a_rn"])
                    elif step == "p_hT":
                        held(dve, S["x1_ready"], p.now)
                        norm_stats(lambda t: x1[:, p.n, t, :], p_st, p_mv, p_ve, p.now,
                                   S["p_stats"], S["p_var"], S["p_vareps"])
                        dve.wait_ge(S["p_rstd"], p.now)
                        normalise(lambda t: h0[:, p.parity, t, :], lambda t: x1[:, p.n, t, :], p_mv, p_rstd, S["p_h0"])
                        dve.tensor_tensor(p_m1[:, :], p_mv[:, :, 1], p_rstd[:, :], ALU.mult).then_inc(S["p_w1"], 1)
                        dve.wait_ge(S["p_w1"], p.now)
                        dve.tensor_tensor(p_m2[:, :], p_m1[:, :], p_rstd[:, :], ALU.mult).then_inc(S["p_w2"], 1)
                        dve.wait_ge(S["p_w2"], p.now)
                        dve.tensor_scalar(p_ms[:, :], p_m2[:, :], EPS, None, ALU.add).then_inc(S["p_ms"], 1)
                    elif step == "p_rows":
                        wait(dve, kz_in, 16 * R * p.n)
                        for n in range(2):
                            bank = await_job(ring, f"p_k{n}").bitcast(BF16)
                            empty(ring, f"p_k{n}", dve.tensor_copy(
                                k_all[:, 2 * n:2 * n + 2, :].rearrange("p g t -> p (g t)"), bank))
                    elif step == "m_max0":
                        for n in range(len(MAX_JOBS)):
                            max_job(m, ring, 0, n)
                    elif step.startswith("m_shift"):
                        g = int(step[-1])
                        last_max = f"max{g}_{len(MAX_JOBS) - 1}"
                        heads = slice(g * R, (g + 1) * R)
                        slot = q_rows[:, m.parity, :, heads, 6, :]
                        mx = nmax[:, :, heads]
                        dve.wait_ge(small_free[ring.bank(last_max)], ring.count(last_max))
                        n = 5 * (G * m.n + g)
                        dve.tensor_copy(slot[:, :, :, 0], mx).then_inc(cut, 1)
                        dve.wait_ge(cut, n + 1)
                        dve.tensor_tensor(nm_r1[:, :, :], mx, slot[:, :, :, 0], ALU.subtract).then_inc(cut, 1)
                        dve.wait_ge(cut, n + 2)
                        dve.tensor_copy(slot[:, :, :, 1], nm_r1[:, :, :]).then_inc(cut, 1)
                        dve.wait_ge(cut, n + 3)
                        dve.tensor_tensor(nm_r2[:, :, :], nm_r1[:, :, :], slot[:, :, :, 1], ALU.subtract).then_inc(cut, 1)
                        dve.wait_ge(cut, n + 4)
                        dve.tensor_copy(slot[:, :, :, 2], nm_r2[:, :, :]).then_inc(cut, 1)
                        bank = await_job(ring, step[2:]).bitcast(BF16)
                        empty(ring, step[2:], dve.tensor_copy(qT2[:, g % 2, :], bank[:, 0:T]))
                    elif step.startswith("m_mix"):
                        g = int(step[-1])
                        if g + 1 < G:
                            for n in range(len(MAX_JOBS)):
                                max_job(m, ring, g + 1, n)
                    if step.startswith("m_pv") and step[-1] != "0" or step == "m_finish":
                        g = G - 1 if step == "m_finish" else int(step[-1]) - 1
                        bank = await_job(ring, f"o{g}").rearrange("p (t r c) -> p t r c", t=NT, r=R)
                        dve.reciprocal(inv[:, g % 2, :, :], bank[:, :, :, HD]).then_inc(inv_done, 1)
                        dve.wait_ge(inv_done, G * m.n + g + 1)
                        o = o_tok[:, :, :].rearrange("p t (g r d) -> p t g r d", g=G, r=R)[:, :, g, :, :]
                        empty(ring, f"o{g}", dve.tensor_tensor(
                            o, bank[:, :, :, 0:HD], inv[:, g % 2, :, :].unsqueeze(3).to_broadcast([P, NT, R, HD]), ALU.mult))
                    if step == "m_finish":
                        bank = await_job(ring, "up")
                        dve.tensor_tensor(res[:, m.n, :, :], bank.rearrange("p (t d) -> p t d", t=NT),
                                          h0[:, m.parity, :, :], ALU.add).then_inc(small_free[ring.bank("up")], 1)
                        dve.wait_ge(S["sq_done"], m.now)
                        dve.tensor_scalar(m_ms[:, :], m_sq[:, :], 1.0 / D, EPS, ALU.mult, ALU.add)\
                           .then_inc(S["m_ms"], 1)
                        bank = await_job(ring, "logits")
                        empty(ring, "logits", dve.tensor_copy(
                            logits[:, m.n, :, :], bank[:, 0:NT * NE].rearrange("p (t e) -> p t e", t=NT)))

            dve.memset(q_rows[:, :, :, :, :, :].rearrange("p a t h s d -> p (a t h s d)").bitcast(F32), 0.0)\
               .then_inc(fills, 1)
            dve.memset(k_rows[:, :, :, :, :].rearrange("p t h s d -> p (t h s d)").bitcast(F32), 0.0).then_inc(filled, 1)
            dve.memset(v_pad[:, :, :, :, :].rearrange("p a t h c -> p (a t h c)"), 0.0).then_inc(filled, 1)
            dve.memset(acc[:, :, :].rearrange("p a t -> p (a t)"), 0.0).then_inc(fills, 1)
            dve.wait_ge(filled, 2)
            dve.memset(k_rows[:, :, :, 6, 0:3].rearrange("p t h c -> p (t h) c"), 1.0).then_inc(fills, 1)
            dve.memset(v_pad[:, :, :, :, HD].rearrange("p a t h -> p (a t h)"), 1.0).then_inc(fills, 1)
            dve.wait_ge(consts_in, 16 * N_CONSTS)
            dve.tensor_copy(idb[:, :], idf[:, :])
            dve.tensor_copy(future_sb[:, :, :], future_in[:, :].unsqueeze(1).to_broadcast([P, R, P]))
            dve.tensor_copy(future_T[:, :, :], future_t_in[:, :].unsqueeze(1).to_broadcast([P, 2, P]))\
               .then_inc(fills, 1)
            dve.wait_ge(fills, N_FILLS)
            iterations(dve, body)

            dve.wait_ge(weights_in, 16 * N_WEIGHTS)
            lg = logits[:, :, :, :].rearrange("p b t e -> p (b t) e")
            wide_of = lambda c: top[:, :, c:c + 1].to_broadcast([P, NB * NT, NE])
            count = 0

            def then(ins):
                nonlocal count
                count += 1
                ins.then_inc(final_step, 1)
                dve.wait_ge(final_step, count)

            dve.wait_ge(small_free[Ring(None, None, jobs("m"), 0).bank("logits")], small_jobs // 2)
            scores = lg
            for n in range(2):
                then(dve.tensor_reduce(top[:, :, n], scores, AX, ALU.max))
                then(dve.tensor_tensor(e_tmp[:, :, :], scores, wide_of(n), ALU.is_equal))
                then(dve.tensor_tensor(e_tmp[:, :, :], e_tmp[:, :, :], slot_sb[:, :, :], ALU.mult))
                then(dve.tensor_reduce(top[:, :, 2], e_tmp[:, :, :], AX, ALU.max))
                then(dve.tensor_tensor(hot[:, n, :, :], slot_sb[:, :, :], wide_of(2), ALU.is_equal))
                if n == 0:
                    then(dve.scalar_tensor_tensor(out=lg2[:, :, :], in0=hot[:, 0, :, :], scalar=-3.0e38, in1=lg,
                                                  op0=ALU.mult, op1=ALU.add))
                    scores = lg2[:, :, :]
            dve.tensor_tensor(top[:, :, 2], top[:, :, 1], top[:, :, 0], ALU.subtract).then_inc(top_diff, 1)
            dve.wait_ge(top_exp, 1)
            then(dve.tensor_scalar(top[:, :, 0], top[:, :, 3], 1.0, None, ALU.add))
            then(dve.reciprocal(top[:, :, 1], top[:, :, 0]))
            then(dve.tensor_tensor(top[:, :, 2], top[:, :, 3], top[:, :, 1], ALU.mult))
            then(dve.tensor_tensor(hot[:, 0, :, :], hot[:, 0, :, :], wide_of(1), ALU.mult))
            then(dve.tensor_tensor(hot[:, 1, :, :], hot[:, 1, :, :], wide_of(2), ALU.mult))
            then(dve.tensor_tensor(gate[:, :, :, :].rearrange("p b t e -> p (b t) e"),
                                   hot[:, 0, :, :], hot[:, 1, :, :], ALU.add))

            with dve.Fori(0, NB) as b:
                hid_jobs = dve.snap(b * NE + CREDIT + NB * G * EXPS // 2)
                y_jobs = dve.snap(b * (NE // 2) + CREDIT + NB * G // 2)

                def hidden(e):
                    for f in range(FH):
                        if e >= 2:
                            dve.wait_ge(acc_full[e % 2], y_jobs + e // 2)
                        dve.wait_ge(silu_done[f], b * NE + e + 1)
                        dve.tensor_tensor(hid[:, e % 2, f, :], silu[:, f, :], wide[:, f, T:2 * T], ALU.mult)\
                           .then_inc(wide_free[f], 1)

                def add(e):
                    dve.wait_ge(acc_full[e % 2], y_jobs + e // 2 + 1)
                    for t in range(NT):
                        ins = dve.scalar_tensor_tensor(out=y[:, t, :], in0=acc[:, e % 2, t * P:(t + 1) * P],
                                                       scalar=gate[:, b, t, e:e + 1],
                                                       in1=y[:, t, :] if e else res[:, b, t, :],
                                                       op0=ALU.mult, op1=ALU.add)
                    ins.then_inc(acc_free[e % 2], 1)
                    dve.wait_ge(acc_free[e % 2], y_jobs + e // 2 + 1)

                for e in range(NE):
                    hidden(e)
                    if e:
                        add(e - 1)
                add(NE - 1)
                norm_stats(lambda t: y[:, t, :], a_st, a_mv, a_ve, b + 1, final_stats, final_mean, final_var)
                dve.wait_ge(final_pow, b + 1)
                normalise(lambda t: a_xn[:, t, :], lambda t: y[:, t, :], a_mv, a_rstd, final_norm)


def tables():
    import numpy as np

    def by_tile(a):
        return np.ascontiguousarray(a.reshape(NT, P, -1).transpose(1, 0, 2))

    f32 = np.float32
    pos = np.arange(T, dtype=f32)[:, None]
    half = D // 2
    freq = np.power(f32(10000.0), -np.arange(half, dtype=f32) / f32(half)).astype(f32)
    ang = pos * freq[None, :]
    cos, sin = np.cos(ang).astype(f32), np.sin(ang).astype(f32)
    cos_a = by_tile(np.concatenate([cos, cos], 1))
    sin_a = by_tile(np.concatenate([-sin, sin], 1))
    inv = (f32(1.0) / np.power(f32(10000.0), np.arange(0, HD, 2, dtype=f32) / f32(HD))).astype(f32)
    ang = pos * inv[None, :]
    cos, sin = np.cos(ang).astype(f32), np.sin(ang).astype(f32)
    cos_b = np.tile(np.repeat(cos, 2, 1), (1, H))
    sin_b = np.tile(np.stack([-sin, sin], -1).reshape(T, HD), (1, H))
    cos_b, sin_b = (np.ascontiguousarray(np.stack([by_tile(a)] * 2, 1)) for a in (cos_b, sin_b))
    q, k = np.arange(P)[:, None], np.arange(P)[None, :]
    future = np.where(k > q, f32(-1e30), f32(0))
    slot_index = np.ascontiguousarray(np.broadcast_to(np.arange(NE, 0, -1, dtype=f32), (P, NB * NT, NE)))
    return {"cos_a": cos_a, "sin_a": sin_a, "cos_b": cos_b, "sin_b": sin_b, "ident_f": np.eye(P, dtype=f32),
            "future": future, "future_t": np.ascontiguousarray(future.T), "slot_index": slot_index}


INPUTS = ["L0_attn_x", "L0_attn_wq", "L0_attn_wk", "L0_attn_wv", "L0_attn_wo", "L0_ffn_g1", "L0_ffn_g2",
          "L0_ffn_w_down", "L0_ffn_wq", "L0_ffn_wk", "L0_ffn_wv", "L0_ffn_w_up", "L0_ffn_router_w",
          "L0_ffn_w1", "L0_ffn_w2", "L0_ffn_w3"]


def kernel(**inputs):
    import numpy as np
    import concourse.bacc as bacc
    from concourse.bass_utils import run_bass_kernel_spmd

    nc = bacc.Bacc("TRN2", target_bir_lowering=False, num_devices=1)
    arrays = {name: np.ascontiguousarray(inputs[name]) for name in INPUTS}
    arrays.update(tables())
    args = [nc.dram_tensor(n, a.shape, mybir.dt.from_np(a.dtype), kind="ExternalInput").ap()
            for n, a in arrays.items()]
    out = nc.dram_tensor("out", (NB, T, D), F32, kind="ExternalOutput").ap()
    program(nc, *args, out)
    r = run_bass_kernel_spmd(nc, [arrays], core_ids=[0])
    return r.results[0]["out"]
```

```python
from contextlib import ExitStack

import concourse.bass as bass
from concourse import mybir

F32 = mybir.dt.float32
BF16 = mybir.dt.bfloat16
ACT = mybir.ActivationFunctionType
ALU = mybir.AluOpType
AX = mybir.AxisListType.X

P = 128
NB = 8
T = 512
NT = T // P
D = 128
L = 64
H = 16
HD = L // H
R = 4
G = H // R
SLOTS = 8
NE = 8
F = 256
FH = F // P
EPS = 1e-5
SCALE_A = 1.0 / D
SCALE_B = HD ** -0.5

JOBS = {
    "a_xT": ["a_xT"], **{f"a_qkv{t}": [f"a_qkv{t}"] for t in range(NT)}, "a_qkT": ["a_qT", "a_kT"],
    **{f"a_s{t}": [f"a_s{t}"] for t in range(NT)}, "a_pT": ["a_p0", "a_p1", "a_p2"],
    "a_oT": ["a_oT"], "a_r": ["a_r"],
    "p_hT": ["p_hT"], "p_cT": ["p_cT"], "p_qkv": ["p_qkv0", "p_qkv1"],
    "p_rows": ["p_k0", "p_k1", "p_q0", "p_q1"],
    "f_pv3": ["pv3", "o2"], "f_o": ["o3"], "f_oT": ["oT"], "f_up": ["up"], "f_tT": ["tT"], "f_logits": ["logits"],
    "m_pv0": ["pv0"], "m_pv1": ["pv1", "o0"], "f_pv2": ["pv2", "o1"],
}
for _g in range(G):
    JOBS[f"m_shift{_g}"] = [f"shift{_g}"]

MAX_JOBS = [(3, r, 1) for r in range(R)] + [(2, r, 1) for r in range(R)] + [(1, 0, 2), (1, 2, 2), (0, 0, R)]
PT_AT = {0: 0, 1: 512, 3: 896}
EXPS = R + 1


def mix_max(s):
    return range(len(MAX_JOBS) * s // EXPS, len(MAX_JOBS) * (s + 1) // EXPS)


SCHEDULE = [
    "m_cut0", "f_pv2", "m_shift0", "a_stats",
    "m_mix00", "a_norm", "m_mix01", "a_xT", "p_stats", "m_mix02", "a_qkv0", "a_qkv1", "p_norm", "m_mix03", "a_qkv2", "a_qkv3",
    "m_mix04", "m_cut1", "f_pv3", "m_shift1", "p_hT",
    "m_mix10", "p_cT", "m_mix11", "p_qkv", "m_mix12", "f_o", "m_mix13", "f_oT", "m_mix14", "m_cut2", "m_pv0", "m_shift2", "f_up",
    "m_mix20", "a_qkT", "m_mix21", "a_s0", "m_mix22", "a_s1", "m_mix23", "a_s2", "m_mix24", "a_s3",
    "m_cut3", "m_pv1", "p_rows", "m_shift3", "a_pT",
    "m_mix30", "f_tT", "m_mix31", "a_oT", "m_mix32", "a_r", "f_logits", "m_mix33", "a_rstats", "m_mix34", "a_rnorm",
    "p_max0",
]


def steps(stages):
    return [s for s in SCHEDULE if s[0] in stages and not (s == "p_max0" and "m" in stages)]


def jobs(stages):
    order = []
    for step in steps(stages):
        if step.startswith("m_mix"):
            g, s = int(step[-2]) + 1, int(step[-1])
            if g < G or "p" in stages:
                order += [f"max{g % G}_{n}" for n in mix_max(s)]
        elif step == "p_max0":
            order += [f"max0_{n}" for n in range(len(MAX_JOBS))]
        else:
            order += JOBS.get(step, [])
    return order


CREDIT = 1
N_CONSTS, N_WEIGHTS, N_FILLS = 19, 3 + NE, 6


def is_max(job):
    return job.startswith("max")


class Batch:

    def __init__(self, n, parity):
        self.n, self.parity, self.now = n, parity, n + 1


class Rings:

    def __init__(self, full, free, order, before):
        self.full, self.free, self.before = full, free, before
        self.order = ([j for j in order if is_max(j)], [j for j in order if not is_max(j)])

    def index(self, job):
        ring = not is_max(job)
        return self.order[ring].index(job) + self.before[ring][1]

    def bank(self, job):
        return self.index(job) % 2 + (0 if is_max(job) else 2)

    def turns(self, job):
        return self.index(job) // 2

    def count(self, job):
        return self.turns_before(self.bank(job)) + self.turns(job) + 1

    def turns_before(self, bank):
        return self.before[bank // 2][0]


def wait(eng, sem, value):
    if not (isinstance(value, int) and value <= 0):
        eng.wait_ge(sem, value)


def program(nc, x, wq_a, wk_a, wv_a, wo_a, g1, g2, w_down, wq_b, wk_b, wv_b, w_up, router_w,
            w1, w2, w3, cos_a, sin_a, cos_b, sin_b, ident_f, future, future_t, slot_index, out):
    with ExitStack() as ctx:
        def sb(name, shape, dt=F32):
            return ctx.enter_context(nc.sbuf_tensor(name, shape, dt))

        def ps(name, shape, dt=F32):
            return ctx.enter_context(nc.psum_tensor(name, shape, dt))

        def sem(name):
            return ctx.enter_context(nc.semaphore(name))

        wqkv_a = sb("wqkv_a_sb", [P, 3 * D])
        wo_sb = sb("wo_sb", [P, D])
        wdown_sb = sb("wdown_sb", [P, L])
        wqkv_b = sb("wqkv_b_sb", [L, 3 * L])
        wup_sb = sb("wup_sb", [L, D])
        router_sb = sb("router_sb", [P, NE])
        g1_sb = sb("g1_sb", [P, 1])
        g2_sb = sb("g2_sb", [P, 1])
        cos_a_sb = sb("cos_a_sb", [P, NT, D])
        sin_a_sb = sb("sin_a_sb", [P, NT, D])
        cos_b_sb = sb("cos_b_sb", [P, 2, NT, L])
        sin_b_sb = sb("sin_b_sb", [P, 2, NT, L])
        idf = sb("idf", [P, P])
        idb = sb("idb", [P, P], BF16)
        future_sb = sb("future_sb", [P, R, P], BF16)
        future_T = sb("future_T", [P, 2, P], BF16)
        neg_half = sb("neg_half", [P, NT])
        x1 = sb("x1", [P, NB, NT, D])
        res = sb("res", [P, NB, NT, D])
        logits = sb("logits", [P, NB, NT, NE])
        future_in = sb("future_in", [P, P])
        future_t_in = sb("future_t_in", [P, P])
        a_st = sb("a_st", [P, NT, 6])
        a_mv = sb("a_mv", [P, NT, 2])
        a_ve = sb("a_ve", [P, NT])
        a_rstd = sb("a_rstd", [P, NT])
        a_xn = sb("a_xn", [P, NT, D])
        a_xT = sb("a_xT_sb", [P, T])
        a_qkv = sb("a_qkv_sb", [P, NT, 3 * D])
        a_work = sb("a_work", [P, 2, NT * 2 * D])
        a_m1, a_m2 = (a_work[:, n, :].rearrange("p (t a d) -> p t a d", t=NT, a=2) for n in range(2))
        a_qT = sb("a_qT_sb", [P, T])
        a_kT = sb("a_kT_sb", [P, T])
        a_nm = sb("a_nm", [P, NT])
        a_nb = sb("a_nb", [P, NT])
        a_p = sb("a_p_sb", [P, NT, T])
        a_sum = sb("a_sum", [P, NT])
        a_ri = sb("a_ri", [P, NT])
        a_pT = a_work[:, :, :].rearrange("p n w -> p (n w)")[:, 0:3 * T].rearrange("p (n w) -> p n w", n=3)
        p_st = sb("p_st", [P, NT, 6])
        p_mv = sb("p_mv", [P, NT, 2])
        p_ve = sb("p_ve", [P, NT])
        p_rstd = sb("p_rstd", [P, NT])
        p_m1 = sb("p_m1", [P, NT])
        p_m2 = sb("p_m2", [P, NT])
        p_ms = sb("p_ms", [P, NT])
        p_rs = sb("p_rs", [P, NT])
        h0 = sb("h0", [P, NT, D])
        p_hT = sb("p_hT_sb", [P, T])
        p_cT = sb("p_cT_sb", [L, T])
        p_qk = sb("p_qk", [P, 2, NT, L])
        p_t1 = sb("p_t1", [P, 2, NT, L])
        p_t2 = sb("p_t2", [P, 2, NT, L])
        part1 = sb("part1", [P, 2, NT * H, HD], BF16)
        part2 = sb("part2", [P, 2, NT * H, HD], BF16)
        part3 = sb("part3", [P, 2, NT * H, HD], BF16)
        q_rows = sb("q_rows", [P, 2, NT, H, SLOTS, HD], BF16)
        k_rows = sb("k_rows", [P, NT, H, SLOTS, HD], BF16)
        k_all = sb("k_all", [P, G, T], BF16)
        kz = sb("kz", [P, 2, G, R, T], BF16)
        qT1 = sb("qT1", [P, 2, G, T], BF16)
        v_pad = sb("v_pad", [P, 2, NT, H, HD + 1])
        nmax = sb("nmax", [P, NT, H])
        nm_r1 = sb("nm_r1", [P, NT, R])
        nm_r2 = sb("nm_r2", [P, NT, R])
        qT2 = sb("qT2", [P, 2, T], BF16)
        pT = sb("pT", [P, 2, EXPS, 2 * T])
        oT_g = sb("oT_g", [P, 2, T])
        inv = sb("inv", [P, 2, NT, R])
        o_tok = sb("o_tok", [P, NT, L])
        oT_sb = sb("oT_sb", [L, T])
        m_sq = sb("m_sq", [P, NT])
        m_ms = sb("m_ms", [P, NT])
        m_rs = sb("m_rs", [P, NT])
        m_t = sb("m_t", [P, NT, D])
        m_tT = sb("m_tT", [P, T])
        def carve(tensor, shapes):
            views, at = [], 0
            for shape in shapes:
                size, names = 1, " ".join(f"d{n}" for n in range(len(shape)))
                for n in shape:
                    size *= n
                view = tensor[:, at:at + size]
                views.append(view.rearrange(f"p ({names}) -> p {names}",
                                            **{f"d{n}": v for n, v in enumerate(shape)}))
                at += size
            return views

        w1_sb, w3_sb, w2_sb, tT = carve(kz[:, :, :, :, :].rearrange("p a g r t -> p (a g r t)").bitcast(F32),
                                        [[NE, F], [NE, F], [NE, FH, D], [2, T]])
        hid, silu, y, gate, hot, lg2, e_tmp, slot_sb, top = carve(
            pT[:, :, :, :].rearrange("p a s t -> p (a s t)"),
            [[2, FH, T], [FH, T], [NT, D], [NB, NT, NE], [2, NB * NT, NE], [NB * NT, NE], [NB * NT, NE],
             [NB * NT, NE], [NB * NT, 4]])
        tokens_T = nc.dram_tensor("tokens_T", (NB, P, T), F32).ap()

        small = ps("small", [P, 4, T])
        wide = ps("wide", [P, 2, 2 * T])
        y_banks = small[:, 2:4, :]

        small_full = [sem(f"small_full{i}") for i in range(4)]
        small_free = [sem(f"small_free{i}") for i in range(4)]
        wide_full = [sem(f"wide_full{i}") for i in range(2)]
        wide_free = [sem(f"wide_free{i}") for i in range(2)]
        y_full = [sem(f"y_full{i}") for i in range(2)]
        y_free = [sem(f"y_free{i}") for i in range(2)]
        consts_in = sem("consts_in")
        weights_in = sem("weights_in")
        fills = sem("fills")
        x_first = sem("x_first")
        x_rest = sem("x_rest")
        names = ["a_stats", "a_var", "a_vareps", "a_rstd", "a_xn", "a_rope1", "a_rope", "a_nmax", "a_nbias",
                 "a_exp", "a_inv", "a_r", "a_rstats", "a_rvar", "a_rvareps", "a_rrstd", "a_rn", "x1_ready",
                 "p_stats", "p_var", "p_vareps", "p_rstd", "p_h0", "p_kept", "p_w1", "p_w2", "p_ms", "p_rs",
                 "p_rope1", "p_rope", "p_part1", "p_rest1", "p_part2", "p_rest2", "p_part3", "p_rows",
                 "sq_done", "m_ms", "m_rs", "m_t", "res_ready", "up_done"]
        S = {n: sem("s_" + n) for n in names}
        kz_in = sem("kz_in")
        tT_kept = sem("tT_kept")
        tT_in = [sem("tT_in0"), sem("tT_in1")]
        cut = sem("cut")
        inv_done = sem("inv_done")
        filled = sem("filled")
        silu_done = [sem("silu_done0"), sem("silu_done1")]
        top_diff = sem("top_diff")
        top_exp = sem("top_exp")
        final_stats = sem("final_stats")
        final_mean = sem("final_mean")
        final_var = sem("final_var")
        final_norm = sem("final_norm")
        final_out = sem("final_out")
        final_step = sem("final_step")
        final_pow = sem("final_pow")
        out_done = sem("out_done")

        block = ctx.enter_context(nc.Block())

        FIRST = ("a", "ap", "apm", "apmf")
        LOOP = "apmf"
        LAST = ("pmf", "mf", "f")
        LOOPED = (len(FIRST), NB)

        def jobs_before(i):
            before = [j for k in range(i) for j in jobs((*FIRST, *[LOOP] * (NB - len(FIRST)), *LAST)[k])]
            maxima = sum(map(is_max, before))
            return [(n // 2, n % 2) for n in (maxima, len(before) - maxima)]

        def iterations(eng, body):
            def one(stages, i, parity, before):
                batch = {s: Batch(i - n, (parity - n) % 2) if s in stages else None for n, s in enumerate("apmf")}
                body(stages, batch["a"], batch["p"], batch["m"], batch["f"],
                     Rings(small_full, small_free, jobs(stages), before))

            for i, stages in enumerate(FIRST):
                one(stages, i, i % 2, jobs_before(i))
            first = LOOPED[0]
            with eng.Fori(LOOPED[0] // 2, LOOPED[1] // 2) as j:
                for par in range(2):
                    i = eng.snap(2 * j + par)
                    before = []
                    for (turns, odd), (turns_next, _) in zip(jobs_before(first), jobs_before(first + 1)):
                        step = turns_next - turns
                        before.append((eng.snap(i * step + (turns - first * step)), odd))
                    one(LOOP, i, par, before)
            for i, stages in enumerate(LAST, LOOPED[1]):
                one(stages, i, i % 2, jobs_before(i))

        last_ring = Rings(small_full, small_free, jobs(LAST[-1]), jobs_before(NB + 2))

        def wide_turns(m, w):
            return m.n * (G * EXPS // 2) + (w // 2 + CREDIT)

        def held(eng, sem_, value):
            value = value if isinstance(value, int) else eng.compute_val(value)
            eng.wait_ge(fills, 1)
            wait(eng, sem_, value)

        @block.sync
        def _(sp):
            def load_x(n, loaded):
                sp.dma_start(x1[:, n, :, :], x[n].rearrange("(t p) d -> p t d", p=P)).then_inc(loaded, 16)

            load_x(0, x_first)
            for dst, src in ((idf[:, :], ident_f), (future_in[:, :], future), (future_t_in[:, :], future_t),
                             (wqkv_a[:, 0:D], wq_a[0]), (wqkv_a[:, D:2 * D], wk_a[0]),
                             (wqkv_a[:, 2 * D:3 * D], wv_a[0]),
                             (cos_a_sb[:, :, :], cos_a), (sin_a_sb[:, :, :], sin_a), (wo_sb[:, :], wo_a[0]),
                             (wdown_sb[:, :], w_down), (wqkv_b[:, 0:L], wq_b), (wqkv_b[:, L:2 * L], wk_b),
                             (wqkv_b[:, 2 * L:3 * L], wv_b), (wup_sb[:, :], w_up), (router_sb[:, :], router_w),
                             (g1_sb[:, :], g1.rearrange("(d o) -> d o", o=1)),
                             (g2_sb[:, :], g2.rearrange("(d o) -> d o", o=1)),
                             (cos_b_sb[:, :, :, :], cos_b), (sin_b_sb[:, :, :, :], sin_b),
                             ):
                sp.dma_start(dst, src).then_inc(consts_in, 16)
            for n in range(1, NB):
                load_x(n, x_rest)
            def body(stages, a, p, m, f, ring):
                for step in steps(stages):
                    if step == "p_rows":
                        c = sp.compute_val(ring.count("p_k1"))
                        sp.wait_ge(fills, 1)
                        sp.wait_ge(small_free[ring.bank("p_k1")], c)
                        for r in range(R):
                            sp.dma_start(kz[32 * r:32 * r + 32, p.parity, :, r, :],
                                         k_all[32 * r:32 * r + 32, :, :]).then_inc(kz_in, 16)
                    if step == "f_tT":
                        c = sp.compute_val(ring.count("tT"))
                        sp.wait_ge(fills, 1)
                        sp.wait_ge(small_free[ring.bank("tT")], c)
                        sp.dma_start(tokens_T[f.n], m_tT[:, :]).then_inc(tT_kept, 16)

            sp.wait_ge(fills, N_FILLS)
            iterations(sp, body)
            sp.wait_ge(small_free[last_ring.bank("pv3")], last_ring.count("pv3"))
            sp.dma_start(slot_sb[:, :, :], slot_index).then_inc(weights_in, 16)
            sp.dma_start(w1_sb[:, :, :], w1.rearrange("e d f -> d e f")).then_inc(weights_in, 16)
            sp.dma_start(w3_sb[:, :, :], w3.rearrange("e d f -> d e f")).then_inc(weights_in, 16)
            for e in range(NE):
                sp.dma_start(w2_sb[:, e, :, :], w2[e].rearrange("(h p) d -> p h d", p=P)).then_inc(weights_in, 16)
            sp.wait_ge(tT_kept, 16 * (CREDIT + NB))
            for b in range(NB):
                if b >= 2:
                    sp.wait_ge(wide_full[1], CREDIT + NB * G * EXPS // 2 + (b - 1) * NE)
                sp.dma_start(tT[:, b % 2, :], tokens_T[b]).then_inc(tT_in[b % 2], 16)
            with sp.Fori(0, NB) as b:
                sp.wait_ge(final_out, b + 1)
                sp.dma_start(out[b].rearrange("(t p) d -> p t d", p=P), x1[:, b, :, :]).then_inc(out_done, 16)
            sp.wait_ge(out_done, 16 * NB)

        @block.tensor
        def _(pe):
            def take(ring, job, after=(), alone=False):
                need = {ring.bank(job): ring.turns(job)}
                for j in after:
                    need[ring.bank(j)] = max(need.get(ring.bank(j), 0), ring.turns(j) + 1)
                for bank, turns in need.items():
                    (held if alone else wait)(pe, small_free[bank], ring.turns_before(bank) + turns)
                return small[:, ring.bank(job), :]

            def full(ring, job, last):
                last.then_inc(small_full[ring.bank(job)], 1)

            def max_job(m, ring, g, n):
                job = f"max{g}_{n}"
                tile, r0, heads = MAX_JOBS[n]
                keys = (tile + 1) * P
                if (g, n) == (0, 0):
                    pe.wait_ge(kz_in, 16 * R * m.now)
                bank = take(ring, job, ["p_q0", "p_q1"] if (g, n) == (0, 0) else ())
                for r in range(r0, r0 + heads):
                    at = (r - r0) * keys
                    pe.matmul(bank[:, at:at + keys], qT1[:, m.parity, g, tile * P:(tile + 1) * P],
                              kz[:, m.parity, g, r, 0:keys], start=(r == r0), stop=False, skip_group_check=True)
                diagonal = bank[:, 0:heads * keys].rearrange("p (h k) -> p h k", h=heads)[:, :, keys - P:keys]
                last = pe.matmul(diagonal, idb[:, :], future_sb[:, 0:heads, :], start=False, stop=True,
                                 skip_group_check=True)
                full(ring, job, last)

            def exp_job(m, g, s):
                w = g * EXPS + s
                wait(pe, wide_free[w % 2], wide_turns(m, w))
                bank = wide[:, w % 2, :]
                if s < R:
                    blocks = [(s, tile, at) for tile, at in PT_AT.items()]
                    diagonals = [bank[:, 0:P], bank[:, T:2 * T].rearrange("p (n k) -> p n k", k=P)[:, 0:NT:3, :]]
                else:
                    blocks = [(r, 2, r * 2 * P) for r in range(R)]
                    diagonals = [bank[:, n * T:(n + 1) * T].rearrange("p (n k) -> p n k", k=P)[:, 0:NT:2, :]
                                 for n in range(2)]
                for r, tile, at in blocks:
                    pe.matmul(bank[:, at:at + T - tile * P], kz[:, m.parity, g, r, tile * P:(tile + 1) * P],
                              qT2[:, g % 2, tile * P:T], start=(at % T == 0), stop=False, skip_group_check=True)
                for diagonal in diagonals:
                    n = 1 if len(diagonal.shape) == 2 else 2
                    last = pe.matmul(diagonal, idb[:, :], future_T[:, 0:n, :] if n > 1 else future_T[:, 0, :],
                                     start=False, stop=True, skip_group_check=True)
                last.then_inc(wide_full[w % 2], 1)

            def transposes(ring, job, source, rows, ident, after=(), alone=False):
                bank = take(ring, job, after, alone)
                for t in range(NT):
                    last = pe.transpose(bank[0:rows, t * P:(t + 1) * P], source(t), ident)
                full(ring, job, last)

            def product_v(m, ring, g):
                for w in (g * EXPS + EXPS - 2, g * EXPS + EXPS - 1):
                    pe.wait_ge(wide_free[w % 2], wide_turns(m, w) + 1)
                bank = take(ring, f"pv{g}")
                for k in range(NT):
                    for r in range(R):
                        if k == 2:
                            probs = pT[:, g % 2, R, r * 2 * P:(r + 1) * 2 * P]
                        else:
                            probs = pT[:, g % 2, r, PT_AT[k]:PT_AT[k] + T - k * P]
                        last = pe.matmul(bank[32 * r:32 * r + HD + 1, k * P:T],
                                         v_pad[:, m.parity, k, g * R + r, :], probs,
                                         start=(k == 0), stop=(k == NT - 1), skip_group_check=True)
                full(ring, f"pv{g}", last)

            def turn_o(m, ring, g):
                transposes(ring, f"o{g}", lambda t: oT_g[:, g % 2, t * P:(t + 1) * P], P, idf[:, :],
                           [f"pv{g}"] if g != 1 else ())

            def body(stages, a, p, m, f, ring):
                for step in steps(stages):
                    if step == "a_xT":
                        pe.wait_ge(S["a_xn"], a.now)
                        transposes(ring, "a_xT", lambda t: a_xn[:, t, :], P, idf[:, :])
                    elif step.startswith("a_qkv"):
                        t = int(step[-1])
                        bank = take(ring, step, ["a_xT"] if t == 0 else ())
                        full(ring, step, pe.matmul(bank[:, 0:3 * D], a_xT[:, t * P:(t + 1) * P],
                                                   wqkv_a[:, :], start=True, stop=True))
                    elif step == "a_qkT":
                        pe.wait_ge(S["a_rope"], a.now)
                        transposes(ring, "a_qT", lambda t: a_m1[:, t, 0, :], P, idf[:, :])
                        transposes(ring, "a_kT", lambda t: a_m1[:, t, 1, :], P, idf[:, :])
                    elif step[:3] == "a_s" and step in JOBS:
                        t = int(step[-1])
                        keys = (t + 1) * P
                        bank = take(ring, step, ["a_qT", "a_kT"] if t == 0 else ())
                        pe.matmul(bank[:, 0:keys], a_qT[:, t * P:keys], a_kT[:, 0:keys],
                                  start=True, stop=False, skip_group_check=True)
                        full(ring, step, pe.matmul(bank[:, t * P:keys], idb[:, :], future_sb[:, 0, :],
                                                   start=False, stop=True, skip_group_check=True))
                    elif step == "a_pT":
                        for job, blocks in (("a_p0", [(0, 0), (1, 0), (2, 0), (3, 0)]),
                                            ("a_p1", [(1, 1), (2, 1), (3, 1), (3, 3)]),
                                            ("a_p2", [(2, 2), (3, 2)])):
                            bank = take(ring, job, ["a_s2", "a_s3"] if job == "a_p0" else ())
                            for n, (i, k) in enumerate(blocks):
                                last = pe.transpose(bank[:, n * P:(n + 1) * P], a_p[:, i, k * P:(k + 1) * P], idf[:, :])
                            full(ring, job, last)
                    elif step == "a_oT":
                        bank = take(ring, "a_oT", ["a_p0", "a_p1", "a_p2"])
                        for k, (n, at) in enumerate(((0, 0), (1, 0), (2, 0), (1, 3 * P))):
                            last = pe.matmul(bank[:, k * P:T], a_qkv[:, k, 2 * D:3 * D],
                                             a_pT[:, n, at:at + T - k * P], start=(k == 0), stop=(k == NT - 1),
                                             skip_group_check=True)
                        full(ring, "a_oT", last)
                    elif step == "a_r":
                        bank = take(ring, "a_r", ["a_oT"])
                        for t in range(NT):
                            last = pe.matmul(bank[:, t * P:(t + 1) * P], a_xT[:, t * P:(t + 1) * P], wo_sb[:, :],
                                             start=True, stop=True)
                        full(ring, "a_r", last)
                    elif step == "p_hT":
                        pe.wait_ge(S["p_h0"], p.now)
                        transposes(ring, "p_hT", lambda t: h0[:, t, :], P, idf[:, :])
                    elif step == "p_cT":
                        bank = take(ring, "p_cT", ["p_hT"])
                        full(ring, "p_cT", pe.matmul(bank[0:L, :], wdown_sb[:, :], p_hT[:, :], start=True, stop=True))
                    elif step == "p_qkv":
                        for n in range(2):
                            bank = take(ring, f"p_qkv{n}", ["p_cT"] if n == 0 else ())
                            for t in (2 * n, 2 * n + 1):
                                at = (t % 2) * 3 * L
                                last = pe.matmul(bank[:, at:at + 3 * L], p_cT[:, t * P:(t + 1) * P], wqkv_b[:, :],
                                                 start=True, stop=True)
                            full(ring, f"p_qkv{n}", last)
                    elif step == "p_rows":
                        pe.wait_ge(S["p_rows"], p.now)
                        for kind, rows in (("k", lambda t, g: k_rows[:, t, g * R:(g + 1) * R, :, :]),
                                           ("q", lambda t, g: q_rows[:, p.parity, t, g * R:(g + 1) * R, :, :])):
                            for n in range(2):
                                bank = take(ring, f"p_{kind}{n}").bitcast(BF16)
                                for g in (2 * n, 2 * n + 1):
                                    for t in range(NT):
                                        at = (g % 2) * T + t * P
                                        last = pe.transpose(bank[:, at:at + P],
                                                            rows(t, g).rearrange("p h s d -> p (h s d)"), idb[:, :])
                                full(ring, f"p_{kind}{n}", last)
                    elif step == "p_max0":
                        for n in range(len(MAX_JOBS)):
                            max_job(p, ring, 0, n)
                    elif step.startswith("m_shift"):
                        g = int(step[-1])
                        pe.wait_ge(cut, 5 * (G * m.n + g + 1))
                        bank = take(ring, step[2:]).bitcast(BF16)
                        for t in range(NT):
                            rows = q_rows[:, m.parity, t, g * R:(g + 1) * R, :, :].rearrange("p h s d -> p (h s d)")
                            last = pe.transpose(bank[:, t * P:(t + 1) * P], rows, idb[:, :])
                        full(ring, step[2:], last)
                    elif step.startswith("m_mix"):
                        g, s = int(step[-2]), int(step[-1])
                        if s == 0:
                            pe.wait_ge(small_free[ring.bank(f"shift{g}")], ring.count(f"shift{g}"))
                        exp_job(m, g, s)
                        if g + 1 < G or p:
                            for n in mix_max(s):
                                max_job(m if g + 1 < G else p, ring, (g + 1) % G, n)
                    elif step[2:4] == "pv":
                        g = int(step[-1])
                        product_v(m if g < 2 else f, ring, g)
                        if g:
                            turn_o(m if g < 2 else f, ring, g - 1)
                    elif step == "f_o":
                        turn_o(f, ring, G - 1)
                    elif step == "f_oT":
                        transposes(ring, "oT", lambda t: o_tok[:, t, :], L, idf[:, :], [f"o{G - 1}"], alone=True)
                    elif step == "f_up":
                        bank = take(ring, "up", ["oT"])
                        for t in range(NT):
                            last = pe.matmul(bank[:, t * P:(t + 1) * P], oT_sb[:, t * P:(t + 1) * P], wup_sb[:, :],
                                             start=True, stop=True)
                        full(ring, "up", last)
                    elif step == "f_tT":
                        pe.wait_ge(S["m_t"], f.now)
                        transposes(ring, "tT", lambda t: m_t[:, t, :], P, idf[:, :])
                    elif step == "f_logits":
                        bank = take(ring, "logits", ["tT"])
                        for t in range(NT):
                            last = pe.matmul(bank[:, t * NE:(t + 1) * NE], m_tT[:, t * P:(t + 1) * P], router_sb[:, :],
                                             start=True, stop=True)
                        full(ring, "logits", last)

            pe.wait_ge(consts_in, 16 * N_CONSTS)
            pe.wait_ge(fills, N_FILLS)
            iterations(pe, body)

            pe.wait_ge(weights_in, 16 * N_WEIGHTS)
            pe.wait_ge(small_free[last_ring.bank("tT")], last_ring.count("tT"))
            pe.wait_ge(small_free[last_ring.bank("logits")], last_ring.count("logits"))
            with pe.Fori(0, NB // 2) as pair:
              for par in range(2):
                b = pe.snap(2 * pair + par)
                pe.wait_ge(tT_in[par], 16 * pair + 16)
                hid_jobs = pe.snap(b * NE + CREDIT + NB * G * EXPS // 2)
                y_jobs = pe.snap(b * (NE // 2) + CREDIT)

                def hidden(e):
                    for f in range(FH):
                        pe.wait_ge(wide_free[f], hid_jobs + e)
                        tokens = tT[:, par, :]
                        pe.matmul(wide[:, f, 0:T], w1_sb[:, e, f * P:(f + 1) * P], tokens, start=True, stop=True)
                        pe.matmul(wide[:, f, T:2 * T], w3_sb[:, e, f * P:(f + 1) * P], tokens,
                                  start=True, stop=True).then_inc(wide_full[f], 1)

                def down(e):
                    for f in range(FH):
                        pe.wait_ge(wide_free[f], hid_jobs + e + 1)
                    pe.wait_ge(y_free[e % 2], y_jobs + e // 2)
                    for t in range(NT):
                        for f in range(FH):
                            last = pe.matmul(y_banks[:, e % 2, t * P:(t + 1) * P], hid[:, e % 2, f, t * P:(t + 1) * P],
                                             w2_sb[:, e, f, :], start=(f == 0), stop=(f == FH - 1))
                    last.then_inc(y_full[e % 2], 1)

                for e in range(NE):
                    hidden(e)
                    if e:
                        down(e - 1)
                down(NE - 1)

        @block.scalar
        def _(act):
            def evacuate(ring, job, out_, in_=None, scale=1.0):
                b = small[:, ring.bank(job), :]
                act.wait_ge(small_full[ring.bank(job)], ring.count(job))
                act.activation(out_, b if in_ is None else in_(b), ACT.Copy, scale=scale)\
                   .then_inc(small_free[ring.bank(job)], 1)

            def body(stages, a, p, m, f, ring):
                for step in steps(stages):
                    if step == "a_xT":
                        evacuate(ring, "a_xT", a_xT[:, :])
                    elif step.startswith("a_qkv"):
                        evacuate(ring, step, a_qkv[:, int(step[-1]), :], lambda b: b[:, 0:3 * D])
                    elif step == "a_qkT":
                        evacuate(ring, "a_qT", a_qT[:, :])
                    elif step[:3] == "a_s" and step in JOBS:
                        t = int(step[-1])
                        keys = (t + 1) * P
                        act.wait_ge(S["a_nbias"], NT * a.n + t + 1)
                        act.activation(a_p[:, t, 0:keys], small[:, ring.bank(step), 0:keys], ACT.Exp,
                                       bias=a_nb[:, t:t + 1], scale=SCALE_A, accum_out=a_sum[:, t:t + 1])\
                           .then_inc(small_free[ring.bank(step)], 1)
                    elif step == "a_pT":
                        evacuate(ring, "a_p0", a_pT[:, 0, :])
                        evacuate(ring, "a_p2", a_pT[:, 2, 0:2 * P], lambda b: b[:, 0:2 * P])
                    elif step == "a_oT":
                        evacuate(ring, "a_oT", a_xT[:, :])
                    elif step == "p_hT":
                        evacuate(ring, "p_hT", p_hT[:, :], scale=g1_sb[:, 0:1])
                    elif step == "p_cT":
                        evacuate(ring, "p_cT", p_cT[:, :], lambda b: b[0:L, :])
                    elif step == "p_qkv":
                        act.wait_ge(S["p_rs"], p.now)
                        for n in range(2):
                            job = f"p_qkv{n}"
                            act.wait_ge(small_full[ring.bank(job)], ring.count(job))
                            for t in (2 * n, 2 * n + 1):
                                bank = small[:, ring.bank(job), (t % 2) * 3 * L:(t % 2 + 1) * 3 * L]
                                act.activation(p_qk[:, :, t, :], bank[:, 0:2 * L].rearrange("p (a l) -> p a l", a=2),
                                               ACT.Copy, scale=p_rs[:, t:t + 1])
                                last = act.activation(v_pad[:, p.parity, t, :, 0:HD],
                                                      bank[:, 2 * L:3 * L].rearrange("p (h d) -> p h d", h=H),
                                                      ACT.Copy, scale=p_rs[:, t:t + 1])
                            last.then_inc(small_free[ring.bank(job)], 1)
                    elif step == "p_rows":
                        for n in range(2):
                            evacuate(ring, f"p_q{n}", qT1[:, p.parity, 2 * n:2 * n + 2, :].rearrange("p g t -> p (g t)"),
                                     lambda b: b.bitcast(BF16))
                    elif step.startswith("m_mix"):
                        g, s = int(step[-2]), int(step[-1])
                        w = g * EXPS + s
                        act.wait_ge(wide_full[w % 2], wide_turns(m, w) + 1)
                        act.activation(pT[:, g % 2, s, :], wide[:, w % 2, :], ACT.Exp, scale=SCALE_B)\
                           .then_inc(wide_free[w % 2], 1)
                    elif step[2:4] == "pv":
                        g = int(step[-1])
                        evacuate(ring, f"pv{g}", oT_g[:, g % 2, :])
                    elif step == "f_oT":
                        evacuate(ring, "oT", oT_sb[:, :], lambda b: b[0:L, :])
                    elif step == "f_up":
                        act.wait_ge(small_free[ring.bank("up")], ring.count("up"))
                        for t in range(NT):
                            last = act.activation(m_t[:, t, :], res[:, f.n, t, :], ACT.Square,
                                                  accum_out=m_sq[:, t:t + 1])
                        last.then_inc(S["sq_done"], 1)
                    elif step == "f_tT":
                        act.wait_ge(tT_kept, 16 * (CREDIT + f.n))
                        evacuate(ring, "tT", m_tT[:, :], scale=g2_sb[:, 0:1])

            act.wait_ge(consts_in, 16 * N_CONSTS)
            act.wait_ge(fills, N_FILLS)
            iterations(act, body)
            act.wait_ge(top_diff, 1)
            act.activation(top[:, :, 3], top[:, :, 2], ACT.Exp).then_inc(top_exp, 1)
            with act.Fori(0, NB) as b:
                hid_jobs = act.snap(b * NE + CREDIT + NB * G * EXPS // 2)
                for e in range(NE):
                    for f in range(FH):
                        act.wait_ge(wide_full[f], hid_jobs + e + 1)
                        act.wait_ge(wide_free[f], hid_jobs + e)
                        act.activation(silu[:, f, :], wide[:, f, 0:T], ACT.Silu).then_inc(silu_done[f], 1)

        @block.gpsimd
        def _(pool):
            def rsqrt(out_, in_, need, value, done):
                pool.wait_ge(need, value)
                pool.tensor_tensor(out_, in_, neg_half[:, :], ALU.pow).then_inc(done, 1)

            def body(stages, a, p, m, f, ring):
                for step in steps(stages):
                    if step == "a_stats":
                        rsqrt(a_rstd[:, :], a_ve[:, :], S["a_vareps"], a.now, S["a_rstd"])
                    elif step == "p_stats":
                        rsqrt(p_rstd[:, :], p_ve[:, :], S["p_vareps"], p.now, S["p_rstd"])
                    elif step == "p_norm":
                        rsqrt(p_rs[:, :], p_ms[:, :], S["p_ms"], p.now, S["p_rs"])
                    elif step == "a_qkv3":
                        for j in ("a_qkv2", "a_qkv3"):
                            pool.wait_ge(small_free[ring.bank(j)], ring.count(j))
                        qk = a_qkv[:, :, 0:2 * D].rearrange("p t (a d) -> p t a d", a=2)
                        for n in range(2):
                            pool.tensor_tensor(a_m1[:, :, n, :], qk[:, :, n, :], cos_a_sb[:, :, :],
                                               ALU.mult).then_inc(S["a_rope1"], 1)
                            for half in range(2):
                                lo, other = half * D // 2, (1 - half) * D // 2
                                pool.tensor_tensor(a_m2[:, :, n, lo:lo + D // 2], qk[:, :, n, other:other + D // 2],
                                                   sin_a_sb[:, :, lo:lo + D // 2], ALU.mult).then_inc(S["a_rope1"], 1)
                        pool.wait_ge(S["a_rope1"], 6 * a.now)
                        pool.tensor_tensor(a_m1[:, :, :, :], a_m1[:, :, :, :], a_m2[:, :, :, :],
                                           ALU.add).then_inc(S["a_rope"], 1)
                    elif step == "a_rstats":
                        rsqrt(a_rstd[:, :], a_ve[:, :], S["a_rvareps"], a.now, S["a_rrstd"])
                    elif step == "a_rnorm":
                        pool.wait_ge(S["a_rn"], a.now)
                        pool.tensor_tensor(x1[:, a.n, :, :], x1[:, a.n, :, :], a_xn[:, :, :],
                                           ALU.add).then_inc(S["x1_ready"], 1)
                    elif step == "p_qkv":
                        for j in ("p_qkv0", "p_qkv1"):
                            pool.wait_ge(small_free[ring.bank(j)], ring.count(j))
                        flat = lambda b: b[:, :, :, :].rearrange("p a t l -> p (a t l)")
                        qk, t1, t2, cos, sin = (flat(b) for b in (p_qk, p_t1, p_t2, cos_b_sb, sin_b_sb))
                        pair = lambda b, n: b.rearrange("p (n two) -> p n two", two=2)[:, :, n]
                        pool.tensor_tensor(t1, qk, cos, ALU.mult).then_inc(S["p_rope1"], 1)
                        for n in range(2):
                            pool.tensor_tensor(pair(t2, n), pair(qk, 1 - n), pair(sin, n),
                                               ALU.mult).then_inc(S["p_rope1"], 1)
                        pool.wait_ge(S["p_rope1"], 3 * p.now)
                        pool.tensor_tensor(t1, t1, t2, ALU.add).then_inc(S["p_rope"], 1)
                        parts = [b[:, :, :, :].rearrange("p a n d -> p (a n d)") for b in (part1, part2, part3)]
                        held(pool, S["p_rope"], p.now)
                        pool.tensor_copy(parts[0], t1).then_inc(S["p_part1"], 1)
                        pool.wait_ge(S["p_part1"], p.now)
                        pool.tensor_tensor(t2, t1, parts[0], ALU.subtract).then_inc(S["p_rest1"], 1)
                        held(pool, S["p_rest1"], p.now)
                        pool.tensor_copy(parts[1], t2).then_inc(S["p_part2"], 1)
                        pool.wait_ge(S["p_part2"], p.now)
                        pool.tensor_tensor(t1, t2, parts[1], ALU.subtract).then_inc(S["p_rest2"], 1)
                        held(pool, S["p_rest2"], p.now)
                        pool.tensor_copy(parts[2], t1).then_inc(S["p_part3"], 1)
                        held(pool, S["p_part3"], p.now)
                        q = q_rows[:, p.parity, :, :, :, :].rearrange("p t h s d -> p (t h) s d")
                        k = k_rows[:, :, :, :, :].rearrange("p t h s d -> p (t h) s d")
                        for b, n, lo, hi, step_ in ((part1, 3, 0, 3, 1), (part2, 2, 3, 5, 1), (part3, 1, 5, 6, 1)):
                            src = b[:, 0, :, :].unsqueeze(2).to_broadcast([P, NT * H, n, HD])
                            pool.tensor_copy(q[:, :, lo:hi, :], src)
                        pool.memset(q[:, :, 6, 0:3], 0.0)
                        for b, slots in ((part1, (0, 3, 5)), (part2, (1, 4)), (part3, (2,))):
                            for s in slots:
                                last = pool.tensor_copy(k[:, :, s, :], b[:, 1, :, :])
                        last.then_inc(S["p_rows"], 1)
                    elif step == "f_up":
                        rsqrt(m_rs[:, :], m_ms[:, :], S["m_ms"], f.now, S["m_rs"])
                        pool.wait_ge(S["m_rs"], f.now)
                        pool.tensor_tensor(m_t[:, :, :], res[:, f.n, :, :],
                                           m_rs[:, :].unsqueeze(2).to_broadcast([P, NT, D]),
                                           ALU.mult).then_inc(S["m_t"], 1)

            for s in (*wide_full, *wide_free, *y_full, *y_free):
                pool.sem_inc(s, CREDIT)
            pool.sem_inc(tT_kept, 16 * CREDIT)
            pool.memset(neg_half[:, :], -0.5).then_inc(fills, 1)
            pool.memset(kz[:, :, :, :, :].rearrange("p a g r t -> p (a g r t)").bitcast(F32), 0.0).then_inc(fills, 1)
            pool.wait_ge(fills, N_FILLS)
            pool.wait_ge(consts_in, 16 * N_CONSTS)
            iterations(pool, body)
            with pool.Fori(0, NB) as b:
                pool.wait_ge(final_var, b + 1)
                pool.tensor_tensor(a_rstd[:, :], a_ve[:, :], neg_half[:, :], ALU.pow).then_inc(final_pow, 1)
                pool.wait_ge(final_norm, b + 1)
                pool.tensor_tensor(x1[:, b, :, :], x1[:, b, :, :], a_xn[:, :, :], ALU.add).then_inc(final_out, 1)

        @block.vector
        def _(dve):
            def empty(ring, job, ins):
                ins.then_inc(small_free[ring.bank(job)], 1)

            def await_job(ring, job):
                dve.wait_ge(small_full[ring.bank(job)], ring.count(job))
                return small[:, ring.bank(job), :]

            def norm_stats(src, st, mv, ve, now, stats, var, vareps):
                for t in range(NT):
                    last = dve.bn_stats(st[:, t, :], src(t))
                last.then_inc(stats, 1)
                held(dve, stats, now)
                for t in range(NT):
                    last = dve.bn_aggr(mv[:, t, :], st[:, t, :])
                last.then_inc(var, 1)
                dve.wait_ge(var, now)
                dve.tensor_scalar(ve[:, :], mv[:, :, 1], EPS, None, ALU.add).then_inc(vareps, 1)

            def normalise(dst, src, mv, rstd, done):
                for t in range(NT):
                    last = dve.tensor_scalar(dst(t), src(t), mv[:, t, 0:1], rstd[:, t:t + 1],
                                             ALU.subtract, ALU.mult)
                last.then_inc(done, 1)

            def max_job(m, ring, g, n):
                job = f"max{g}_{n}"
                tile, r0, heads = MAX_JOBS[n]
                bank = await_job(ring, job)
                ins = dve.tensor_reduce(nmax[:, tile, g * R + r0:g * R + r0 + heads],
                                        bank[:, 0:heads * (tile + 1) * P].rearrange("p (h k) -> p h k", h=heads),
                                        AX, ALU.max, negate=True)
                empty(ring, job, ins)
                if (g, n) == (0, len(MAX_JOBS) - 1):
                    dve.wait_ge(small_free[ring.bank(job)], ring.count(job))

            def body(stages, a, p, m, f, ring):
                for step in steps(stages):
                    if step == "a_stats":
                        if isinstance(a.n, int) and a.n == 0:
                            dve.wait_ge(x_first, 16)
                        else:
                            dve.wait_ge(x_rest, 16 * (NB - 1))
                        norm_stats(lambda t: x1[:, a.n, t, :], a_st, a_mv, a_ve, a.now,
                                   S["a_stats"], S["a_var"], S["a_vareps"])
                    elif step == "a_norm":
                        dve.wait_ge(S["a_rstd"], a.now)
                        normalise(lambda t: a_xn[:, t, :], lambda t: x1[:, a.n, t, :], a_mv, a_rstd, S["a_xn"])
                    elif step == "p_hT":
                        dve.wait_ge(S["p_h0"], p.now)
                        dve.tensor_copy(res[:, p.n, :, :], h0[:, :, :]).then_inc(S["p_kept"], 1)
                    elif step == "a_qkT":
                        empty(ring, "a_kT", dve.tensor_copy(a_kT[:, :], await_job(ring, "a_kT")))
                    elif step[:3] == "a_s" and step in JOBS:
                        t = int(step[-1])
                        bank = await_job(ring, step)
                        dve.tensor_reduce(a_nm[:, t:t + 1], bank[:, 0:(t + 1) * P], AX, ALU.max, negate=True)\
                           .then_inc(S["a_nmax"], 1)
                        dve.wait_ge(S["a_nmax"], NT * a.n + t + 1)
                        dve.tensor_scalar(a_nb[:, t:t + 1], a_nm[:, t:t + 1], SCALE_A, None, ALU.mult)\
                           .then_inc(S["a_nbias"], 1)
                    elif step == "a_pT":
                        empty(ring, "a_p1", dve.tensor_copy(a_pT[:, 1, :], await_job(ring, "a_p1")))
                    elif step == "a_r":
                        dve.wait_ge(small_free[ring.bank("a_s3")], ring.count("a_s3"))
                        dve.reciprocal(a_ri[:, :], a_sum[:, :]).then_inc(S["a_inv"], 1)
                        bank = await_job(ring, "a_r")
                        dve.wait_ge(S["a_inv"], a.now)
                        ins = dve.tensor_tensor(a_xn[:, :, :], bank.rearrange("p (t d) -> p t d", t=NT),
                                                a_ri[:, :].unsqueeze(2).to_broadcast([P, NT, D]), ALU.mult)
                        empty(ring, "a_r", ins)
                    elif step == "a_rstats":
                        held(dve, small_free[ring.bank("a_r")], ring.count("a_r"))
                        norm_stats(lambda t: a_xn[:, t, :], a_st, a_mv, a_ve, a.now,
                                   S["a_rstats"], S["a_rvar"], S["a_rvareps"])
                    elif step == "a_rnorm":
                        dve.wait_ge(S["a_rrstd"], a.now)
                        normalise(lambda t: a_xn[:, t, :], lambda t: a_xn[:, t, :], a_mv, a_rstd, S["a_rn"])
                    elif step == "p_stats":
                        held(dve, S["x1_ready"], p.now)
                        norm_stats(lambda t: x1[:, p.n, t, :], p_st, p_mv, p_ve, p.now,
                                   S["p_stats"], S["p_var"], S["p_vareps"])
                    elif step == "p_norm":
                        dve.wait_ge(S["p_rstd"], p.now)
                        normalise(lambda t: h0[:, t, :], lambda t: x1[:, p.n, t, :], p_mv, p_rstd, S["p_h0"])
                        dve.tensor_tensor(p_m1[:, :], p_mv[:, :, 1], p_rstd[:, :], ALU.mult).then_inc(S["p_w1"], 1)
                        dve.wait_ge(S["p_w1"], p.now)
                        dve.tensor_tensor(p_m2[:, :], p_m1[:, :], p_rstd[:, :], ALU.mult).then_inc(S["p_w2"], 1)
                        dve.wait_ge(S["p_w2"], p.now)
                        dve.tensor_scalar(p_ms[:, :], p_m2[:, :], EPS, None, ALU.add).then_inc(S["p_ms"], 1)
                    elif step == "p_rows":
                        wait(dve, kz_in, 16 * R * p.n)
                        for n in range(2):
                            bank = await_job(ring, f"p_k{n}").bitcast(BF16)
                            empty(ring, f"p_k{n}", dve.tensor_copy(
                                k_all[:, 2 * n:2 * n + 2, :].rearrange("p g t -> p (g t)"), bank))
                    elif step == "p_max0":
                        for n in range(len(MAX_JOBS)):
                            max_job(p, ring, 0, n)
                    elif step.startswith("m_cut"):
                        g = int(step[-1])
                        heads = slice(g * R, (g + 1) * R)
                        slot = q_rows[:, m.parity, :, heads, 6, :]
                        mx = nmax[:, :, heads]
                        last_max = f"max{g}_{len(MAX_JOBS) - 1}"
                        if g:
                            dve.wait_ge(small_free[ring.bank(last_max)], ring.count(last_max))
                        n = 5 * (G * m.n + g)
                        dve.tensor_copy(slot[:, :, :, 0], mx).then_inc(cut, 1)
                        dve.wait_ge(cut, n + 1)
                        dve.tensor_tensor(nm_r1[:, :, :], mx, slot[:, :, :, 0], ALU.subtract).then_inc(cut, 1)
                        dve.wait_ge(cut, n + 2)
                        dve.tensor_copy(slot[:, :, :, 1], nm_r1[:, :, :]).then_inc(cut, 1)
                        dve.wait_ge(cut, n + 3)
                        dve.tensor_tensor(nm_r2[:, :, :], nm_r1[:, :, :], slot[:, :, :, 1], ALU.subtract).then_inc(cut, 1)
                        dve.wait_ge(cut, n + 4)
                        dve.tensor_copy(slot[:, :, :, 2], nm_r2[:, :, :]).then_inc(cut, 1)
                    elif step.startswith("m_shift"):
                        g = int(step[-1])
                        bank = await_job(ring, step[2:]).bitcast(BF16)
                        empty(ring, step[2:], dve.tensor_copy(qT2[:, g % 2, :], bank[:, 0:T]))
                    elif step.startswith("m_mix"):
                        g, s = int(step[-2]), int(step[-1])
                        if g + 1 < G or p:
                            for n in mix_max(s):
                                max_job(m if g + 1 < G else p, ring, (g + 1) % G, n)
                    elif step in ("m_pv1", "f_pv2", "f_pv3", "f_o"):
                        g = G - 1 if step == "f_o" else int(step[-1]) - 1
                        bank = await_job(ring, f"o{g}").rearrange("p (t r c) -> p t r c", t=NT, r=R)
                        dve.reciprocal(inv[:, g % 2, :, :], bank[:, :, :, HD]).then_inc(inv_done, 1)
                        dve.wait_ge(inv_done, G * (m if step[0] == "m" else f).n + g + 1)
                        o = o_tok[:, :, :].rearrange("p t (g r d) -> p t g r d", g=G, r=R)[:, :, g, :, :]
                        empty(ring, f"o{g}", dve.tensor_tensor(
                            o, bank[:, :, :, 0:HD], inv[:, g % 2, :, :].unsqueeze(3).to_broadcast([P, NT, R, HD]), ALU.mult))
                    elif step == "f_up":
                        dve.wait_ge(S["p_kept"], f.now)
                        bank = await_job(ring, "up")
                        dve.tensor_tensor(res[:, f.n, :, :], bank.rearrange("p (t d) -> p t d", t=NT),
                                          res[:, f.n, :, :], ALU.add).then_inc(small_free[ring.bank("up")], 1)
                        dve.wait_ge(S["sq_done"], f.now)
                        dve.tensor_scalar(m_ms[:, :], m_sq[:, :], 1.0 / D, EPS, ALU.mult, ALU.add)\
                           .then_inc(S["m_ms"], 1)
                    elif step == "f_logits":
                        bank = await_job(ring, "logits")
                        empty(ring, "logits", dve.tensor_copy(
                            logits[:, f.n, :, :], bank[:, 0:NT * NE].rearrange("p (t e) -> p t e", t=NT)))

            dve.memset(q_rows[:, :, :, :, :, :].rearrange("p a t h s d -> p (a t h s d)").bitcast(F32), 0.0)\
               .then_inc(fills, 1)
            dve.memset(k_rows[:, :, :, :, :].rearrange("p t h s d -> p (t h s d)").bitcast(F32), 0.0).then_inc(filled, 1)
            dve.memset(v_pad[:, :, :, :, :].rearrange("p a t h c -> p (a t h c)"), 0.0).then_inc(filled, 1)
            dve.wait_ge(filled, 2)
            dve.memset(k_rows[:, :, :, 6, 0:3].rearrange("p t h c -> p (t h) c"), 1.0).then_inc(fills, 1)
            dve.memset(v_pad[:, :, :, :, HD].rearrange("p a t h -> p (a t h)"), 1.0).then_inc(fills, 1)
            dve.wait_ge(consts_in, 16 * N_CONSTS)
            dve.tensor_copy(idb[:, :], idf[:, :])
            dve.tensor_copy(future_sb[:, :, :], future_in[:, :].unsqueeze(1).to_broadcast([P, R, P]))
            dve.tensor_copy(future_T[:, :, :], future_t_in[:, :].unsqueeze(1).to_broadcast([P, 2, P]))\
               .then_inc(fills, 1)
            dve.wait_ge(fills, N_FILLS)
            iterations(dve, body)

            dve.wait_ge(weights_in, 16 * N_WEIGHTS)
            lg = logits[:, :, :, :].rearrange("p b t e -> p (b t) e")
            wide_of = lambda c: top[:, :, c:c + 1].to_broadcast([P, NB * NT, NE])
            count = 0

            def then(ins):
                nonlocal count
                count += 1
                ins.then_inc(final_step, 1)
                dve.wait_ge(final_step, count)

            dve.wait_ge(small_free[last_ring.bank("logits")], last_ring.count("logits"))
            scores = lg
            for n in range(2):
                then(dve.tensor_reduce(top[:, :, n], scores, AX, ALU.max))
                then(dve.tensor_tensor(e_tmp[:, :, :], scores, wide_of(n), ALU.is_equal))
                then(dve.tensor_tensor(e_tmp[:, :, :], e_tmp[:, :, :], slot_sb[:, :, :], ALU.mult))
                then(dve.tensor_reduce(top[:, :, 2], e_tmp[:, :, :], AX, ALU.max))
                then(dve.tensor_tensor(hot[:, n, :, :], slot_sb[:, :, :], wide_of(2), ALU.is_equal))
                if n == 0:
                    then(dve.scalar_tensor_tensor(out=lg2[:, :, :], in0=hot[:, 0, :, :], scalar=-3.0e38, in1=lg,
                                                  op0=ALU.mult, op1=ALU.add))
                    scores = lg2[:, :, :]
            dve.tensor_tensor(top[:, :, 2], top[:, :, 1], top[:, :, 0], ALU.subtract).then_inc(top_diff, 1)
            dve.wait_ge(top_exp, 1)
            then(dve.tensor_scalar(top[:, :, 0], top[:, :, 3], 1.0, None, ALU.add))
            then(dve.reciprocal(top[:, :, 1], top[:, :, 0]))
            then(dve.tensor_tensor(top[:, :, 2], top[:, :, 3], top[:, :, 1], ALU.mult))
            then(dve.tensor_tensor(hot[:, 0, :, :], hot[:, 0, :, :], wide_of(1), ALU.mult))
            then(dve.tensor_tensor(hot[:, 1, :, :], hot[:, 1, :, :], wide_of(2), ALU.mult))
            then(dve.tensor_tensor(gate[:, :, :, :].rearrange("p b t e -> p (b t) e"),
                                   hot[:, 0, :, :], hot[:, 1, :, :], ALU.add))

            with dve.Fori(0, NB) as b:
                hid_jobs = dve.snap(b * NE + CREDIT + NB * G * EXPS // 2)
                y_jobs = dve.snap(b * (NE // 2) + CREDIT)

                def hidden(e):
                    for f in range(FH):
                        if e >= 2:
                            dve.wait_ge(y_full[e % 2], y_jobs + e // 2)
                        dve.wait_ge(silu_done[f], b * NE + e + 1)
                        dve.tensor_tensor(hid[:, e % 2, f, :], silu[:, f, :], wide[:, f, T:2 * T], ALU.mult)\
                           .then_inc(wide_free[f], 1)

                def add(e):
                    dve.wait_ge(y_full[e % 2], y_jobs + e // 2 + 1)
                    for t in range(NT):
                        ins = dve.scalar_tensor_tensor(out=y[:, t, :], in0=y_banks[:, e % 2, t * P:(t + 1) * P],
                                                       scalar=gate[:, b, t, e:e + 1],
                                                       in1=y[:, t, :] if e else res[:, b, t, :],
                                                       op0=ALU.mult, op1=ALU.add)
                    ins.then_inc(y_free[e % 2], 1)
                    dve.wait_ge(y_free[e % 2], y_jobs + e // 2 + 1)

                for e in range(NE):
                    hidden(e)
                    if e:
                        add(e - 1)
                add(NE - 1)
                norm_stats(lambda t: y[:, t, :], a_st, a_mv, a_ve, b + 1, final_stats, final_mean, final_var)
                dve.wait_ge(final_pow, b + 1)
                normalise(lambda t: a_xn[:, t, :], lambda t: y[:, t, :], a_mv, a_rstd, final_norm)


def tables():
    import numpy as np

    def by_tile(a):
        return np.ascontiguousarray(a.reshape(NT, P, -1).transpose(1, 0, 2))

    f32 = np.float32
    pos = np.arange(T, dtype=f32)[:, None]
    half = D // 2
    freq = np.power(f32(10000.0), -np.arange(half, dtype=f32) / f32(half)).astype(f32)
    ang = pos * freq[None, :]
    cos, sin = np.cos(ang).astype(f32), np.sin(ang).astype(f32)
    cos_a = by_tile(np.concatenate([cos, cos], 1))
    sin_a = by_tile(np.concatenate([-sin, sin], 1))
    inv = (f32(1.0) / np.power(f32(10000.0), np.arange(0, HD, 2, dtype=f32) / f32(HD))).astype(f32)
    ang = pos * inv[None, :]
    cos, sin = np.cos(ang).astype(f32), np.sin(ang).astype(f32)
    cos_b = np.tile(np.repeat(cos, 2, 1), (1, H))
    sin_b = np.tile(np.stack([-sin, sin], -1).reshape(T, HD), (1, H))
    cos_b, sin_b = (np.ascontiguousarray(np.stack([by_tile(a)] * 2, 1)) for a in (cos_b, sin_b))
    q, k = np.arange(P)[:, None], np.arange(P)[None, :]
    future = np.where(k > q, f32(-1e30), f32(0))
    slot_index = np.ascontiguousarray(np.broadcast_to(np.arange(NE, 0, -1, dtype=f32), (P, NB * NT, NE)))
    return {"cos_a": cos_a, "sin_a": sin_a, "cos_b": cos_b, "sin_b": sin_b, "ident_f": np.eye(P, dtype=f32),
            "future": future, "future_t": np.ascontiguousarray(future.T), "slot_index": slot_index}


INPUTS = ["L0_attn_x", "L0_attn_wq", "L0_attn_wk", "L0_attn_wv", "L0_attn_wo", "L0_ffn_g1", "L0_ffn_g2",
          "L0_ffn_w_down", "L0_ffn_wq", "L0_ffn_wk", "L0_ffn_wv", "L0_ffn_w_up", "L0_ffn_router_w",
          "L0_ffn_w1", "L0_ffn_w2", "L0_ffn_w3"]


def kernel(**inputs):
    import numpy as np
    import concourse.bacc as bacc
    from concourse.bass_utils import run_bass_kernel_spmd

    nc = bacc.Bacc("TRN2", target_bir_lowering=False, num_devices=1)
    arrays = {name: np.ascontiguousarray(inputs[name]) for name in INPUTS}
    arrays.update(tables())
    args = [nc.dram_tensor(n, a.shape, mybir.dt.from_np(a.dtype), kind="ExternalInput").ap()
            for n, a in arrays.items()]
    out = nc.dram_tensor("out", (NB, T, D), F32, kind="ExternalOutput").ap()
    program(nc, *args, out)
    r = run_bass_kernel_spmd(nc, [arrays], core_ids=[0])
    return r.results[0]["out"]
```

```python
from contextlib import ExitStack

import concourse.bass as bass
from concourse import mybir

F32 = mybir.dt.float32
U32 = mybir.dt.uint32
BF16 = mybir.dt.bfloat16
ACT = mybir.ActivationFunctionType
ALU = mybir.AluOpType
AX = mybir.AxisListType.X

P = 128
NB = 8
T = 512
NT = T // P
D = 128
L = 64
H = 16
HD = L // H
R = 4
G = H // R
SLOTS = 8
NE = 8
F = 256
FH = F // P
EPS = 1e-5
SCALE_A = 1.0 / D
SCALE_B = HD ** -0.5

JOBS = {
    "a_xT": ["a_xT"], **{f"a_qkv{t}": [f"a_qkv{t}"] for t in range(NT)}, "a_qkT": ["a_qT", "a_kT"],
    **{f"a_s{t}": [f"a_s{t}"] for t in range(NT)}, "a_pT": ["a_p0", "a_p1", "a_p2"],
    "a_oT": ["a_oT"], "a_r": ["a_r"],
    "p_hT": ["p_hT"], "p_cT": ["p_cT"], "p_qkv": ["p_qkv0", "p_qkv1"],
    "p_rows": ["p_k0", "p_k1", "p_q0", "p_q1"],
    "f_pv3": ["pv3", "o2"], "f_o": ["o3"], "f_oT": ["oT"], "f_up": ["up"], "f_tT": ["tT"],
    "f_logits": ["logits"], "f_rank": ["rank"],
    "m_pv0": ["pv0"], "m_pv1": ["pv1", "o0"], "f_pv2": ["pv2", "o1"],
}
for _g in range(G):
    JOBS[f"m_shift{_g}"] = [f"shift{_g}"]

MAX_JOBS = [(3, r, 1) for r in range(R)] + [(2, r, 1) for r in range(R)] + [(1, 0, 2), (1, 2, 2), (0, 0, R)]
PT_AT = {0: 0, 1: 512, 3: 896}
EXPS = R + 1


def mix_max(s):
    return range(len(MAX_JOBS) * s // EXPS, len(MAX_JOBS) * (s + 1) // EXPS)


SCHEDULE = [
    "m_cut0", "f_pv2", "m_shift0", "p_rnorm", "a_stats",
    "m_mix00", "a_norm", "m_mix01", "a_xT", "p_stats", "m_mix02", "a_qkv0", "a_qkv1", "m_mix03",
    "a_qkv2", "p_norm", "m_mix04", "a_qkv3", "m_cut1", "f_pv3", "m_shift1", "p_hT",
    "m_mix10", "p_cT", "m_mix11", "p_qkv", "m_mix12", "f_o", "m_mix13", "f_oT", "p_cut", "m_mix14",
    "m_cut2", "m_pv0", "m_shift2", "f_up",
    "m_mix20", "a_qkT", "m_mix21", "a_s0", "p_slots", "m_mix22", "a_s1", "f_tT", "m_mix23", "a_s2", "f_logits",
    "m_mix24", "a_s3", "f_route0",
    "m_cut3", "m_pv1", "f_route1", "p_rows", "f_route2", "m_shift3", "a_pT",
    "m_mix30", "f_route3", "m_mix31", "a_oT", "f_rank", "m_mix32", "a_r", "f_route4", "m_mix33", "f_route5",
    "m_mix34", "a_rstats",
]
FILL_SCHEDULE = [
    "p_rnorm", "a_stats", "p_stats", "a_norm", "a_xT", "p_norm", "a_qkv0", "a_qkv1", "a_qkv2", "a_qkv3",
    "p_hT", "p_cT", "p_qkv", "a_qkT", "a_s0", "p_cut", "a_s1", "a_s2", "a_s3", "p_slots", "p_rows",
    "a_pT", "a_oT", "p_max0",
    "a_r", "a_rstats",
]


def steps(stages):
    order = SCHEDULE if "m" in stages or "f" in stages else FILL_SCHEDULE
    return [s for s in order if s[0] in stages]


def jobs(stages):
    order = []
    for step in steps(stages):
        if step.startswith("m_mix"):
            g, s = int(step[-2]) + 1, int(step[-1])
            if g < G or "p" in stages:
                order += [f"max{g % G}_{n}" for n in mix_max(s)]
        elif step == "p_max0":
            order += [f"max0_{n}" for n in range(len(MAX_JOBS))]
        else:
            order += JOBS.get(step, [])
    return order


NTOK = NB * T
TOP = 2
ROW = D + 1
REGION = NTOK + P
TILES = (TOP * NTOK + NE * (P - 1)) // P
SPARE = TILES - TOP * NTOK // P
FULL = NTOK // P
BUFS = 8
E_CREDIT = BUFS
DIFF_AT, SEL_AT, PLACE_AT, ROUTE_OPS = 12, 13, 18, 23
CREDIT = 1
N_FIRST, N_SECOND, N_CONSTS, N_WEIGHTS, N_FILLS = 4, 6, 13, 2 + NE, 6


class Tile:

    def __init__(self, u, c):
        self.u, self.c, self.n = u, c, BUFS * u + c
        self.buf, self.half, self.turn = c % BUFS, c % 2, u + c // BUFS

    def __add__(self, d):
        return Tile(self.u, self.c + d)

    def exists(self):
        return not isinstance(self.n, int) or 0 <= self.n < TILES


def tile_steps(eng, body, begin=lambda first, count: None):
    looped = (TILES - 3) // BUFS * BUFS
    begin(0, BUFS + 2)
    for s in range(-2, 1 + BUFS):
        body(Tile(0, s))
    with eng.Fori(1, looped // BUFS) as u:
        begin(BUFS * u, BUFS + 2)
        for s in range(1, 1 + BUFS):
            body(Tile(u, s))
    begin(looped, TILES - looped)
    for s in range(1 + looped, TILES + 1):
        body(Tile(0, s))


def batch_steps(eng, body):
    body(0, 0)
    with eng.Fori(0, NB // 2 - 1) as j:
        for n in (1, 2):
            body(eng.snap(2 * j + n), n % 2)
    body(NB - 1, 1)
    body(NB, 0)


def is_max(job):
    return job.startswith("max")


class Batch:

    def __init__(self, n, parity):
        self.n, self.parity, self.now = n, parity, n + 1


class Rings:

    def __init__(self, full, free, order, before):
        self.full, self.free, self.before = full, free, before
        self.order = ([j for j in order if is_max(j)], [j for j in order if not is_max(j)])

    def index(self, job):
        ring = not is_max(job)
        return self.order[ring].index(job) + self.before[ring][1]

    def bank(self, job):
        return self.index(job) % 2 + (0 if is_max(job) else 2)

    def turns(self, job):
        return self.index(job) // 2

    def count(self, job):
        return self.turns_before(self.bank(job)) + self.turns(job) + 1

    def turns_before(self, bank):
        return self.before[bank // 2][0]


def wait(eng, sem, value):
    if not (isinstance(value, int) and value <= 0):
        eng.wait_ge(sem, value)


def program(nc, x, wq_a, wk_a, wv_a, wo_a, g1, g2, w_down, wq_b, wk_b, wv_b, w_up, router_w,
            w1, w2, w3, cos_a, sin_a, cos_b, sin_b, ident_f, future, future_t, first_slot, region_at,
            full_tiles, tile_numbers, up_to, result_at, before, padding, out):
    with ExitStack() as ctx:
        def sb(name, shape, dt=F32):
            return ctx.enter_context(nc.sbuf_tensor(name, shape, dt))

        def ps(name, shape, dt=F32):
            return ctx.enter_context(nc.psum_tensor(name, shape, dt))

        def sem(name):
            return ctx.enter_context(nc.semaphore(name))

        wqkv_a = sb("wqkv_a_sb", [P, 3 * D])
        wo_sb = sb("wo_sb", [P, D])
        wdown_sb = sb("wdown_sb", [P, L])
        wqkv_b = sb("wqkv_b_sb", [L, 3 * L])
        wup_sb = sb("wup_sb", [L, D])
        router_sb = sb("router_sb", [P, NE])
        g1_sb = sb("g1_sb", [P, 1])
        g2_sb = sb("g2_sb", [P, 1])
        cos_a_sb = sb("cos_a_sb", [P, NT, D])
        sin_a_sb = sb("sin_a_sb", [P, NT, D])
        cos_b_sb = sb("cos_b_sb", [P, 2, NT, L])
        sin_b_sb = sb("sin_b_sb", [P, 2, NT, L])
        idf = sb("idf", [P, P])
        idb = sb("idb", [P, P], BF16)
        future_sb = sb("future_sb", [P, R, P], BF16)
        future_T = sb("future_T", [P, 2, P], BF16)
        neg_half = sb("neg_half", [P, NT])
        x1 = sb("x1", [P, NB, NT, D])
        res = sb("res", [P, NB, NT, D])
        gate = sb("gate", [P, NB, NT, TOP])
        a_st = sb("a_st", [P, NT, 6])
        a_mv = sb("a_mv", [P, NT, 2])
        a_ve = sb("a_ve", [P, NT])
        a_rstd = sb("a_rstd", [P, NT])
        a_xn = sb("a_xn", [P, NT, D])
        a_xT = sb("a_xT_sb", [P, T])
        a_qkv = sb("a_qkv_sb", [P, NT, 3 * D])
        a_work = sb("a_work", [P, 2, NT * 2 * D])
        a_m1, a_m2 = (a_work[:, n, :].rearrange("p (t a d) -> p t a d", t=NT, a=2) for n in range(2))
        a_qT = sb("a_qT_sb", [P, T])
        a_kT = sb("a_kT_sb", [P, T])
        a_nm = sb("a_nm", [P, NT])
        a_nb = sb("a_nb", [P, NT])
        a_p = sb("a_p_sb", [P, NT, T])
        a_sum = sb("a_sum", [P, NT])
        a_ri = sb("a_ri", [P, NT])
        a_pT = a_work[:, :, :].rearrange("p n w -> p (n w)")[:, 0:3 * T].rearrange("p (n w) -> p n w", n=3)
        p_st = sb("p_st", [P, NT, 6])
        p_mv = sb("p_mv", [P, NT, 2])
        p_ve = sb("p_ve", [P, NT])
        p_rstd = sb("p_rstd", [P, NT])
        p_m1 = sb("p_m1", [P, NT])
        p_m2 = sb("p_m2", [P, NT])
        p_ms = sb("p_ms", [P, NT])
        p_rs = sb("p_rs", [P, NT])
        p_hT = sb("p_hT_sb", [P, T])
        p_cT = sb("p_cT_sb", [L, T])
        p_qk = sb("p_qk", [P, 2, NT, L])
        p_t1 = sb("p_t1", [P, 2, NT, L])
        h0 = p_t1[:, :, :, :].rearrange("p a t l -> p (a t l)").rearrange("p (t d) -> p t d", t=NT)
        p_t2 = sb("p_t2", [P, 2, NT, L])
        part1 = sb("part1", [P, 2, NT * H, HD], BF16)
        part2 = sb("part2", [P, 2, NT * H, HD], BF16)
        part3 = sb("part3", [P, 2, NT * H, HD], BF16)
        q_rows = sb("q_rows", [P, 2, NT, H, SLOTS, HD], BF16)
        k_rows = sb("k_rows", [P, NT, H, SLOTS, HD], BF16)
        k_all = sb("k_all", [P, G, T], BF16)
        kz = sb("kz", [P, 2, G, R, T], BF16)
        qT1 = sb("qT1", [P, 2, G, T], BF16)
        v_pad = sb("v_pad", [P, 2, NT, H, HD + 1])
        nmax = sb("nmax", [P, NT, H])
        nm_r1 = sb("nm_r1", [P, NT, R])
        nm_r2 = sb("nm_r2", [P, NT, R])
        qT2 = sb("qT2", [P, 2, T], BF16)
        pT = sb("pT", [P, 2, EXPS, 2 * T])
        oT_g = sb("oT_g", [P, 2, T])
        inv = sb("inv", [P, 2, NT, R])
        o_tok = sb("o_tok", [P, NT, L])
        oT_sb = sb("oT_sb", [L, T])
        m_sq = sb("m_sq", [P, NT])
        m_ms = sb("m_ms", [P, NT])
        m_rs = sb("m_rs", [P, NT])
        m_row = sb("m_row", [P, TOP, NT, ROW])
        m_tT = sb("m_tT", [P, T])
        slot_sb = sb("slot_sb", [P, NT, NE])
        region_sb = sb("region_sb", [P, NT, NE])
        before_sb = sb("before_sb", [P, P], BF16)
        ones = sb("ones", [P, P], BF16)
        result_sb = sb("result_sb", [P, TOP, NT])
        lgs = sb("lgs", [P, NT, NE])
        lg2 = sb("lg2", [P, NT, NE])
        e_tmp = sb("e_tmp", [P, NT, NE])
        top = sb("top", [P, NT, 5])
        hot = sb("hot", [P, TOP, NT, NE])
        sel = sb("sel", [P, NT, NE], BF16)
        sel_sum = sb("sel_sum", [P, NE])
        sel_before = sb("sel_before", [P, NT, NE], BF16)
        place = sb("place", [P, NT, NE])
        place2 = sb("place2", [P, TOP, NT, NE])
        place_f = sb("place_f", [P, TOP, NT])
        place_u = sb("place_u", [P, TOP, NT], U32)
        def carve(tensor, shapes):
            views, at = [], 0
            for shape in shapes:
                size, names = 1, " ".join(f"d{n}" for n in range(len(shape)))
                for n in shape:
                    size *= n
                view = tensor[:, at:at + size]
                views.append(view.rearrange(f"p ({names}) -> p {names}",
                                            **{f"d{n}": v for n, v in enumerate(shape)}))
                at += -(-size // 4) * 4
            return views

        w13, w2_sb, yin = carve(kz[:, :, :, :, :].rearrange("p a g r t -> p (a g r t)").bitcast(F32),
                                [[NE, 2 * F], [NE, FH, D], [2, TOP, NT * D]])
        (x_rows, x_T, silu, hid, hid_T, y_rows, parts, y, xn, gate_now, le, le2, cmp, full_sb, up_to_sb,
         chosen, tiles_of, tiles_to, pad_f, pad_uf, numbers_sb, tile_e, tile_first, tile_row, row_uf, expert_uf) = carve(
            pT[:, :, :, :].rearrange("p a s t -> p (a s t)"),
            [[BUFS, ROW], [2, D], [2, F], [2, F], [2, F], [BUFS, D], 
             [2, TOP, NT, D], [2, NT, D], [2, NT, D], [2, NT, TOP], [TILES, NE],
             [TILES, NE], [NE, FULL], [NE, FULL], [NE, NE], *[[NE]] * 5, *[[TILES]] * 6])
        pad_u, row_u, expert_u = (v.bitcast(U32) for v in (pad_uf, row_uf, expert_uf))
        masks_in = pT[:, 0, 0, 0:3 * P].rearrange("p (n k) -> p n k", n=3)
        future_in, future_t_in, before_in = (masks_in[:, n, :] for n in range(3))
        dest = sb("dest", [P, BUFS], U32)
        token_rows = nc.dram_tensor("token_rows", (NE * REGION + SPARE * P, ROW), F32).ap()
        result_rows = nc.dram_tensor("result_rows", (TOP * NTOK + (NE + SPARE) * P, D), F32).ap()

        small = ps("small", [P, 4, T])
        wide = ps("wide", [P, 2, 2 * T])

        small_full = [sem(f"small_full{i}") for i in range(4)]
        small_free = [sem(f"small_free{i}") for i in range(4)]
        wide_full = [sem(f"wide_full{i}") for i in range(2)]
        wide_free = [sem(f"wide_free{i}") for i in range(2)]
        first_in = sem("first_in")
        second_in = sem("second_in")
        masks_done = sem("masks_done")
        consts_in = sem("consts_in")
        weights_in = sem("weights_in")
        fills = sem("fills")
        x_first = sem("x_first")
        x_rest = sem("x_rest")
        names = ["a_stats", "a_var", "a_vareps", "a_rstd", "a_xn", "a_rope1_q", "a_rope1_k", "a_rope_q",
                 "a_rope_k", "a_nmax", "a_nbias",
                 "a_inv", "a_rstats", "a_rvar", "a_rvareps", "a_rrstd", "a_rn", "x1_ready",
                 "p_stats", "p_var", "p_vareps", "p_rstd", "p_h0", "p_kept", "p_w1", "p_w2", "p_ms", "p_rs",
                 "p_rope1", "p_rope", "p_part1", "p_rest1", "p_part2", "p_rest2", "p_part3", "p_rows", "p_qrows",
                 "sq_done", "m_ms", "m_rs", "m_t"]
        names += ["q_" + n for n in ("rope1", "rope", "part1", "rest1", "part2", "rest2", "part3")]
        S = {n: sem("s_" + n) for n in names}
        kz_in = sem("kz_in")
        route = sem("route")
        sent = sem("sent")
        totals_full = sem("totals_full")
        tables_done = sem("tables_done")
        pads_done = sem("pads_done")
        spare_in = sem("spare_in")
        tables_in = sem("tables_in")
        pad_in = sem("pad_in")
        x_in = [sem(f"x_in{i}") for i in range(BUFS)]
        y_out = [sem(f"y_out{i}") for i in range(BUFS)]
        xT_full, xT_free, h_full, e_silu, hid_done, hT_full, hT_free, y_full, y_free, dest_done = (
            sem("e_" + n) for n in ("xT_full", "xT_free", "h_full", "silu", "hid_done", "hT_full", "hT_free",
                                    "y_full", "y_free", "dest_done"))
        yin_in = [sem(f"yin_in{i}") for i in range(2)]
        yin_used = sem("yin_used")
        summed = sem("summed")
        weighted = sem("weighted")
        gate_in = sem("gate_in")
        cut = sem("cut")
        inv_done = sem("inv_done")
        filled = sem("filled")
        top_exp = sem("top_exp")
        final_stats = sem("final_stats")
        final_mean = sem("final_mean")
        final_var = sem("final_var")
        final_norm = sem("final_norm")
        final_out = sem("final_out")
        table_step = sem("table_step")
        final_pow = sem("final_pow")
        out_done = sem("out_done")

        block = ctx.enter_context(nc.Block())

        FIRST = ("a", "ap", "apm", "apmf")
        LOOP = "apmf"
        LAST = ("pmf", "mf", "f")
        LOOPED = (len(FIRST), NB)

        def jobs_before(i):
            before = [j for k in range(i) for j in jobs((*FIRST, *[LOOP] * (NB - len(FIRST)), *LAST)[k])]
            maxima = sum(map(is_max, before))
            return [(n // 2, n % 2) for n in (maxima, len(before) - maxima)]

        def iterations(eng, body):
            def one(stages, i, parity, before):
                batch = {s: Batch(i - n, (parity - n) % 2) if s in stages else None for n, s in enumerate("apmf")}
                body(stages, batch["a"], batch["p"], batch["m"], batch["f"],
                     Rings(small_full, small_free, jobs(stages), before))

            for i, stages in enumerate(FIRST):
                one(stages, i, i % 2, jobs_before(i))
            first = LOOPED[0]
            with eng.Fori(LOOPED[0] // 2, LOOPED[1] // 2) as j:
                for par in range(2):
                    i = eng.snap(2 * j + par)
                    before = [(eng.snap(j * (after - turns) + (turns - first // 2 * (after - turns))), odd)
                              for (turns, odd), (after, _) in zip(jobs_before(first + par), jobs_before(first + par + 2))]
                    one(LOOP, i, par, before)
            for i, stages in enumerate(LAST, LOOPED[1]):
                one(stages, i, i % 2, jobs_before(i))

        last_count = [0] * 4
        for _i in range(NB + 3):
            _stages = (*FIRST, *[LOOP] * (NB - len(FIRST)), *LAST)[_i]
            _ring = Rings(small_full, small_free, jobs(_stages), jobs_before(_i))
            for _job in jobs(_stages):
                last_count[_ring.bank(_job)] = _ring.count(_job)
        last_ring = Rings(small_full, small_free, jobs(LAST[-1]), jobs_before(NB + 2))

        def wide_turns(m, w):
            return m.n * (G * EXPS // 2) + (w // 2 + CREDIT)

        def read_table(eng, table, first, count, top_value):
            at = table[0:1, first:first + count] if isinstance(first, int) else table[0:1, bass.ds(first, count)]
            return nc.values_load_multi_w_load_instructions(
                at, (eng.engine,), min_val=0, max_val=top_value,
                skip_runtime_bounds_check_because="the tables are built within these bounds")[1]

        def first_waits(eng, step, a, p):
            first = lambda batch: batch and isinstance(batch.n, int) and batch.n == 0
            if step == "a_qkv3" and first(a):
                eng.wait_ge(second_in, 16 * N_SECOND)
            if step == "a_s0" and first(a) and eng.engine == mybir.EngineType.PE:
                eng.wait_ge(masks_done, 1)
            if step == "p_hT" and first(p):
                eng.wait_ge(fills, N_FILLS)
                eng.wait_ge(consts_in, 16 * N_CONSTS)

        def in_fill(batch):
            return isinstance(batch.n, int) and batch.n < 2

        def p_in_fill(batch):
            return isinstance(batch.n, int) and batch.n == 0

        def rotate_p(eng, ring, p, kinds, chain):
            for j in ("p_qkv0", "p_qkv1"):
                eng.wait_ge(small_free[ring.bank(j)], ring.count(j))
            eng.wait_ge(S["p_kept"], p.now)
            flat = lambda b: b[:, kinds, :, :].rearrange("p a t l -> p (a t l)")
            qk, t1, t2, cos, sin = (flat(b) for b in (p_qk, p_t1, p_t2, cos_b_sb, sin_b_sb))
            pair = lambda b, n: b.rearrange("p (n two) -> p n two", two=2)[:, :, n]
            eng.tensor_tensor(t1, qk, cos, ALU.mult).then_inc(S[chain + "rope1"], 1)
            for n in range(2):
                eng.tensor_tensor(pair(t2, n), pair(qk, 1 - n), pair(sin, n), ALU.mult)\
                   .then_inc(S[chain + "rope1"], 1)
            eng.wait_ge(S[chain + "rope1"], 3 * p.now)
            eng.tensor_tensor(t1, t1, t2, ALU.add).then_inc(S[chain + "rope"], 1)

        def cut_p(eng, p, kinds, chain):
            t1, t2 = (b[:, kinds, :, :].rearrange("p a t l -> p (a t l)") for b in (p_t1, p_t2))
            parts = [b[:, kinds, :, :].rearrange("p a n d -> p (a n d)") for b in (part1, part2, part3)]
            held(eng, S[chain + "rope"], p.now)
            eng.tensor_copy(parts[0], t1).then_inc(S[chain + "part1"], 1)
            eng.wait_ge(S[chain + "part1"], p.now)
            eng.tensor_tensor(t2, t1, parts[0], ALU.subtract).then_inc(S[chain + "rest1"], 1)
            held(eng, S[chain + "rest1"], p.now)
            eng.tensor_copy(parts[1], t2).then_inc(S[chain + "part2"], 1)
            eng.wait_ge(S[chain + "part2"], p.now)
            eng.tensor_tensor(t1, t2, parts[1], ALU.subtract).then_inc(S[chain + "rest2"], 1)
            held(eng, S[chain + "rest2"], p.now)
            eng.tensor_copy(parts[2], t1).then_inc(S[chain + "part3"], 1)

        def rotate_a(eng, ring, a, kind):
            for j in ("a_qkv2", "a_qkv3"):
                eng.wait_ge(small_free[ring.bank(j)], ring.count(j))
            n = "qk".index(kind)
            x_in_ = a_qkv[:, :, n * D:(n + 1) * D]
            products, done = S["a_rope1_" + kind], S["a_rope_" + kind]
            eng.tensor_tensor(a_m1[:, :, n, :], x_in_, cos_a_sb[:, :, :], ALU.mult).then_inc(products, 1)
            for half in range(2):
                lo, other = half * D // 2, (1 - half) * D // 2
                eng.tensor_tensor(a_m2[:, :, n, lo:lo + D // 2], x_in_[:, :, other:other + D // 2],
                                  sin_a_sb[:, :, lo:lo + D // 2], ALU.mult).then_inc(products, 1)
            eng.wait_ge(products, 3 * a.now)
            eng.tensor_tensor(a_m1[:, :, n, :], a_m1[:, :, n, :], a_m2[:, :, n, :], ALU.add).then_inc(done, 1)

        def held(eng, sem_, value):
            value = value if isinstance(value, int) else eng.compute_val(value)
            eng.wait_ge(fills, 1)
            wait(eng, sem_, value)

        @block.sync
        def _(sp):
            def load_x(n, loaded):
                sp.dma_start(x1[:, n, :, :], x[n].rearrange("(t p) d -> p t d", p=P)).then_inc(loaded, 16)

            load_x(0, x_first)
            for dst, src in ((idf[:, :], ident_f), (wqkv_a[:, 0:D], wq_a[0]), (wqkv_a[:, D:2 * D], wk_a[0]),
                             (wqkv_a[:, 2 * D:3 * D], wv_a[0])):
                sp.dma_start(dst, src).then_inc(first_in, 16)
            for dst, src in ((cos_a_sb[:, :, :], cos_a), (sin_a_sb[:, :, :], sin_a), (wo_sb[:, :], wo_a[0]),
                             (future_in, future), (future_t_in, future_t), (before_in, before)):
                sp.dma_start(dst, src).then_inc(second_in, 16)
            load_x(1, x_rest)
            for dst, src in ((wdown_sb[:, :], w_down), (wqkv_b[:, 0:L], wq_b), (wqkv_b[:, L:2 * L], wk_b),
                             (wqkv_b[:, 2 * L:3 * L], wv_b), (wup_sb[:, :], w_up), (router_sb[:, :], router_w),
                             (g1_sb[:, :], g1.rearrange("(d o) -> d o", o=1)),
                             (g2_sb[:, :], g2.rearrange("(d o) -> d o", o=1)),
                             (cos_b_sb[:, :, :, :], cos_b), (sin_b_sb[:, :, :, :], sin_b),
                             (slot_sb[:, :, :], first_slot), (region_sb[:, :, :], region_at),
                             (result_sb[:, :, :], result_at)):
                sp.dma_start(dst, src).then_inc(consts_in, 16)
            for n in range(2, NB):
                load_x(n, x_rest)
            sp.dma_start(token_rows[NE * REGION:NE * REGION + SPARE * P, :],
                         padding[NE:NE + SPARE].rearrange("n p d -> (n p) d")).then_inc(spare_in, 16)

            def body(stages, a, p, m, f, ring):
                for step in steps(stages):
                    first_waits(sp, step, None, p)
                    if step == "p_rows":
                        c = sp.compute_val(ring.count("p_k1"))
                        sp.wait_ge(fills, 1)
                        sp.wait_ge(small_free[ring.bank("p_k1")], c)
                        for r in range(R):
                            sp.dma_start(kz[32 * r:32 * r + 32, p.parity, :, r, :],
                                         k_all[32 * r:32 * r + 32, :, :]).then_inc(kz_in, 16)

            iterations(sp, body)
            sp.wait_ge(small_free[last_ring.bank("pv3")], last_ring.count("pv3"))
            for dst, src in ((full_sb, full_tiles), (numbers_sb, tile_numbers), (up_to_sb, up_to)):
                sp.dma_start(dst, src).then_inc(tables_in, 16)
            sp.dma_start(w13[:, :, 0:F], w1.rearrange("e d f -> d e f")).then_inc(weights_in, 16)
            sp.dma_start(w13[:, :, F:2 * F], w3.rearrange("e d f -> d e f")).then_inc(weights_in, 16)
            for e in range(NE):
                sp.dma_start(w2_sb[:, e, :, :], w2[e].rearrange("(h p) d -> p h d", p=P)).then_inc(weights_in, 16)
            sp.wait_ge(pads_done, 1)
            for e, row in enumerate(read_table(sp, pad_u, 0, NE, NE * REGION - P)):
                sp.dma_start(token_rows[bass.ds(row, P), :], padding[e]).then_inc(pad_in, 16)
            sp.wait_ge(tables_done, 1)

            rows = {}

            def load_rows(tile):
                if tile.exists():
                    sp.wait_ge(xT_full, tile.n + (E_CREDIT + 1 - BUFS))
                    sp.wait_ge(dest_done, tile.n + (E_CREDIT + 1 - BUFS))
                    sp.dma_start(x_rows[:, tile.buf, :], token_rows[bass.ds(rows[tile.c % BUFS], P), :])\
                        .then_inc(x_in[tile.buf], 16)

            def read_rows(first, count):
                rows.update(enumerate(read_table(sp, row_u, first, min(count, BUFS), NE * REGION + (SPARE - 1) * P)))

            sp.wait_ge(pad_in, 16 * NE)
            sp.wait_ge(spare_in, 16)
            sp.wait_ge(sent, 16 * TOP * NT * NB)
            tile_steps(sp, lambda s: load_rows(s + -1), read_rows)
            for i in range(BUFS):
                sp.wait_ge(y_out[i], 16 * len(range(i, TILES, BUFS)))
            for b in range(NB):
                if b >= 2:
                    sp.wait_ge(weighted, b - 1)
                for n in range(TOP):
                    at = n * NTOK + b * T
                    sp.dma_start(yin[:, b % 2, n, :].rearrange("p (t d) -> p t d", t=NT),
                                 result_rows[at:at + T, :].rearrange("(t p) d -> p t d", p=P))\
                        .then_inc(yin_in[b % 2], 16)
            with sp.Fori(0, NB) as b:
                sp.wait_ge(final_out, b + 1)
                sp.dma_start(out[b].rearrange("(t p) d -> p t d", p=P), x1[:, b, :, :]).then_inc(out_done, 16)
            sp.wait_ge(out_done, 16 * NB)

        @block.tensor
        def _(pe):
            def take(ring, job, after=(), alone=False):
                need = {ring.bank(job): ring.turns(job)}
                for j in after:
                    need[ring.bank(j)] = max(need.get(ring.bank(j), 0), ring.turns(j) + 1)
                for bank, turns in need.items():
                    (held if alone else wait)(pe, small_free[bank], ring.turns_before(bank) + turns)
                return small[:, ring.bank(job), :]

            def full(ring, job, last):
                last.then_inc(small_full[ring.bank(job)], 1)

            def max_job(m, ring, g, n):
                job = f"max{g}_{n}"
                tile, r0, heads = MAX_JOBS[n]
                keys = (tile + 1) * P
                if (g, n) == (0, 0):
                    pe.wait_ge(kz_in, 16 * R * m.now)
                bank = take(ring, job, ["p_q0", "p_q1"] if (g, n) == (0, 0) else ())
                for r in range(r0, r0 + heads):
                    at = (r - r0) * keys
                    pe.matmul(bank[:, at:at + keys], qT1[:, m.parity, g, tile * P:(tile + 1) * P],
                              kz[:, m.parity, g, r, 0:keys], start=(r == r0), stop=False, skip_group_check=True)
                diagonal = bank[:, 0:heads * keys].rearrange("p (h k) -> p h k", h=heads)[:, :, keys - P:keys]
                last = pe.matmul(diagonal, idb[:, :], future_sb[:, 0:heads, :], start=False, stop=True,
                                 skip_group_check=True)
                full(ring, job, last)

            def exp_job(m, g, s):
                w = g * EXPS + s
                wait(pe, wide_free[w % 2], wide_turns(m, w))
                bank = wide[:, w % 2, :]
                if s < R:
                    blocks = [(s, tile, at) for tile, at in PT_AT.items()]
                    diagonals = [bank[:, 0:P], bank[:, T:2 * T].rearrange("p (n k) -> p n k", k=P)[:, 0:NT:3, :]]
                else:
                    blocks = [(r, 2, r * 2 * P) for r in range(R)]
                    diagonals = [bank[:, n * T:(n + 1) * T].rearrange("p (n k) -> p n k", k=P)[:, 0:NT:2, :]
                                 for n in range(2)]
                for r, tile, at in blocks:
                    pe.matmul(bank[:, at:at + T - tile * P], kz[:, m.parity, g, r, tile * P:(tile + 1) * P],
                              qT2[:, g % 2, tile * P:T], start=(at % T == 0), stop=False, skip_group_check=True)
                for diagonal in diagonals:
                    n = 1 if len(diagonal.shape) == 2 else 2
                    last = pe.matmul(diagonal, idb[:, :], future_T[:, 0:n, :] if n > 1 else future_T[:, 0, :],
                                     start=False, stop=True, skip_group_check=True)
                last.then_inc(wide_full[w % 2], 1)

            def transposes(ring, job, source, rows, ident, after=(), alone=False):
                bank = take(ring, job, after, alone)
                for t in range(NT):
                    last = pe.transpose(bank[0:rows, t * P:(t + 1) * P], source(t), ident)
                full(ring, job, last)

            def product_v(m, ring, g):
                for w in (g * EXPS + EXPS - 2, g * EXPS + EXPS - 1):
                    pe.wait_ge(wide_free[w % 2], wide_turns(m, w) + 1)
                bank = take(ring, f"pv{g}")
                for k in range(NT):
                    for r in range(R):
                        if k == 2:
                            probs = pT[:, g % 2, R, r * 2 * P:(r + 1) * 2 * P]
                        else:
                            probs = pT[:, g % 2, r, PT_AT[k]:PT_AT[k] + T - k * P]
                        last = pe.matmul(bank[32 * r:32 * r + HD + 1, k * P:T],
                                         v_pad[:, m.parity, k, g * R + r, :], probs,
                                         start=(k == 0), stop=(k == NT - 1), skip_group_check=True)
                full(ring, f"pv{g}", last)

            def turn_o(m, ring, g):
                transposes(ring, f"o{g}", lambda t: oT_g[:, g % 2, t * P:(t + 1) * P], P, idf[:, :],
                           [f"pv{g}"] if g != 1 else ())

            def body(stages, a, p, m, f, ring):
                for step in steps(stages):
                    first_waits(pe, step, a, p)
                    if step == "a_xT":
                        pe.wait_ge(S["a_xn"], a.now)
                        transposes(ring, "a_xT", lambda t: a_xn[:, t, :], P, idf[:, :])
                    elif step.startswith("a_qkv"):
                        t = int(step[-1])
                        bank = take(ring, step, ["a_xT"] if t == 0 else ())
                        full(ring, step, pe.matmul(bank[:, 0:3 * D], a_xT[:, t * P:(t + 1) * P],
                                                   wqkv_a[:, :], start=True, stop=True))
                    elif step == "a_qkT":
                        pe.wait_ge(S["a_rope_q"], a.now)
                        transposes(ring, "a_qT", lambda t: a_m1[:, t, 0, :], P, idf[:, :])
                        pe.wait_ge(S["a_rope_k"], a.now)
                        transposes(ring, "a_kT", lambda t: a_m1[:, t, 1, :], P, idf[:, :])
                    elif step[:3] == "a_s" and step in JOBS:
                        t = int(step[-1])
                        keys = (t + 1) * P
                        bank = take(ring, step, ["a_qT", "a_kT"] if t == 0 else ())
                        pe.matmul(bank[:, 0:keys], a_qT[:, t * P:keys], a_kT[:, 0:keys],
                                  start=True, stop=False, skip_group_check=True)
                        full(ring, step, pe.matmul(bank[:, t * P:keys], idb[:, :], future_sb[:, 0, :],
                                                   start=False, stop=True, skip_group_check=True))
                    elif step == "a_pT":
                        for job, blocks in (("a_p0", [(0, 0), (1, 0), (2, 0), (3, 0)]),
                                            ("a_p1", [(1, 1), (2, 1), (3, 1), (3, 3)]),
                                            ("a_p2", [(2, 2), (3, 2)])):
                            bank = take(ring, job, ["a_s2", "a_s3"] if job == "a_p0" else ())
                            for n, (i, k) in enumerate(blocks):
                                last = pe.transpose(bank[:, n * P:(n + 1) * P], a_p[:, i, k * P:(k + 1) * P], idf[:, :])
                            full(ring, job, last)
                    elif step == "a_oT":
                        bank = take(ring, "a_oT", ["a_p0", "a_p1", "a_p2"])
                        for k, (n, at) in enumerate(((0, 0), (1, 0), (2, 0), (1, 3 * P))):
                            last = pe.matmul(bank[:, k * P:T], a_qkv[:, k, 2 * D:3 * D],
                                             a_pT[:, n, at:at + T - k * P], start=(k == 0), stop=(k == NT - 1),
                                             skip_group_check=True)
                        full(ring, "a_oT", last)
                    elif step == "a_r":
                        bank = take(ring, "a_r", ["a_oT"])
                        for t in range(NT):
                            last = pe.matmul(bank[:, t * P:(t + 1) * P], a_xT[:, t * P:(t + 1) * P], wo_sb[:, :],
                                             start=True, stop=True)
                        full(ring, "a_r", last)
                    elif step == "p_hT":
                        pe.wait_ge(S["p_h0"], p.now)
                        transposes(ring, "p_hT", lambda t: h0[:, t, :], P, idf[:, :])
                    elif step == "p_cT":
                        bank = take(ring, "p_cT", ["p_hT"])
                        full(ring, "p_cT", pe.matmul(bank[0:L, :], wdown_sb[:, :], p_hT[:, :], start=True, stop=True))
                    elif step == "p_qkv":
                        for n in range(2):
                            bank = take(ring, f"p_qkv{n}", ["p_cT"] if n == 0 else ())
                            for t in (2 * n, 2 * n + 1):
                                at = (t % 2) * 3 * L
                                last = pe.matmul(bank[:, at:at + 3 * L], p_cT[:, t * P:(t + 1) * P], wqkv_b[:, :],
                                                 start=True, stop=True)
                            full(ring, f"p_qkv{n}", last)
                    elif step == "p_rows":
                        pe.wait_ge(S["p_rows"], p.now)
                        pe.wait_ge(S["p_qrows"], p.now)
                        for kind, rows in (("k", lambda t, g: k_rows[:, t, g * R:(g + 1) * R, :, :]),
                                           ("q", lambda t, g: q_rows[:, p.parity, t, g * R:(g + 1) * R, :, :])):
                            for n in range(2):
                                bank = take(ring, f"p_{kind}{n}").bitcast(BF16)
                                for g in (2 * n, 2 * n + 1):
                                    for t in range(NT):
                                        at = (g % 2) * T + t * P
                                        last = pe.transpose(bank[:, at:at + P],
                                                            rows(t, g).rearrange("p h s d -> p (h s d)"), idb[:, :])
                                full(ring, f"p_{kind}{n}", last)
                    elif step == "p_max0":
                        for n in range(len(MAX_JOBS)):
                            max_job(p, ring, 0, n)
                    elif step.startswith("m_shift"):
                        g = int(step[-1])
                        pe.wait_ge(cut, 5 * (G * m.n + g + 1))
                        bank = take(ring, step[2:]).bitcast(BF16)
                        for t in range(NT):
                            rows = q_rows[:, m.parity, t, g * R:(g + 1) * R, :, :].rearrange("p h s d -> p (h s d)")
                            last = pe.transpose(bank[:, t * P:(t + 1) * P], rows, idb[:, :])
                        full(ring, step[2:], last)
                    elif step.startswith("m_mix"):
                        g, s = int(step[-2]), int(step[-1])
                        if s == 0:
                            pe.wait_ge(small_free[ring.bank(f"shift{g}")], ring.count(f"shift{g}"))
                        exp_job(m, g, s)
                        if g + 1 < G or p:
                            for n in mix_max(s):
                                max_job(m if g + 1 < G else p, ring, (g + 1) % G, n)
                    elif step[2:4] == "pv":
                        g = int(step[-1])
                        product_v(m if g < 2 else f, ring, g)
                        if g:
                            turn_o(m if g < 2 else f, ring, g - 1)
                    elif step == "f_o":
                        turn_o(f, ring, G - 1)
                    elif step == "f_oT":
                        transposes(ring, "oT", lambda t: o_tok[:, t, :], L, idf[:, :], [f"o{G - 1}"], alone=True)
                    elif step == "f_up":
                        bank = take(ring, "up", ["oT"])
                        for t in range(NT):
                            last = pe.matmul(bank[:, t * P:(t + 1) * P], oT_sb[:, t * P:(t + 1) * P], wup_sb[:, :],
                                             start=True, stop=True)
                        full(ring, "up", last)
                    elif step == "f_tT":
                        pe.wait_ge(S["m_t"], TOP * f.n + 1)
                        transposes(ring, "tT", lambda t: m_row[:, 0, t, 0:D], P, idf[:, :])
                    elif step == "f_logits":
                        bank = take(ring, "logits", ["tT"])
                        for t in range(NT):
                            last = pe.matmul(bank[:, t * NE:(t + 1) * NE], m_tT[:, t * P:(t + 1) * P], router_sb[:, :],
                                             start=True, stop=True)
                        full(ring, "logits", last)
                    elif step == "f_rank":
                        pe.wait_ge(route, ROUTE_OPS * f.n + SEL_AT)
                        bank = take(ring, "rank")
                        chosen_all = sel[:, :, :].rearrange("p t e -> p (t e)")
                        pe.matmul(bank[:, 0:NT * NE], before_sb[:, :], chosen_all, start=True, stop=False,
                                  skip_group_check=True)
                        for d in range(1, NT):
                            pe.matmul(bank[:, d * NE:NT * NE], ones[:, :], chosen_all[:, 0:(NT - d) * NE],
                                      start=False, stop=False, skip_group_check=True)
                        full(ring, "rank", pe.matmul(bank[:, 0:NT * NE], ones[:, :],
                                                     sel_before[:, :, :].rearrange("p t e -> p (t e)"),
                                                     start=False, stop=True, skip_group_check=True))

            pe.wait_ge(first_in, 16 * N_FIRST)
            iterations(pe, body)

            pe.wait_ge(route, ROUTE_OPS * NB)
            for w in range(2):
                pe.wait_ge(wide_free[w], CREDIT + NB * G * EXPS // 2)
            pe.matmul(wide[:, 0, 0:NE], ones[:, :], sel_before[:, 0, :], start=True, stop=True).then_inc(totals_full, 1)
            pe.wait_ge(weights_in, 16 * N_WEIGHTS)
            pe.wait_ge(tables_done, 1)
            for bank in range(4):
                pe.wait_ge(small_free[bank], last_count[bank])

            experts, group = {}, [0]
            group_index = lambda tile: tile.c - group[0]

            def read_experts(first, count):
                experts.update(enumerate(read_table(pe, expert_u, first, count, NE - 1)))

            def turn_rows(tile):
                pe.wait_ge(x_in[tile.buf], 16 * (tile.turn + 1))
                pe.wait_ge(xT_free, tile.n + (E_CREDIT - 1))
                pe.transpose(wide[:, tile.half, T:T + P], x_rows[:, tile.buf, 0:D], idf[:, :]).then_inc(xT_full, 1)

            def hidden(tile):
                e = experts[group_index(tile)]
                pe.wait_ge(xT_free, tile.n + (E_CREDIT + 1))
                pe.wait_ge(hid_done, tile.n + (E_CREDIT - 1))
                pe.matmul(wide[:, tile.half, 0:T], x_T[:, tile.half, :], w13[:, e, :],
                          start=True, stop=True).then_inc(h_full, 1)

            def turn_hidden(tile):
                pe.wait_ge(hid_done, tile.n + (E_CREDIT + 1))
                pe.wait_ge(hT_free, tile.n + (E_CREDIT - 1))
                for h in range(FH):
                    last = pe.transpose(small[:, tile.half, h * P:(h + 1) * P], hid[:, tile.half, h * P:(h + 1) * P],
                                        idf[:, :])
                last.then_inc(hT_full, 1)

            def down(tile):
                e = experts[group_index(tile)]
                pe.wait_ge(hT_free, tile.n + (E_CREDIT + 1))
                pe.wait_ge(y_free, tile.n + (E_CREDIT - 1))
                for h in range(FH):
                    last = pe.matmul(small[:, 2 + tile.half, 0:D], hid_T[:, tile.half, h * P:(h + 1) * P],
                                     w2_sb[:, e, h, :], start=(h == 0), stop=(h == FH - 1))
                last.then_inc(y_full, 1)

            def tile_step(s):
                group[0] = (s.c - 1) // BUFS * BUFS if s.c > BUFS else 0
                for part, tile in ((turn_rows, s + 2), (hidden, s + 1), (turn_hidden, s), (down, s + -1)):
                    if tile.exists():
                        part(tile)

            tile_steps(pe, tile_step, read_experts)

        @block.scalar
        def _(act):
            def evacuate(ring, job, out_, in_=None, scale=1.0):
                b = small[:, ring.bank(job), :]
                act.wait_ge(small_full[ring.bank(job)], ring.count(job))
                act.activation(out_, b if in_ is None else in_(b), ACT.Copy, scale=scale)\
                   .then_inc(small_free[ring.bank(job)], 1)

            def body(stages, a, p, m, f, ring):
                for step in steps(stages):
                    first_waits(act, step, a, p)
                    if step == "a_xT":
                        evacuate(ring, "a_xT", a_xT[:, :])
                    elif step.startswith("a_qkv"):
                        evacuate(ring, step, a_qkv[:, int(step[-1]), :], lambda b: b[:, 0:3 * D])
                    elif step == "a_qkT":
                        evacuate(ring, "a_qT", a_qT[:, :])
                    elif step[:3] == "a_s" and step in JOBS:
                        t = int(step[-1])
                        keys = (t + 1) * P
                        act.wait_ge(S["a_nbias"], NT * a.n + t + 1)
                        act.activation(a_p[:, t, 0:keys], small[:, ring.bank(step), 0:keys], ACT.Exp,
                                       bias=a_nb[:, t:t + 1], scale=SCALE_A, accum_out=a_sum[:, t:t + 1])\
                           .then_inc(small_free[ring.bank(step)], 1)
                    elif step == "a_pT":
                        evacuate(ring, "a_p0", a_pT[:, 0, :])
                        evacuate(ring, "a_p2", a_pT[:, 2, 0:2 * P], lambda b: b[:, 0:2 * P])
                    elif step == "a_oT":
                        evacuate(ring, "a_oT", a_xT[:, :])
                    elif step == "p_hT":
                        evacuate(ring, "p_hT", p_hT[:, :], scale=g1_sb[:, 0:1])
                    elif step == "p_cT":
                        evacuate(ring, "p_cT", p_cT[:, :], lambda b: b[0:L, :])
                    elif step == "p_qkv":
                        act.wait_ge(S["p_rs"], p.now)
                        for n in range(2):
                            job = f"p_qkv{n}"
                            act.wait_ge(small_full[ring.bank(job)], ring.count(job))
                            for t in (2 * n, 2 * n + 1):
                                bank = small[:, ring.bank(job), (t % 2) * 3 * L:(t % 2 + 1) * 3 * L]
                                act.activation(p_qk[:, :, t, :], bank[:, 0:2 * L].rearrange("p (a l) -> p a l", a=2),
                                               ACT.Copy, scale=p_rs[:, t:t + 1])
                                last = act.activation(v_pad[:, p.parity, t, :, 0:HD],
                                                      bank[:, 2 * L:3 * L].rearrange("p (h d) -> p h d", h=H),
                                                      ACT.Copy, scale=p_rs[:, t:t + 1])
                            last.then_inc(small_free[ring.bank(job)], 1)
                    elif step == "p_slots":
                        q = q_rows[:, p.parity, :, :, :, :].rearrange("p t h s d -> p (t h) s d")
                        act.wait_ge(S["q_part3" if p_in_fill(p) else "p_part3"], p.now)
                        for part, lo, hi in ((part1, 0, 3), (part2, 3, 5), (part3, 5, 6)):
                            last = act.activation(q[:, :, lo:hi, :],
                                                  part[:, 0, :, :].unsqueeze(2).to_broadcast([P, NT * H, hi - lo, HD]),
                                                  ACT.Copy)
                        last.then_inc(S["p_qrows"], 1)
                    elif step == "p_rows":
                        for n in range(2):
                            evacuate(ring, f"p_q{n}", qT1[:, p.parity, 2 * n:2 * n + 2, :].rearrange("p g t -> p (g t)"),
                                     lambda b: b.bitcast(BF16))
                    elif step.startswith("m_mix"):
                        g, s = int(step[-2]), int(step[-1])
                        w = g * EXPS + s
                        act.wait_ge(wide_full[w % 2], wide_turns(m, w) + 1)
                        act.activation(pT[:, g % 2, s, :], wide[:, w % 2, :], ACT.Exp, scale=SCALE_B)\
                           .then_inc(wide_free[w % 2], 1)
                    elif step[2:4] == "pv":
                        g = int(step[-1])
                        evacuate(ring, f"pv{g}", oT_g[:, g % 2, :])
                    elif step == "f_oT":
                        evacuate(ring, "oT", oT_sb[:, :], lambda b: b[0:L, :])
                    elif step == "f_up":
                        act.wait_ge(small_free[ring.bank("up")], ring.count("up"))
                        wait(act, sent, 16 * TOP * NT * f.n)
                        for t in range(NT):
                            last = act.activation(m_row[:, 0, t, 0:D], res[:, f.n, t, :], ACT.Square,
                                                  accum_out=m_sq[:, t:t + 1])
                        last.then_inc(S["sq_done"], 1)
                    elif step == "f_tT":
                        evacuate(ring, "tT", m_tT[:, :], scale=g2_sb[:, 0:1])
                    elif step == "f_route3":
                        act.wait_ge(route, ROUTE_OPS * f.n + DIFF_AT)
                        act.activation(top[:, :, 3], top[:, :, 2], ACT.Exp).then_inc(top_exp, 1)

            iterations(act, body)

            def rows_turned(tile):
                act.wait_ge(xT_full, tile.n + (E_CREDIT + 1))
                act.wait_ge(h_full, tile.n + (E_CREDIT - 1))
                act.activation(x_T[:, tile.half, :], wide[:, tile.half, T:T + P], ACT.Copy, scale=g2_sb[:, 0:1])\
                   .then_inc(xT_free, 1)

            def silu_of(tile):
                act.wait_ge(h_full, tile.n + (E_CREDIT + 1))
                act.wait_ge(hid_done, tile.n + (E_CREDIT - 1))
                act.activation(silu[:, tile.half, :], wide[:, tile.half, 0:F], ACT.Silu).then_inc(e_silu, 1)

            def hidden_turned(tile):
                act.wait_ge(hT_full, tile.n + (E_CREDIT + 1))
                act.wait_ge(y_full, tile.n + (E_CREDIT - 1))
                act.activation(hid_T[:, tile.half, :], small[:, tile.half, 0:F], ACT.Copy).then_inc(hT_free, 1)

            def tile_step(s):
                for part, tile in ((rows_turned, s + 2), (silu_of, s + 1), (hidden_turned, s)):
                    if tile.exists():
                        part(tile)

            tile_steps(act, tile_step)

            def final_step_of(b, par):
                if isinstance(b, int) and b == NB:
                    return
                act.activation(gate_now[:, par, :, :], gate[:, b, :, :], ACT.Copy).then_inc(gate_in, 1)
                act.wait_ge(yin_in[par], 16 * TOP * ((b - par) // 2 + 1))
                act.wait_ge(gate_in, b + 1)
                if not isinstance(b, int) or b >= 2:
                    act.wait_ge(yin_used, b - 1)
                for n in range(TOP):
                    for t in range(NT):
                        last = act.activation(parts[:, par, n, t, :], yin[:, par, n, t * D:(t + 1) * D], ACT.Copy,
                                              scale=gate_now[:, par, t, n:n + 1])
                last.then_inc(weighted, 1)

            batch_steps(act, final_step_of)

        @block.gpsimd
        def _(pool):
            def rsqrt(out_, in_, need, value, done):
                pool.wait_ge(need, value)
                pool.tensor_tensor(out_, in_, neg_half[:, :], ALU.pow).then_inc(done, 1)

            def send_rows(n):
                for t in range(NT):
                    pool.indirect_dma_start(token_rows[:, :],
                                            bass.IndirectOffsetOnAxis(ap=place_u[:, n, t:t + 1], axis=0),
                                            m_row[:, n, t, :], None).then_inc(sent, 16)

            def body(stages, a, p, m, f, ring):
                for step in steps(stages):
                    first_waits(pool, step, a, p)
                    if step == "a_stats":
                        rsqrt(a_rstd[:, :], a_ve[:, :], S["a_vareps"], a.now, S["a_rstd"])
                    elif step == "p_stats":
                        rsqrt(p_rstd[:, :], p_ve[:, :], S["p_vareps"], p.now, S["p_rstd"])
                    elif step == "p_norm":
                        rsqrt(p_rs[:, :], p_ms[:, :], S["p_ms"], p.now, S["p_rs"])
                    elif step == "a_qkv3":
                        for kind in ("k",) if in_fill(a) else ("q", "k"):
                            rotate_a(pool, ring, a, kind)
                    elif step == "a_r" and isinstance(a.n, int) and a.n == 0:
                        pool.memset(kz[:, :, :, :, :].rearrange("p a g r t -> p (a g r t)").bitcast(F32), 0.0)\
                            .then_inc(fills, 1)
                    elif step == "a_rstats":
                        rsqrt(a_rstd[:, :], a_ve[:, :], S["a_rvareps"], a.now, S["a_rrstd"])
                    elif step == "p_rnorm":
                        pool.wait_ge(S["a_rn"], p.now)
                        pool.tensor_tensor(x1[:, p.n, :, :], x1[:, p.n, :, :], a_xn[:, :, :],
                                           ALU.add).then_inc(S["x1_ready"], 1)
                    elif step == "p_qkv":
                        rotate_p(pool, ring, p, slice(1, 2) if p_in_fill(p) else slice(0, 2), "p_")
                    elif step == "p_cut":
                        cut_p(pool, p, slice(1, 2) if p_in_fill(p) else slice(0, 2), "p_")
                    elif step == "p_slots":
                        held(pool, S["p_part3"], p.now)
                        q = q_rows[:, p.parity, :, :, :, :].rearrange("p t h s d -> p (t h) s d")
                        k = k_rows[:, :, :, :, :].rearrange("p t h s d -> p (t h) s d")
                        pool.memset(q[:, :, 6, 0:3], 0.0)
                        for b, slots in ((part1, (0, 3, 5)), (part2, (1, 4)), (part3, (2,))):
                            for s in slots:
                                last = pool.tensor_copy(k[:, :, s, :], b[:, 1, :, :])
                        last.then_inc(S["p_rows"], 1)
                    elif step == "f_up":
                        rsqrt(m_rs[:, :], m_ms[:, :], S["m_ms"], f.now, S["m_rs"])
                        pool.wait_ge(S["m_rs"], f.now)
                        for n in range(TOP):
                            pool.tensor_tensor(m_row[:, n, :, 0:D], res[:, f.n, :, :],
                                               m_rs[:, :].unsqueeze(2).to_broadcast([P, NT, D]),
                                               ALU.mult).then_inc(S["m_t"], 1)
                    elif step == "f_rank":
                        held(pool, S["m_t"], TOP * f.now)
                        held(pool, route, ROUTE_OPS * f.n + PLACE_AT)
                        for n in range(TOP):
                            send_rows(n)

            for s in (*wide_full, *wide_free):
                pool.sem_inc(s, CREDIT)
            for s in (xT_full, xT_free, h_full, e_silu, hid_done, hT_full, hT_free, y_full, y_free, dest_done):
                pool.sem_inc(s, E_CREDIT)
            pool.memset(neg_half[:, :], -0.5).then_inc(fills, 1)
            iterations(pool, body)

            def send_result(tile):
                if tile.exists():
                    held(pool, y_free, tile.n + (E_CREDIT + 1))
                    pool.indirect_dma_start(result_rows[:, :],
                                            bass.IndirectOffsetOnAxis(ap=dest[:, tile.buf:tile.buf + 1], axis=0),
                                            y_rows[:, tile.buf, :], None).then_inc(y_out[tile.buf], 16)

            tile_steps(pool, lambda s: send_result(s + -1))
            stats = ((a_ve, a_rstd), (p_ve, p_rstd))

            def add_residual(b, par):
                pool.wait_ge(weighted, b + 1)
                pool.tensor_tensor(parts[:, par, 0, :, :], parts[:, par, 0, :, :], res[:, b, :, :], ALU.add)\
                    .then_inc(summed, 1)

            def final_step_of(b, par):
                if not isinstance(b, int) or b < NB:
                    if isinstance(b, int) and b == 0:
                        add_residual(b, par)
                    if not isinstance(b, int) or b < NB - 1:
                        add_residual(b + 1, 1 - par)
                    ve, rstd = stats[par]
                    pool.wait_ge(final_var, b + 1)
                    pool.tensor_tensor(rstd[:, :], ve[:, :], neg_half[:, :], ALU.pow).then_inc(final_pow, 1)

            batch_steps(pool, final_step_of)

        @block.vector
        def _(dve):
            def empty(ring, job, ins):
                ins.then_inc(small_free[ring.bank(job)], 1)

            def await_job(ring, job):
                dve.wait_ge(small_full[ring.bank(job)], ring.count(job))
                return small[:, ring.bank(job), :]

            def norm_stats(src, st, mv, ve, now, stats, var, vareps):
                for t in range(NT):
                    last = dve.bn_stats(st[:, t, :], src(t))
                last.then_inc(stats, 1)
                held(dve, stats, now)
                for t in range(NT):
                    last = dve.bn_aggr(mv[:, t, :], st[:, t, :])
                last.then_inc(var, 1)
                dve.wait_ge(var, now)
                dve.tensor_scalar(ve[:, :], mv[:, :, 1], EPS, None, ALU.add).then_inc(vareps, 1)

            def normalise(dst, src, mv, rstd, done):
                for t in range(NT):
                    last = dve.tensor_scalar(dst(t), src(t), mv[:, t, 0:1], rstd[:, t:t + 1],
                                             ALU.subtract, ALU.mult)
                last.then_inc(done, 1)

            def max_job(m, ring, g, n):
                job = f"max{g}_{n}"
                tile, r0, heads = MAX_JOBS[n]
                bank = await_job(ring, job)
                ins = dve.tensor_reduce(nmax[:, tile, g * R + r0:g * R + r0 + heads],
                                        bank[:, 0:heads * (tile + 1) * P].rearrange("p (h k) -> p h k", h=heads),
                                        AX, ALU.max, negate=True)
                empty(ring, job, ins)
                if (g, n) == (0, len(MAX_JOBS) - 1):
                    dve.wait_ge(small_free[ring.bank(job)], ring.count(job))

            def prepare():
                dve.wait_ge(first_in, 16 * N_FIRST)
                dve.tensor_copy(idb[:, :], idf[:, :])
                dve.tensor_copy(before_sb[:, :], before_in)
                dve.tensor_copy(future_sb[:, :, :], future_in.unsqueeze(1).to_broadcast([P, R, P]))
                dve.tensor_copy(future_T[:, :, :], future_t_in.unsqueeze(1).to_broadcast([P, 2, P]))\
                   .then_inc(masks_done, 1)
                dve.memset(q_rows[:, :, :, :, :, :].rearrange("p a t h s d -> p (a t h s d)").bitcast(F32), 0.0)\
                   .then_inc(fills, 1)
                dve.memset(k_rows[:, :, :, :, :].rearrange("p t h s d -> p (t h s d)").bitcast(F32), 0.0).then_inc(filled, 1)
                dve.memset(v_pad[:, :, :, :, :].rearrange("p a t h c -> p (a t h c)"), 0.0).then_inc(filled, 1)
                dve.wait_ge(filled, 2)
                dve.memset(k_rows[:, :, :, 6, 0:3].rearrange("p t h c -> p (t h) c"), 1.0).then_inc(fills, 1)
                dve.memset(ones[:, :], 1.0)
                dve.memset(sel_before[:, :, :], 0.0).then_inc(fills, 1)
                dve.memset(v_pad[:, :, :, :, HD].rearrange("p a t h -> p (a t h)"), 1.0).then_inc(fills, 1)

            routed = [0]

            def then(f, ins):
                routed[0] += 1
                ins.then_inc(route, 1)
                dve.wait_ge(route, ROUTE_OPS * f.n + routed[0])

            def find_top(f, n, scores, parts=range(5)):
                wide_of = lambda c: top[:, :, c:c + 1].to_broadcast([P, NT, NE])
                ops = (
                    lambda: dve.tensor_reduce(top[:, :, n], scores[:, :, :], AX, ALU.max),
                    lambda: dve.tensor_tensor(e_tmp[:, :, :], scores[:, :, :], wide_of(n), ALU.is_equal),
                    lambda: dve.tensor_tensor(e_tmp[:, :, :], e_tmp[:, :, :], slot_sb[:, :, :], ALU.mult),
                    lambda: dve.tensor_reduce(top[:, :, 2], e_tmp[:, :, :], AX, ALU.max),
                    lambda: dve.tensor_tensor(hot[:, n, :, :], slot_sb[:, :, :], wide_of(2), ALU.is_equal))
                for k in parts:
                    then(f, ops[k]())

            def body(stages, a, p, m, f, ring):
                for step in steps(stages):
                    first_waits(dve, step, a, p)
                    if step == "a_stats":
                        if isinstance(a.n, int) and a.n == 0:
                            dve.wait_ge(x_first, 16)
                        else:
                            dve.wait_ge(x_rest, 16 * (NB - 1))
                        norm_stats(lambda t: x1[:, a.n, t, :], a_st, a_mv, a_ve, a.now,
                                   S["a_stats"], S["a_var"], S["a_vareps"])
                    elif step == "a_norm":
                        dve.wait_ge(S["a_rstd"], a.now)
                        normalise(lambda t: a_xn[:, t, :], lambda t: x1[:, a.n, t, :], a_mv, a_rstd, S["a_xn"])
                    elif step == "p_qkv" and p_in_fill(p):
                        rotate_p(dve, ring, p, slice(0, 1), "q_")
                    elif step == "p_cut" and p_in_fill(p):
                        cut_p(dve, p, slice(0, 1), "q_")
                    elif step == "a_qkv3" and in_fill(a):
                        rotate_a(dve, ring, a, "q")
                        if a.n == 0:
                            prepare()
                    elif step == "p_hT":
                        dve.wait_ge(S["p_h0"], p.now)
                        dve.tensor_copy(res[:, p.n, :, :], h0[:, :, :]).then_inc(S["p_kept"], 1)
                    elif step == "a_qkT":
                        empty(ring, "a_kT", dve.tensor_copy(a_kT[:, :], await_job(ring, "a_kT")))
                    elif step[:3] == "a_s" and step in JOBS:
                        t = int(step[-1])
                        bank = await_job(ring, step)
                        dve.tensor_reduce(a_nm[:, t:t + 1], bank[:, 0:(t + 1) * P], AX, ALU.max, negate=True)\
                           .then_inc(S["a_nmax"], 1)
                        dve.wait_ge(S["a_nmax"], NT * a.n + t + 1)
                        dve.tensor_scalar(a_nb[:, t:t + 1], a_nm[:, t:t + 1], SCALE_A, None, ALU.mult)\
                           .then_inc(S["a_nbias"], 1)
                    elif step == "a_pT":
                        empty(ring, "a_p1", dve.tensor_copy(a_pT[:, 1, :], await_job(ring, "a_p1")))
                    elif step == "a_r":
                        dve.wait_ge(small_free[ring.bank("a_s3")], ring.count("a_s3"))
                        dve.reciprocal(a_ri[:, :], a_sum[:, :]).then_inc(S["a_inv"], 1)
                        bank = await_job(ring, "a_r")
                        dve.wait_ge(S["a_inv"], a.now)
                        ins = dve.tensor_tensor(a_xn[:, :, :], bank.rearrange("p (t d) -> p t d", t=NT),
                                                a_ri[:, :].unsqueeze(2).to_broadcast([P, NT, D]), ALU.mult)
                        empty(ring, "a_r", ins)
                    elif step == "a_rstats":
                        held(dve, small_free[ring.bank("a_r")], ring.count("a_r"))
                        norm_stats(lambda t: a_xn[:, t, :], a_st, a_mv, a_ve, a.now,
                                   S["a_rstats"], S["a_rvar"], S["a_rvareps"])
                    elif step == "p_rnorm":
                        dve.wait_ge(S["a_rrstd"], p.now)
                        normalise(lambda t: a_xn[:, t, :], lambda t: a_xn[:, t, :], a_mv, a_rstd, S["a_rn"])
                    elif step == "p_stats":
                        held(dve, S["x1_ready"], p.now)
                        norm_stats(lambda t: x1[:, p.n, t, :], p_st, p_mv, p_ve, p.now,
                                   S["p_stats"], S["p_var"], S["p_vareps"])
                    elif step == "p_norm":
                        dve.wait_ge(S["p_rstd"], p.now)
                        normalise(lambda t: h0[:, t, :], lambda t: x1[:, p.n, t, :], p_mv, p_rstd, S["p_h0"])
                        dve.tensor_tensor(p_m1[:, :], p_mv[:, :, 1], p_rstd[:, :], ALU.mult).then_inc(S["p_w1"], 1)
                        dve.wait_ge(S["p_w1"], p.now)
                        dve.tensor_tensor(p_m2[:, :], p_m1[:, :], p_rstd[:, :], ALU.mult).then_inc(S["p_w2"], 1)
                        dve.wait_ge(S["p_w2"], p.now)
                        dve.tensor_scalar(p_ms[:, :], p_m2[:, :], EPS, None, ALU.add).then_inc(S["p_ms"], 1)
                    elif step == "p_rows":
                        wait(dve, kz_in, 16 * R * p.n)
                        for n in range(2):
                            bank = await_job(ring, f"p_k{n}").bitcast(BF16)
                            empty(ring, f"p_k{n}", dve.tensor_copy(
                                k_all[:, 2 * n:2 * n + 2, :].rearrange("p g t -> p (g t)"), bank))
                    elif step == "p_max0":
                        for n in range(len(MAX_JOBS)):
                            max_job(p, ring, 0, n)
                    elif step.startswith("m_cut"):
                        g = int(step[-1])
                        heads = slice(g * R, (g + 1) * R)
                        slot = q_rows[:, m.parity, :, heads, 6, :]
                        mx = nmax[:, :, heads]
                        last_max = f"max{g}_{len(MAX_JOBS) - 1}"
                        if g:
                            dve.wait_ge(small_free[ring.bank(last_max)], ring.count(last_max))
                        n = 5 * (G * m.n + g)
                        dve.tensor_copy(slot[:, :, :, 0], mx).then_inc(cut, 1)
                        dve.wait_ge(cut, n + 1)
                        dve.tensor_tensor(nm_r1[:, :, :], mx, slot[:, :, :, 0], ALU.subtract).then_inc(cut, 1)
                        dve.wait_ge(cut, n + 2)
                        dve.tensor_copy(slot[:, :, :, 1], nm_r1[:, :, :]).then_inc(cut, 1)
                        dve.wait_ge(cut, n + 3)
                        dve.tensor_tensor(nm_r2[:, :, :], nm_r1[:, :, :], slot[:, :, :, 1], ALU.subtract).then_inc(cut, 1)
                        dve.wait_ge(cut, n + 4)
                        dve.tensor_copy(slot[:, :, :, 2], nm_r2[:, :, :]).then_inc(cut, 1)
                    elif step.startswith("m_shift"):
                        g = int(step[-1])
                        bank = await_job(ring, step[2:]).bitcast(BF16)
                        empty(ring, step[2:], dve.tensor_copy(qT2[:, g % 2, :], bank[:, 0:T]))
                    elif step.startswith("m_mix"):
                        g, s = int(step[-2]), int(step[-1])
                        if g + 1 < G or p:
                            for n in mix_max(s):
                                max_job(m if g + 1 < G else p, ring, (g + 1) % G, n)
                    elif step in ("m_pv1", "f_pv2", "f_pv3", "f_o"):
                        g = G - 1 if step == "f_o" else int(step[-1]) - 1
                        bank = await_job(ring, f"o{g}").rearrange("p (t r c) -> p t r c", t=NT, r=R)
                        dve.reciprocal(inv[:, g % 2, :, :], bank[:, :, :, HD]).then_inc(inv_done, 1)
                        dve.wait_ge(inv_done, G * (m if step[0] == "m" else f).n + g + 1)
                        o = o_tok[:, :, :].rearrange("p t (g r d) -> p t g r d", g=G, r=R)[:, :, g, :, :]
                        empty(ring, f"o{g}", dve.tensor_tensor(
                            o, bank[:, :, :, 0:HD], inv[:, g % 2, :, :].unsqueeze(3).to_broadcast([P, NT, R, HD]), ALU.mult))
                    elif step == "f_up":
                        dve.wait_ge(S["p_kept"], f.now)
                        bank = await_job(ring, "up")
                        dve.tensor_tensor(res[:, f.n, :, :], bank.rearrange("p (t d) -> p t d", t=NT),
                                          res[:, f.n, :, :], ALU.add).then_inc(small_free[ring.bank("up")], 1)
                        dve.wait_ge(S["sq_done"], f.now)
                        dve.tensor_scalar(m_ms[:, :], m_sq[:, :], 1.0 / D, EPS, ALU.mult, ALU.add)\
                           .then_inc(S["m_ms"], 1)
                    elif step == "f_logits":
                        bank = await_job(ring, "logits")
                        empty(ring, "logits", dve.tensor_copy(
                            lgs[:, :, :], bank[:, 0:NT * NE].rearrange("p (t e) -> p t e", t=NT)))
                    elif step == "f_route0":
                        dve.wait_ge(small_free[ring.bank("logits")], ring.count("logits"))
                        routed[0] = 0
                        find_top(f, 0, lgs)
                    elif step == "f_route1":
                        then(f, dve.scalar_tensor_tensor(out=lg2[:, :, :], in0=hot[:, 0, :, :], scalar=-3.0e38,
                                                         in1=lgs[:, :, :], op0=ALU.mult, op1=ALU.add))
                        find_top(f, 1, lg2, range(2))
                    elif step == "f_route2":
                        find_top(f, 1, lg2, range(2, 5))
                    elif step == "f_route3":
                        then(f, dve.tensor_tensor(top[:, :, 2], top[:, :, 1], top[:, :, 0], ALU.subtract))
                        assert routed[0] == DIFF_AT
                        then(f, dve.tensor_tensor(sel[:, :, :], hot[:, 0, :, :], hot[:, 1, :, :], ALU.add))
                        assert routed[0] == SEL_AT
                        wait(dve, sent, 16 * TOP * NT * f.n)
                        then(f, dve.tensor_copy(m_row[:, :, :, D], result_sb[:, :, :]))
                        then(f, dve.tensor_scalar(result_sb[:, :, :], result_sb[:, :, :], float(T), None, ALU.add))
                    elif step == "f_rank":
                        bank = await_job(ring, "rank")
                        empty(ring, "rank", dve.tensor_tensor(
                            place[:, :, :], bank[:, 0:NT * NE].rearrange("p (t e) -> p t e", t=NT),
                            region_sb[:, :, :], ALU.add))
                        dve.wait_ge(small_free[ring.bank("rank")], ring.count("rank"))
                        for n in range(TOP):
                            last = dve.tensor_tensor(place2[:, n, :, :], hot[:, n, :, :], place[:, :, :], ALU.mult)
                        then(f, last)
                        then(f, dve.tensor_reduce(place_f[:, :, :], place2[:, :, :, :], AX, ALU.add))
                        then(f, dve.tensor_copy(place_u[:, :, :], place_f[:, :, :]))
                        assert routed[0] == PLACE_AT
                    elif step == "f_route4":
                        then(f, dve.tensor_reduce(sel_sum[:, :], sel[:, :, :].rearrange("p t e -> p e t"), AX, ALU.add))
                        then(f, dve.tensor_tensor(sel_before[:, :, :], sel_before[:, :, :],
                                                  sel_sum[:, :].unsqueeze(1).to_broadcast([P, NT, NE]), ALU.add))
                    elif step == "f_route5":
                        dve.wait_ge(top_exp, f.now)
                        then(f, dve.tensor_scalar(top[:, :, 4], top[:, :, 3], 1.0, None, ALU.add))
                        then(f, dve.reciprocal(gate[:, f.n, :, 0], top[:, :, 4]))
                        assert routed[0] + 1 == ROUTE_OPS
                        then(f, dve.tensor_tensor(gate[:, f.n, :, 1], top[:, :, 3], gate[:, f.n, :, 0], ALU.mult))

            iterations(dve, body)

            dve.wait_ge(totals_full, 1)
            dve.wait_ge(tables_in, 16 * 3)
            count = 0

            def table(ins):
                nonlocal count
                count += 1
                ins.then_inc(table_step, 1)
                dve.wait_ge(table_step, count)

            table(dve.tensor_copy(chosen[:, :], wide[:, 0, 0:NE]))
            table(dve.tensor_tensor(pad_f[:, :], chosen[:, :], region_sb[:, 0, :], ALU.add))
            dve.tensor_copy(pad_u[:, :], pad_f[:, :]).then_inc(pads_done, 1)
            table(dve.tensor_tensor(cmp[:, :, :], chosen[:, :].unsqueeze(2).to_broadcast([P, NE, FULL]),
                                    full_sb[:, :, :], ALU.is_gt))
            table(dve.tensor_reduce(tiles_of[:, :], cmp[:, :, :], AX, ALU.add))
            each = tiles_of[:, :].unsqueeze(1)
            table(dve.tensor_tensor(le[:, 0:NE, :], each.to_broadcast([P, NE, NE]), up_to_sb[:, :, :], ALU.mult))
            table(dve.tensor_reduce(tiles_to[:, :], le[:, 0:NE, :], AX, ALU.add))
            table(dve.tensor_tensor(le[:, :, :], numbers_sb[:, :].unsqueeze(2).to_broadcast([P, TILES, NE]),
                                    tiles_to[:, :].unsqueeze(1).to_broadcast([P, TILES, NE]), ALU.is_ge))
            table(dve.tensor_reduce(tile_e[:, :], le[:, :, :], AX, ALU.add))
            table(dve.tensor_tensor(le2[:, :, :], le[:, :, :], each.to_broadcast([P, TILES, NE]), ALU.mult))
            table(dve.tensor_reduce(tile_first[:, :], le2[:, :, :], AX, ALU.add))
            table(dve.tensor_tensor(tile_first[:, :], numbers_sb[:, :], tile_first[:, :], ALU.subtract))
            table(dve.tensor_scalar(tile_row[:, :], tile_e[:, :], float(REGION // P), None, ALU.mult))
            table(dve.tensor_tensor(tile_row[:, :], tile_row[:, :], tile_first[:, :], ALU.add))
            table(dve.tensor_scalar(row_u[:, :], tile_row[:, :], float(P), None, ALU.mult))
            dve.tensor_scalar(expert_u[:, :], tile_e[:, :], float(NE - 1), None, ALU.min).then_inc(tables_done, 1)

            def take_dest(tile):
                dve.wait_ge(x_in[tile.buf], 16 * (tile.turn + 1))
                wait(dve, y_out[tile.buf], 16 * tile.turn)
                dve.tensor_copy(dest[:, tile.buf:tile.buf + 1], x_rows[:, tile.buf, D:D + 1]).then_inc(dest_done, 1)

            def gated(tile):
                dve.wait_ge(e_silu, tile.n + (E_CREDIT + 1))
                dve.wait_ge(hT_full, tile.n + (E_CREDIT - 1))
                dve.tensor_tensor(hid[:, tile.half, :], silu[:, tile.half, :], wide[:, tile.half, F:2 * F], ALU.mult)\
                   .then_inc(hid_done, 1)

            def result(tile):
                dve.wait_ge(y_full, tile.n + (E_CREDIT + 1))
                dve.tensor_copy(y_rows[:, tile.buf, :], small[:, 2 + tile.half, 0:D]).then_inc(y_free, 1)

            def tile_step(s):
                for part, tile in ((take_dest, s + 2), (gated, s + 1), (result, s + -1)):
                    if tile.exists():
                        part(tile)

            tile_steps(dve, tile_step)

            stats = ((a_st, a_mv, a_ve, a_rstd), (p_st, p_mv, p_ve, p_rstd))

            def final_step_of(b, par):
                if not isinstance(b, int) or b < NB:
                    st, mv, ve, _ = stats[par]
                    dve.wait_ge(summed, b + 1)
                    dve.tensor_tensor(y[:, par, :, :], parts[:, par, 0, :, :], parts[:, par, 1, :, :], ALU.add)\
                       .then_inc(yin_used, 1)
                    dve.wait_ge(yin_used, b + 1)
                    norm_stats(lambda t: y[:, par, t, :], st, mv, ve, b + 1, final_stats, final_mean, final_var)
                if not isinstance(b, int) or b > 0:
                    _, mv, _, rstd = stats[1 - par]
                    dve.wait_ge(final_pow, b)
                    normalise(lambda t: xn[:, 1 - par, t, :], lambda t: y[:, 1 - par, t, :], mv, rstd, final_norm)
                    dve.wait_ge(final_norm, b)
                    dve.tensor_tensor(x1[:, b - 1, :, :], x1[:, b - 1, :, :], xn[:, 1 - par, :, :], ALU.add)\
                        .then_inc(final_out, 1)

            batch_steps(dve, final_step_of)


def tables():
    import numpy as np

    def by_tile(a):
        return np.ascontiguousarray(a.reshape(NT, P, -1).transpose(1, 0, 2))

    f32 = np.float32
    pos = np.arange(T, dtype=f32)[:, None]
    half = D // 2
    freq = np.power(f32(10000.0), -np.arange(half, dtype=f32) / f32(half)).astype(f32)
    ang = pos * freq[None, :]
    cos, sin = np.cos(ang).astype(f32), np.sin(ang).astype(f32)
    cos_a = by_tile(np.concatenate([cos, cos], 1))
    sin_a = by_tile(np.concatenate([-sin, sin], 1))
    inv = (f32(1.0) / np.power(f32(10000.0), np.arange(0, HD, 2, dtype=f32) / f32(HD))).astype(f32)
    ang = pos * inv[None, :]
    cos, sin = np.cos(ang).astype(f32), np.sin(ang).astype(f32)
    cos_b = np.tile(np.repeat(cos, 2, 1), (1, H))
    sin_b = np.tile(np.stack([-sin, sin], -1).reshape(T, HD), (1, H))
    cos_b, sin_b = (np.ascontiguousarray(np.stack([by_tile(a)] * 2, 1)) for a in (cos_b, sin_b))
    q, k = np.arange(P)[:, None], np.arange(P)[None, :]
    future = np.where(k > q, f32(-1e30), f32(0))
    across = lambda a: np.ascontiguousarray(np.broadcast_to(np.asarray(a, dtype=f32)[None], (P, *np.shape(a))))
    e, tiles_ = np.arange(NE), np.ones((NT, 1))
    padding = np.zeros((NE + SPARE, P, ROW), f32)
    padding[:, :, D] = TOP * NTOK + np.arange((NE + SPARE) * P).reshape(NE + SPARE, P)
    result_at = (np.arange(TOP)[None, :, None] * NTOK + np.arange(NT)[None, None, :] * P
                 + np.arange(P)[:, None, None]).astype(f32)
    return {"cos_a": cos_a, "sin_a": sin_a, "cos_b": cos_b, "sin_b": sin_b, "ident_f": np.eye(P, dtype=f32),
            "future": future, "future_t": np.ascontiguousarray(future.T),
            "first_slot": across(tiles_ * (NE - e)), "region_at": across(tiles_ * (e * REGION)),
            "full_tiles": across(np.ones((NE, 1)) * np.arange(FULL) * P), "tile_numbers": across(np.arange(TILES)),
            "up_to": across(e[None, :] <= e[:, None]), "result_at": result_at,
            "before": (q < k).astype(f32), "padding": padding}


INPUTS = ["L0_attn_x", "L0_attn_wq", "L0_attn_wk", "L0_attn_wv", "L0_attn_wo", "L0_ffn_g1", "L0_ffn_g2",
          "L0_ffn_w_down", "L0_ffn_wq", "L0_ffn_wk", "L0_ffn_wv", "L0_ffn_w_up", "L0_ffn_router_w",
          "L0_ffn_w1", "L0_ffn_w2", "L0_ffn_w3"]


def kernel(**inputs):
    import numpy as np
    import concourse.bacc as bacc
    from concourse.bass_utils import run_bass_kernel_spmd

    nc = bacc.Bacc("TRN2", target_bir_lowering=False, num_devices=1)
    arrays = {name: np.ascontiguousarray(inputs[name]) for name in INPUTS}
    arrays.update(tables())
    args = [nc.dram_tensor(n, a.shape, mybir.dt.from_np(a.dtype), kind="ExternalInput").ap()
            for n, a in arrays.items()]
    out = nc.dram_tensor("out", (NB, T, D), F32, kind="ExternalOutput").ap()
    program(nc, *args, out)
    r = run_bass_kernel_spmd(nc, [arrays], core_ids=[0])
    return r.results[0]["out"]
```
